# Optimizing a Trainium2 kernel written in Bass

```python
import numpy as np
import jax
import jax.numpy as jnp

def _softmax(x, axis=-1):
    return jax.nn.softmax(x, axis=axis)

def _gelu(x):
    return jax.nn.gelu(x, approximate=True)

def _silu(x):
    return jax.nn.silu(x)

def _sigmoid(x):
    return jax.nn.sigmoid(x)

def _layernorm(x, axis=-1, eps=1e-05):
    m = jnp.mean(x, axis=axis, keepdims=True)
    v = jnp.var(x, axis=axis, keepdims=True)
    return (x - m) / jnp.sqrt(v + eps)

def _scatter_add(tgt, idx, src, axis=0):
    return tgt.at[idx].add(src)

def _segment_sum(src, seg, n):
    return jax.ops.segment_sum(src, seg, n)
kernel_name = 'mk_xattn_ffn_d2_seqx_r4_8068d3'

def setup_inputs(seed: int=0):
    np.random.seed(seed)
    _w = jnp.asarray

    def _rec_inputs():
        import jax
        import jax.numpy as jnp
        _rk = jax.random.key(seed)
        x = 7.22e-05 + 1 * jax.random.normal(jax.random.fold_in(_rk, 1), (4, 512, 256), jnp.float32)
        _lenS = 512 - jax.random.randint(jax.random.fold_in(_rk, 7), (4,), 0, max(1, 512 // 4) + 1, jnp.int32)
        _lenS2 = 512 - jax.random.randint(jax.random.fold_in(_rk, 8), (4,), 0, max(1, 512 // 4) + 1, jnp.int32)
        _ctx_1024P = jax.random.normal(jax.random.fold_in(_rk, 11), (4, 16, 256), jnp.float32)
        _ctx_1024c = jax.random.dirichlet(jax.random.fold_in(_rk, 511), 0.3 * jnp.ones((16,), jnp.float32), (4, 512))
        _ctx_1024t = jnp.einsum('bsk,bkd->bsd', _ctx_1024c, _ctx_1024P)
        _ctx_1024t = _ctx_1024t * jax.lax.rsqrt(jnp.mean(jnp.square(_ctx_1024t)) + 1e-12) * 0.953939
        ctx_1024 = 4.13588e-05 + 0.999923 * (_ctx_1024t + 0.3 * jax.random.normal(jax.random.fold_in(_rk, 611), (4, 512, 256), jnp.float32))
        _validS = jnp.arange(512)[None, :] < _lenS[:, None]
        _validS2 = jnp.arange(512)[None, :] < _lenS2[:, None]
        _causal = jnp.tril(jnp.ones((512, 512), dtype=bool))
        mask_Bx1xSxS2_ik1 = jnp.where(jnp.broadcast_to(_validS2[:, None, None, :], (4, 1, 512, 512)), 1, 0).astype(jnp.int32)
        return (x, ctx_1024, mask_Bx1xSxS2_ik1)
    x, ctx_1024, mask_Bx1xSxS2_ik1 = _rec_inputs()

    def _L0_xattn_setup():
        import jax, jax.numpy as jnp
        import numpy as np
        B, T, D, H = (4, 512, 256, 1024)
        S = 64
        EPS = 1e-05

        def _layer_norm(x, gamma, beta):
            mu = jnp.mean(x, axis=-1, keepdims=True)
            var = jnp.mean(jnp.square(x - mu), axis=-1, keepdims=True)
            return (x - mu) * jax.lax.rsqrt(var + EPS) * gamma + beta

        def _aft_local(emb, wq, bq, wk, bk, wv, bv, wo, bo, pos_bias):
            q = emb @ wq + bq
            k = emb @ wk + bk
            v = emb @ wv + bv
            idx = jnp.arange(T)
            mask = (jnp.abs(idx[:, None] - idx[None, :]) < S).astype(pos_bias.dtype)
            w = pos_bias * mask
            max_k = jnp.max(k, axis=1, keepdims=True)
            max_w = jnp.max(w, axis=1, keepdims=True)
            ek = jnp.exp(k - max_k)
            ew = jnp.exp(w - max_w)
            num = jnp.einsum('tj,bjd->btd', ew, ek * v)
            den = jnp.einsum('tj,bjd->btd', ew, ek)
            y = jax.nn.sigmoid(q) * num / den
            return y @ wo + bo
        key = jax.random.key(seed)
        ks = jax.random.split(key, 16)
        sd = 0.02
        return {'x': jax.random.normal(ks[0], (B, T, D), jnp.float32), 'pos_encod': jax.random.normal(ks[1], (B, T, D), jnp.float32), 'wq': jax.random.normal(ks[2], (D, D), jnp.float32) * sd, 'bq': jnp.zeros((D,), jnp.float32), 'wk': jax.random.normal(ks[3], (D, D), jnp.float32) * sd, 'bk': jnp.zeros((D,), jnp.float32), 'wv': jax.random.normal(ks[4], (D, D), jnp.float32) * sd, 'bv': jnp.zeros((D,), jnp.float32), 'wo': jax.random.normal(ks[5], (D, D), jnp.float32) * sd, 'bo': jnp.zeros((D,), jnp.float32), 'pos_bias': jax.random.normal(ks[6], (T, T), jnp.float32) * sd, 'gamma': jnp.ones((D,), jnp.float32), 'beta': jnp.zeros((D,), jnp.float32), 'w1': jax.random.normal(ks[7], (D, H), jnp.float32) * sd, 'b1': jnp.zeros((H,), jnp.float32), 'w2': jax.random.normal(ks[8], (H, D), jnp.float32) * sd, 'b2': jnp.zeros((D,), jnp.float32)}
    _L0_xattn_all = _L0_xattn_setup()
    _L0_xattn_in = {k: v for k, v in _L0_xattn_all.items() if k in ('wq', 'bq', 'wk', 'bk', 'wv', 'bv', 'wo', 'bo', 'pos_bias', 'gamma', 'beta', 'w1', 'b1', 'w2', 'b2')}
    del _L0_xattn_all

    def _L0_ffn_setup():
        import jax, jax.numpy as jnp
        import numpy as np
        B, S, D = (4, 128, 256)
        E, K, H = (64, 8, 64)
        ES, HS = (2, 512)
        key = jax.random.key(seed)
        ks = jax.random.split(key, 8)
        scale = 0.02
        rn = lambda k, shape, s: jax.random.normal(k, shape, jnp.float32) * s
        return {'x': rn(ks[0], (B, S, D), 1.0), 'router_w': rn(ks[1], (D, E), scale), 'router_b': jnp.zeros((E,), jnp.float32), 'w1': rn(ks[2], (E, D, H), scale), 'b1': jnp.zeros((E, H), jnp.float32), 'w2': rn(ks[3], (E, H, D), scale), 'b2': jnp.zeros((E, D), jnp.float32), 'sw1': rn(ks[4], (ES, D, HS), scale), 'sb1': jnp.zeros((ES, HS), jnp.float32), 'sw2': rn(ks[5], (ES, HS, D), scale), 'sb2': jnp.zeros((ES, D), jnp.float32)}
    _L0_ffn_all = _L0_ffn_setup()
    _L0_ffn_in = {k: v for k, v in _L0_ffn_all.items() if k in ('router_w', 'router_b', 'w1', 'b1', 'w2', 'b2', 'sw1', 'sb1', 'sw2', 'sb2')}
    del _L0_ffn_all

    def _L1_xattn_setup():
        import jax, jax.numpy as jnp
        import numpy as np
        EMB, HEADS = (256, 16)
        B, S = (4, 512)
        key = jax.random.key(seed)
        ks = jax.random.split(key, 12)
        scale = 1.0 / np.sqrt(EMB)
        inp = {'q': jax.random.normal(ks[0], (B, S, EMB), jnp.float32), 'k': jax.random.normal(ks[1], (B, S, EMB), jnp.float32), 'v': jax.random.normal(ks[2], (B, S, EMB), jnp.float32), 'mask': jax.random.randint(ks[3], (B, 1, S, S), 0, 2, jnp.int32), 'Wq': jax.random.normal(ks[4], (EMB, EMB), jnp.float32) * scale, 'bq': jnp.zeros((EMB,), jnp.float32), 'Wk': jax.random.normal(ks[5], (EMB, EMB), jnp.float32) * scale, 'bk': jnp.zeros((EMB,), jnp.float32), 'Wv': jax.random.normal(ks[6], (EMB, EMB), jnp.float32) * scale, 'bv': jnp.zeros((EMB,), jnp.float32), 'Wo': jax.random.normal(ks[7], (EMB, EMB), jnp.float32) * scale, 'bo': jnp.zeros((EMB,), jnp.float32)}
        return inp
    _L1_xattn_all = _L1_xattn_setup()
    _L1_xattn_in = {k: v for k, v in _L1_xattn_all.items() if k in ('Wq', 'bq', 'Wk', 'bk', 'Wv', 'bv', 'Wo', 'bo')}
    del _L1_xattn_all

    def _L1_ffn_setup():
        import jax, jax.numpy as jnp
        import numpy as np

        def _binarize(w):
            alpha = jax.lax.stop_gradient(jnp.mean(jnp.abs(w), axis=1, keepdims=True))
            bw = alpha * jnp.sign(w)
            return w + jax.lax.stop_gradient(bw - w)
        key = jax.random.key(seed)
        k1, k2, k3, k4, k5 = jax.random.split(key, 5)
        D, H = (256, 1024)
        x = jax.random.normal(k1, (64, 196, D), dtype=jnp.float32)
        w1 = jax.random.normal(k2, (H, D), dtype=jnp.float32) * 0.02
        b1 = jax.random.normal(k3, (H,), dtype=jnp.float32) * 0.02
        w2 = jax.random.normal(k4, (D, H), dtype=jnp.float32) * 0.02
        b2 = jax.random.normal(k5, (D,), dtype=jnp.float32) * 0.02
        return {'x': x, 'w1': w1, 'b1': b1, 'w2': w2, 'b2': b2}
    _L1_ffn_all = _L1_ffn_setup()
    _L1_ffn_in = {k: v for k, v in _L1_ffn_all.items() if k in ('w1', 'b1', 'w2', 'b2')}
    del _L1_ffn_all
    return {'x': x, 'ctx_1024': ctx_1024, 'mask_Bx1xSxS2_ik1': mask_Bx1xSxS2_ik1, 'L0_xattn_wq': _L0_xattn_in['wq'], 'L0_xattn_bq': _L0_xattn_in['bq'], 'L0_xattn_wk': _L0_xattn_in['wk'], 'L0_xattn_bk': _L0_xattn_in['bk'], 'L0_xattn_wv': _L0_xattn_in['wv'], 'L0_xattn_bv': _L0_xattn_in['bv'], 'L0_xattn_wo': _L0_xattn_in['wo'], 'L0_xattn_bo': _L0_xattn_in['bo'], 'L0_xattn_pos_bias': _L0_xattn_in['pos_bias'], 'L0_xattn_gamma': _L0_xattn_in['gamma'], 'L0_xattn_beta': _L0_xattn_in['beta'], 'L0_xattn_w1': _L0_xattn_in['w1'], 'L0_xattn_b1': _L0_xattn_in['b1'], 'L0_xattn_w2': _L0_xattn_in['w2'], 'L0_xattn_b2': _L0_xattn_in['b2'], 'L0_ffn_router_w': _L0_ffn_in['router_w'], 'L0_ffn_router_b': _L0_ffn_in['router_b'], 'L0_ffn_w1': _L0_ffn_in['w1'], 'L0_ffn_b1': _L0_ffn_in['b1'], 'L0_ffn_w2': _L0_ffn_in['w2'], 'L0_ffn_b2': _L0_ffn_in['b2'], 'L0_ffn_sw1': _L0_ffn_in['sw1'], 'L0_ffn_sb1': _L0_ffn_in['sb1'], 'L0_ffn_sw2': _L0_ffn_in['sw2'], 'L0_ffn_sb2': _L0_ffn_in['sb2'], 'L1_xattn_Wq': _L1_xattn_in['Wq'], 'L1_xattn_bq': _L1_xattn_in['bq'], 'L1_xattn_Wk': _L1_xattn_in['Wk'], 'L1_xattn_bk': _L1_xattn_in['bk'], 'L1_xattn_Wv': _L1_xattn_in['Wv'], 'L1_xattn_bv': _L1_xattn_in['bv'], 'L1_xattn_Wo': _L1_xattn_in['Wo'], 'L1_xattn_bo': _L1_xattn_in['bo'], 'L1_ffn_w1': _L1_ffn_in['w1'], 'L1_ffn_b1': _L1_ffn_in['b1'], 'L1_ffn_w2': _L1_ffn_in['w2'], 'L1_ffn_b2': _L1_ffn_in['b2']}

def reference(x, ctx_1024, mask_Bx1xSxS2_ik1, L0_xattn_wq, L0_xattn_bq, L0_xattn_wk, L0_xattn_bk, L0_xattn_wv, L0_xattn_bv, L0_xattn_wo, L0_xattn_bo, L0_xattn_pos_bias, L0_xattn_gamma, L0_xattn_beta, L0_xattn_w1, L0_xattn_b1, L0_xattn_w2, L0_xattn_b2, L0_ffn_router_w, L0_ffn_router_b, L0_ffn_w1, L0_ffn_b1, L0_ffn_w2, L0_ffn_b2, L0_ffn_sw1, L0_ffn_sb1, L0_ffn_sw2, L0_ffn_sb2, L1_xattn_Wq, L1_xattn_bq, L1_xattn_Wk, L1_xattn_bk, L1_xattn_Wv, L1_xattn_bv, L1_xattn_Wo, L1_xattn_bo, L1_ffn_w1, L1_ffn_b1, L1_ffn_w2, L1_ffn_b2):
    import jax
    import jax.numpy as jnp

    def _L0_xattn_ref(x, pos_encod, wq, bq, wk, bk, wv, bv, wo, bo, pos_bias, gamma, beta, w1, b1, w2, b2):
        import jax, jax.numpy as jnp
        import numpy as np
        B, T, D, H = (4, 512, 256, 1024)
        S = 64
        EPS = 1e-05

        def _layer_norm(x, gamma, beta):
            mu = jnp.mean(x, axis=-1, keepdims=True)
            var = jnp.mean(jnp.square(x - mu), axis=-1, keepdims=True)
            return (x - mu) * jax.lax.rsqrt(var + EPS) * gamma + beta

        def _aft_local(emb, wq, bq, wk, bk, wv, bv, wo, bo, pos_bias):
            q = emb @ wq + bq
            k = emb @ wk + bk
            v = emb @ wv + bv
            idx = jnp.arange(T)
            mask = (jnp.abs(idx[:, None] - idx[None, :]) < S).astype(pos_bias.dtype)
            w = pos_bias * mask
            max_k = jnp.max(k, axis=1, keepdims=True)
            max_w = jnp.max(w, axis=1, keepdims=True)
            ek = jnp.exp(k - max_k)
            ew = jnp.exp(w - max_w)
            num = jnp.einsum('tj,bjd->btd', ew, ek * v)
            den = jnp.einsum('tj,bjd->btd', ew, ek)
            y = jax.nn.sigmoid(q) * num / den
            return y @ wo + bo
        emb = x + pos_encod
        attn = _aft_local(emb, wq, bq, wk, bk, wv, bv, wo, bo, pos_bias)
        a = _layer_norm(attn + emb, gamma, beta)
        ff = jax.nn.relu(a @ w1 + b1) @ w2 + b2
        return _layer_norm(ff + a, gamma, beta)

    def _L0_ffn_ref(x, router_w, router_b, w1, b1, w2, b2, sw1, sb1, sw2, sb2):
        import jax, jax.numpy as jnp
        import numpy as np
        B, S, D = (4, 128, 256)
        E, K, H = (64, 8, 64)
        ES, HS = (2, 512)
        b_, s_, d_ = x.shape
        xf = x.reshape(-1, d_)
        probs = jax.nn.softmax(xf @ router_w + router_b, axis=-1)
        tw, ti = jax.lax.top_k(probs, K)
        tw = tw / jnp.sum(tw, axis=-1, keepdims=True)

        def body(acc, p):
            W1, B1, W2, B2, e = p
            h = jax.nn.silu(xf @ W1 + B1) @ W2 + B2
            cw = jnp.sum(jnp.where(ti == e, tw, 0.0), axis=-1)
            return (acc + cw[:, None] * h, None)
        routed, _ = jax.lax.scan(body, jnp.zeros_like(xf), (w1, b1, w2, b2, jnp.arange(w1.shape[0])))

        def shared_mlp(W1, B1, W2, B2):
            return jax.nn.silu(xf @ W1 + B1) @ W2 + B2
        shared = jnp.sum(jax.vmap(shared_mlp)(sw1, sb1, sw2, sb2), axis=0)
        return (routed + shared).reshape(b_, s_, d_)

    def _L1_xattn_ref(q, k, v, mask, Wq, bq, Wk, bk, Wv, bv, Wo, bo):
        import jax, jax.numpy as jnp
        import numpy as np
        EMB, HEADS = (256, 16)
        B, S = (4, 512)
        Bq, Sq, E = q.shape
        H = HEADS
        D = E // H
        Q = (q @ Wq.T + bq).reshape(Bq, Sq, H, D).transpose(0, 2, 1, 3)
        K = (k @ Wk.T + bk).reshape(Bq, -1, H, D).transpose(0, 2, 1, 3)
        V = (v @ Wv.T + bv).reshape(Bq, -1, H, D).transpose(0, 2, 1, 3)
        scores = jnp.einsum('bhqd,bhkd->bhqk', Q, K) / jnp.sqrt(jnp.float32(D))
        scores = jnp.where(mask == 1, jnp.float32(-1000000000.0), scores)
        attn = jax.nn.softmax(scores, axis=-1)
        out = jnp.einsum('bhqk,bhkd->bhqd', attn, V)
        out = out.transpose(0, 2, 1, 3).reshape(Bq, Sq, E)
        return out @ Wo.T + bo

    def _L1_ffn_ref(x, w1, b1, w2, b2):
        import jax, jax.numpy as jnp
        import numpy as np

        def _binarize(w):
            alpha = jax.lax.stop_gradient(jnp.mean(jnp.abs(w), axis=1, keepdims=True))
            bw = alpha * jnp.sign(w)
            return w + jax.lax.stop_gradient(bw - w)
        bw1 = _binarize(w1)
        h = jnp.einsum('bsd,hd->bsh', x, bw1) + b1
        h = jax.nn.gelu(h, approximate=False)
        bw2 = _binarize(w2)
        out = jnp.einsum('bsh,dh->bsd', h, bw2) + b2
        return out
    x = x + _L0_xattn_ref(_layernorm(x, axis=-1), ctx_1024, L0_xattn_wq, L0_xattn_bq, L0_xattn_wk, L0_xattn_bk, L0_xattn_wv, L0_xattn_bv, L0_xattn_wo, L0_xattn_bo, L0_xattn_pos_bias, L0_xattn_gamma, L0_xattn_beta, L0_xattn_w1, L0_xattn_b1, L0_xattn_w2, L0_xattn_b2)
    x = x + _L0_ffn_ref(_layernorm(x, axis=-1), L0_ffn_router_w, L0_ffn_router_b, L0_ffn_w1, L0_ffn_b1, L0_ffn_w2, L0_ffn_b2, L0_ffn_sw1, L0_ffn_sb1, L0_ffn_sw2, L0_ffn_sb2)
    x = x + _L1_xattn_ref(_layernorm(x, axis=-1), ctx_1024, ctx_1024, mask_Bx1xSxS2_ik1, L1_xattn_Wq, L1_xattn_bq, L1_xattn_Wk, L1_xattn_bk, L1_xattn_Wv, L1_xattn_bv, L1_xattn_Wo, L1_xattn_bo)
    x = x + _L1_ffn_ref(_layernorm(x, axis=-1), L1_ffn_w1, L1_ffn_b1, L1_ffn_w2, L1_ffn_b2)
    return x

_drawn_inputs = setup_inputs


def setup_inputs(seed=0):
    import zlib

    import numpy as np

    out = dict(_drawn_inputs(seed))
    spreads = {'L0_xattn_bq': (0.0, 0.8),
     'L0_xattn_bk': (0.0, 2.0),
     'L0_xattn_bv': (0.0, 0.8),
     'L0_xattn_bo': (0.0, 0.1),
     'L0_xattn_gamma': (1.0, 0.2),
     'L0_xattn_beta': (0.0, 0.1),
     'L0_xattn_b1': (0.0, 0.403),
     'L0_xattn_b2': (0.0, 0.1),
     'L0_ffn_router_b': (0.0, 0.791),
     'L0_ffn_b1': (0.0, 0.8),
     'L0_ffn_b2': (0.0, 0.451),
     'L0_ffn_sb1': (0.0, 0.453),
     'L0_ffn_sb2': (0.0, 0.1),
     'L1_xattn_bq': (0.0, 0.723),
     'L1_xattn_bk': (0.0, 2.0),
     'L1_xattn_bv': (0.0, 0.1),
     'L1_xattn_bo': (0.0, 0.1)}
    factors = {'L0_xattn_wq': 8.0,
     'L0_xattn_wk': 8.0,
     'L0_xattn_wv': 5.502,
     'L0_xattn_wo': 4.548,
     'L0_xattn_pos_bias': 8.0,
     'L0_ffn_router_w': 3.3,
     'L0_ffn_w1': 8.0,
     'L0_ffn_w2': 8.0,
     'L1_ffn_b1': 21.977,
     'L1_ffn_b2': 5.892}
    for name, (base, spread) in spreads.items():
        noise = np.random.default_rng([zlib.crc32(name.encode()), seed]).standard_normal(out[name].shape)
        drawn = base * np.exp(spread * noise) if base else spread * noise
        out[name] = jnp.asarray(drawn.astype(out[name].dtype))
    for name, factor in factors.items():
        out[name] = (out[name] * factor).astype(out[name].dtype)
    return out
```

```python
from contextlib import ExitStack

import concourse.bass as bass
from concourse import mybir

F32 = mybir.dt.float32
FR = mybir.dt.float32r
BF16 = mybir.dt.bfloat16
I32 = mybir.dt.int32
ALU = mybir.AluOpType
ACT = mybir.ActivationFunctionType
AX = mybir.AxisListType
ds = bass.ds

P = 128
B, T, D, H = 4, 512, 256, 1024
C = D // P
NT = B * T // P
TT = T // P
HT = H // P
E, K_TOP, HE = 64, 8, 64
GR = E * HE // H
EG = E // GR
HEADS, HD = 16, 16
HPB = 4
BAND = 64
EPS = 1e-5
NEG = -(2.0 ** 100)
PASSES = ((0, 0), (1, 0), (0, 1))


class Shared:
    pass


class Chain:

    def __init__(self, eng, sem, start, per, passed=None):
        self.eng, self.sem, self.start, self.per, self.passed, self.k = eng, sem, start, per, passed, 0

    def inc(self, ins):
        self.k += 1
        ins.then_inc(self.sem, 1)

    def wait(self):
        self.eng.wait_ge(self.sem, self.start + self.k)

    def hold(self):
        self.wait()
        self.eng.sem_inc(self.passed, 1)

    def link(self, ins):
        self.inc(ins)
        self.wait()

    def end(self):
        assert self.k == self.per, (self.k, self.per)


def f(ap):
    return ap.bitcast(F32)


class Norm:

    def __init__(self, sb, sem, name):
        self.st6 = sb(name + "_st6", [P, TT, 6], F32)
        self.mv = sb(name + "_mv", [P, TT, 2], F32)
        self.var = sb(name + "_var", [P, TT], F32)
        self.rstd = sb(name + "_rstd", [P, TT], F32)
        self.stats = sem(name + "_stats")
        self.var_eps = sem(name + "_var_eps")
        self.root = sem(name + "_root")
        self.passed = sem(name + "_passed")


def norm_dve(dve, nm, n, chain, src, dst, scale_shift=None):
    for tt in range(TT):
        chain.inc(dve.bn_stats(nm.st6[:, tt, :], src(tt)))
    chain.hold()
    for tt in range(TT):
        dve.bn_aggr(nm.mv[:, tt, :], nm.st6[:, tt, :]).then_inc(nm.stats, 1)
    dve.wait_ge(nm.root, n + 1)
    for tt in range(TT):
        chain.inc(dve.tensor_scalar(dst(tt), src(tt), nm.mv[:, tt, 0:1], nm.rstd[:, tt:tt + 1],
                                    ALU.subtract, ALU.mult))
    if scale_shift is not None:
        for w, op in zip(scale_shift, (ALU.mult, ALU.add)):
            chain.wait()
            for tt in range(TT):
                chain.inc(dve.tensor_tensor(dst(tt), dst(tt), w, op))


def norm_pool(pool, nm, n, power):
    pool.wait_ge(nm.stats, n * TT + TT)
    pool.sem_inc(nm.passed, 1)
    pool.tensor_scalar(nm.var[:, :], nm.mv[:, :, 1], EPS, 0.0, ALU.add, ALU.add).then_inc(nm.var_eps, 1)
    pool.wait_ge(nm.var_eps, n + 1)
    pool.tensor_tensor(nm.rstd[:, :], nm.var[:, :], power[:, 0:TT], ALU.pow).then_inc(nm.root, 1)


class Turn:

    def __init__(self, sem, name, banks):
        self.banks = banks
        self.ready = sem(name + "_turn_in")
        self.turned = sem(name + "_turned")
        self.hi = sem(name + "_turn_hi")
        self.lo = sem(name + "_turn_lo")


def turn_pe(pe, tn, n, src, ident):
    pe.wait_ge(tn.ready, n + 1)
    for c in range(C):
        pe.wait_ge(tn.lo, n * C + c + 1)
        for tt in range(TT):
            last = pe.transpose(tn.banks[c][:, tt * P:(tt + 1) * P], src(tt)[:, c * P:(c + 1) * P], ident)
        last.then_inc(tn.turned, 1)


def turn_act(act, tn, n, hi):
    for c in range(C):
        act.wait_ge(tn.turned, n * C + c + 1)
        act.activation(hi(c), tn.banks[c][:, :], ACT.Copy).then_inc(tn.hi, 1)


def turn_dve(dve, tn, n, hi, lo):
    for c in range(C):
        dve.wait_ge(tn.hi, n * C + c + 1)
        dve.tensor_tensor(lo(c), tn.banks[c][:, :], f(hi(c)), ALU.subtract).then_inc(tn.lo, 1)


def products(pe, out, lhs, rhs, chunks=C, passes=PASSES, start=True, stop=True, skip=False):
    n, m = 0, chunks * len(passes)
    for c in range(chunks):
        for a, b in passes:
            last = pe.matmul(out, lhs(a, c), rhs(b, c), start=start and n == 0, stop=stop and n == m - 1,
                             skip_group_check=skip)
            n += 1
    return last


RING = 4
LAG = 2


class Mlp:

    def __init__(self, sb, ps, sem, name, groups, gated=0):
        self.groups, self.gated = groups, gated
        self.hid = [ps(f"{name}_hid{i}", [P, T], F32) for i in range(2)]
        self.y = [ps(f"{name}_y{i}", [P, 2 * D], F32) for i in range(2)]
        self.hs = sb(name + "_hs", [P, 2, T], F32)
        self.h = [sb(f"{name}_h{'hl'[i]}", [P, RING, T], FR) for i in range(2)]
        if gated:
            self.gate = [ps(f"{name}_gate{i}", [P, T], F32) for i in range(2)]
            self.ms = sb(name + "_ms", [P, RING, T], F32)
            self.gate_ready = sem(name + "_gate_ready")
            self.gate_used = sem(name + "_gated")
        self.hid_ready = sem(name + "_hid_ready")
        self.activated = sem(name + "_activated")
        self.hi_gated = sem(name + "_hi_gated")
        self.hi_plain = sem(name + "_hi_plain")
        self.split = sem(name + "_split")
        self.h_used = sem(name + "_h_used")
        self.y_used = sem(name + "_y_used")


class Tile:

    def __init__(self, q, i, s, first=False):
        self.first = first
        self.q, self.i, self.t, self.n = q, i, s, q * B * HT + i * HT + s
        if s >= HT:
            self.i, self.t = i + 1, s - HT


def mlp_stream(eng, m, step, batch_end=None):
    for s in range(LAG):
        step(Tile(0, 0, s, s == 0), Tile(0, 0, s - 1) if s else None, None)

    def batch(q, i, peeled):
        def at(s):
            if not peeled or s < HT:
                return Tile(q, i, s)
            return Tile(q + 1, 0, s - HT, s == HT) if q + 1 < m.groups else None
        for s in range(LAG, HT + LAG):
            step(at(s), at(s - 1), at(s - LAG))
        if batch_end is not None:
            batch_end(q, i)

    for q in range(m.groups):
        with eng.Fori(0, B - 1) as i:
            batch(q, i, False)
        batch(q, B - 1, True)


def mlp_pe(pe, m, weights, xt, gate=None, new_group=None, p1=PASSES, p2=PASSES):
    pe.sem_inc(m.h_used, RING)

    def step(cur, _, back):
        if cur is not None:
            if new_group is not None and cur.first:
                new_group(cur.q)
            pe.wait_ge(m.activated, cur.n + 1)
            x = xt(cur.i)
            w1 = weights(cur.q)[0]
            products(pe, m.hid[cur.t % 2][:, :], lambda a, c: w1(a, c, cur.t), x, passes=p1).then_inc(m.hid_ready, 1)
            if cur.q < m.gated:
                pe.wait_ge(m.gate_used, cur.n + 1)
                pe.matmul(m.gate[cur.t % 2][:, :], *gate(cur), start=True, stop=True).then_inc(m.gate_ready, 1)
        if back is not None:
            t, w2 = back.t, weights(back.q)[1]
            pe.wait_ge(m.split, back.n + 1 + RING)
            if t == 0:
                pe.wait_ge(m.y_used, back.q * B + back.i + 1)
            for tt in range(TT):
                last = products(pe, m.y[tt // 2][:, (tt % 2) * D:(tt % 2 + 1) * D],
                                lambda a, c: m.h[a][:, t % RING, tt * P:(tt + 1) * P], lambda b, c: w2(b, t), chunks=1,
                                passes=p2, start=t == 0 and tt % 2 == 0, stop=t == HT - 1, skip=True)
            last.then_inc(m.h_used, 1)

    mlp_stream(pe, m, step)


def mlp_act(act, m, func, bias, scale=None):
    act.sem_inc(m.activated, 2)

    def step(cur, prev, _):
        if cur is not None:
            act.wait_ge(m.hid_ready, cur.n + 1)
            if cur.q < m.gated:
                act.wait_ge(m.gate_used, cur.n + 1)
            else:
                act.wait_ge(m.split, cur.n + RING - 1)
            act.activation(m.hs[:, cur.t % 2, :], m.hid[cur.t % 2][:, :], func, bias=bias(cur),
                           scale=1.0 if scale is None else scale(cur)).then_inc(m.activated, 1)
        if prev is not None and prev.q < m.gated:
            act.wait_ge(m.gate_used, prev.n + 3)
            act.wait_ge(m.h_used, prev.n + 1)
            act.activation(m.h[0][:, prev.t % RING, :], m.ms[:, prev.t % RING, :], ACT.Copy).then_inc(m.hi_gated, 1)

    mlp_stream(act, m, step)


def mlp_dve(dve, m, add_y):
    dve.sem_inc(m.split, RING)
    dve.sem_inc(m.y_used, 1)
    if m.gated:
        dve.sem_inc(m.gate_used, 2)

    def step(cur, prev, _):
        if cur is not None:
            r = cur.t % RING
            dve.wait_ge(m.activated, cur.n + 3)
            if cur.q < m.gated:
                dve.wait_ge(m.gate_ready, cur.n + 1)
                dve.wait_ge(m.split, cur.n + 1)
                dve.tensor_tensor(m.ms[:, r, :], m.hs[:, cur.t % 2, :], m.gate[cur.t % 2][:, :], ALU.mult)\
                   .then_inc(m.gate_used, 1)
            else:
                dve.wait_ge(m.h_used, cur.n + 1)
                dve.tensor_copy(m.h[0][:, r, :], m.hs[:, cur.t % 2, :]).then_inc(m.hi_plain, 1)
        if prev is not None:
            r = prev.t % RING
            src = m.ms[:, r, :] if prev.q < m.gated else m.hs[:, prev.t % 2, :]
            if prev.q < m.gated:
                dve.wait_ge(m.hi_gated, prev.n + 1)
            else:
                dve.wait_ge(m.hi_plain, prev.n + 1 - m.gated * B * HT)
            dve.tensor_tensor(m.h[1][:, r, :], src, f(m.h[0][:, r, :]), ALU.subtract).then_inc(m.split, 1)

    def batch_end(q, i):
        dve.wait_ge(m.h_used, Tile(q, i, HT).n + RING)
        for j in range(2):
            last = add_y(q, i, j, m.y[j][:, :].rearrange("p (t d) -> p t d", d=D))
        last.then_inc(m.y_used, 1)

    mlp_stream(dve, m, step, batch_end)


COLS = {"bq0": C, "bk0": C, "bv0": C, "b1_0": HT, "rb": 1, "eb1": GR * HT, "sb1": HT, "bq1": C, "bk1": C,
        "b1_1": HT}
ROWS = ("bo0", "gamma", "beta", "b2_0", "sb2a", "sb2b", "bv1", "bo1", "b2_1")


def col_at(name, j=0):
    names = list(COLS)
    return sum(COLS[n] for n in names[:names.index(name)]) + j


def tile_of(buf, i):
    return lambda tt: buf[:, ds(i * TT + tt, 1), :].rearrange("p a d -> p (a d)")


def own(buf):
    return lambda tt: buf[:, tt, :]


def split_dma(sp, s, dst, srcs):
    for j, src in enumerate(srcs):
        sp.dma_start(dst[:, j], src.rearrange("(c p) n -> p c n", p=P)).then_inc(s, 16)


def build(nc, a, out):
    with ExitStack() as whole:
        def maker(stack):
            def sb(name, shape, dt):
                return stack.enter_context(nc.sbuf_tensor(name, shape, dt))

            def ps(name, shape, dt):
                return stack.enter_context(nc.psum_tensor(name, shape, dt))
            return sb, ps

        def sem(name):
            return whole.enter_context(nc.semaphore(name))

        g = Shared()
        g.a, g.out, g.sem = a, out, sem
        sb, _ = maker(whole)
        g.x_res = sb("x_res", [P, NT, D], F32)
        g.xT = [sb(f"xT_{p}", [P, C, B * T], FR) for p in "hl"]
        g.ident = sb("ident", [P, P], F32)
        g.power = sb("power", [P, TT], F32)
        g.cols = sb("cols", [P, sum(COLS.values())], F32)
        g.rows = sb("rows", [P, len(ROWS), D], F32)
        g.w_stage = sb("w_stage", [P, 2, 2 * H], F32)
        g.consts = sem("constants_loaded")
        g.w_staged = sem("w_stage_loaded")
        g.w_split = sem("w_split")
        g.col = lambda name, j=0: g.cols[:, col_at(name, j):col_at(name, j) + 1]
        g.row = lambda name: g.rows[:, ROWS.index(name), :]
        g.xT_of = lambda i: (lambda q, c: g.xT[q][:, c, ds(i * T, T)])

        g.W1, g.W2 = [], []

        def group_buffers(stack, k):
            gsb, _ = maker(stack)
            g.W1.append([gsb(f"W1_{k}{p}", [P, C, H], FR) for p in "hl"])
            g.W2.append([gsb(f"W2_{k}{p}", [P, HT, D], FR) for p in "hl"])

        with ExitStack() as st:
            group_buffers(st, 0)
            g.attn = maker(st)[0]("attn", [P, NT, D], F32)
            with ExitStack() as st1:
                aft_phase(nc, g, *maker(st1))
            with ExitStack() as st1:
                group_buffers(st1, 1)
                g.cwT = maker(st1)[0]("cwT", [P, B * T], FR)
                with ExitStack() as st2:
                    ffn0_phase(nc, g, *maker(st2))
                with ExitStack() as st2:
                    router_phase(nc, g, *maker(st2))
                with ExitStack() as st2:
                    moe_phase(nc, g, *maker(st2))
        with ExitStack() as st1:
            norm_phase(nc, g, *maker(st1), "n1")
        with ExitStack() as st1:
            attention_phase(nc, g, *maker(st1))
        with ExitStack() as st1:
            sb1, ps1 = maker(st1)
            g.S1 = sb1("S1", [P, C, H], FR)
            g.S2 = sb1("S2", [P, HT, D], FR)
            g.alpha1 = sb1("alpha1", [P, HT], F32)
            g.alpha2 = sb1("alpha2", [P, D], F32)
            with ExitStack() as st2:
                binary_phase(nc, g, *maker(st2))
            ffn1_phase(nc, g, sb1, ps1)


def group_dma(sp, g, k):
    if k:
        sp.wait_ge(g.w_split, 4 * k)
    name1, name2, at = (("w1_0", "w2_0", 0) if k == 0 else ("ew1", "ew2", (k - 1) * H) if k <= GR
                        else ("sw1", "sw2", 0) if k == GR + 1 else ("w1_1", "w2_1", 0))
    sp.dma_start(g.w_stage[:, 0, :].rearrange("p (c n) -> p c n", c=C),
                 g.a[name1][:, at:at + H].rearrange("(c p) n -> p c n", p=P)).then_inc(g.w_staged, 16)
    sp.dma_start(g.w_stage[:, 1, :].rearrange("p (t n) -> p t n", t=HT),
                 g.a[name2][at:at + H, :].rearrange("(t p) n -> p t n", p=P)).then_inc(g.w_staged, 16)


def group_split(pool, g, k):
    pool.wait_ge(g.w_staged, 32 * (k + 1))
    for j, w in enumerate((g.W1, g.W2)):
        hi, lo = (w[k % 2][q][:, :, :].rearrange("p a b -> p (a b)") for q in range(2))
        pool.tensor_copy(hi, g.w_stage[:, j, :]).then_inc(g.w_split, 1)
        pool.wait_ge(g.w_split, 4 * k + 2 * j + 1)
        pool.tensor_tensor(lo, g.w_stage[:, j, :], f(hi), ALU.subtract).then_inc(g.w_split, 1)


def group_weights(g, k):
    return (lambda q, c, t: g.W1[k % 2][q][:, c, t * P:(t + 1) * P]), (lambda q, t: g.W2[k % 2][q][:, t, :])


def aft_phase(nc, g, sb, ps):
    a, sem = g.a, g.sem
    pair = sb("aft_pair", [P, 2, C, T], F32)
    wst = pair[:, :, :, :].rearrange("p a c t -> p (a c t)").rearrange("p (w c n) -> p w c n", w=4, c=C)
    ek, ekv = pair[:, 0], pair[:, 1]
    W = [sb(f"aft_w{p}", [P, 4, C, D], FR) for p in "hl"]
    pos = sb("aft_pos", [P, TT, T], F32)
    npm = sb("aft_npm", [P, TT], F32)
    ewT = [sb(f"aft_ewT{p}", [P, TT, T], FR) for p in "hl"]
    emb = sb("aft_emb", [P, TT, D], F32)
    embT = [sb(f"aft_embT{p}", [P, C, T], FR) for p in "hl"]
    km = sb("aft_km", [P, 3, C], F32)
    nbq = sb("aft_nbq", [P, C], F32)
    sg = sb("aft_sg", [P, C, T], F32)
    ekT = [sb(f"aft_ekT{p}", [P, TT, D], FR) for p in "hl"]
    ekvT = [sb(f"aft_ekvT{p}", [P, TT, D], FR) for p in "hl"]
    y, yT = ekv, embT
    TP = [ps(f"aft_tp{i}", [P, T], F32) for i in range(2)]
    KB = [ps(f"aft_k{i}", [P, T], F32) for i in range(2)]
    VB = [ps(f"aft_v{i}", [P, T], F32) for i in range(2)]
    QB = [ps(f"aft_q{i}", [P, T], F32) for i in range(2)]
    nm, tn = Norm(sb, sem, "aft"), Turn(sem, "aft", TP)
    s_x, s_w, s_pos, s_ctx = (sem("aft_" + n) for n in ("x_loaded", "w_loaded", "pos_loaded", "ctx_loaded"))
    s_wh, s_wl = sem("aft_w_hi"), sem("aft_w_lo")
    s_band, s_npm, s_ew = sem("aft_band"), sem("aft_npm_done"), sem("aft_ew_done")
    s_ewt, s_ewh, s_ewl = sem("aft_ew_turned"), sem("aft_ew_hi"), sem("aft_ew_lo")
    s_c, s_pass = sem("aft_dve_chain"), sem("aft_dve_passed")
    s_pool = sem("aft_pool")
    names = ("k", "q", "v", "nb", "ek", "e", "ekv", "ekT", "ekTh", "ekTl", "ekvT", "ekvTh", "ekvTl", "den",
             "num", "y", "yh", "yl", "attn")
    s = {n: sem("aft_s_" + n) for n in names}
    PRE, PER = 1, 37

    with nc.Block() as block:
        @block.sync
        def _(sp):
            sp.dma_start(g.x_res[:, :, :], a["x"].rearrange("(t p) d -> p t d", p=P)).then_inc(s_x, 16)
            sp.dma_start(g.attn[:, :, :], a["ctx"].rearrange("(t p) d -> p t d", p=P)).then_inc(s_ctx, 16)
            sp.dma_start(g.cols[:, :], a["cols"]).then_inc(g.consts, 16)
            sp.dma_start(g.ident[:, :], a["ident"]).then_inc(g.consts, 16)
            sp.dma_start(g.rows[:, :, :].rearrange("p r d -> p (r d)"),
                         a["rows"].rearrange("r d -> (r d)").partition_broadcast(P)).then_inc(g.consts, 16)
            group_dma(sp, g, 0)
            group_dma(sp, g, 1)

        @block.scalar
        def _(act):
            for j, n in enumerate(("wq0", "wk0", "wv0", "wo0")):
                act.dma_start(wst[:, j], a[n].rearrange("(c p) n -> p c n", p=P)).then_inc(s_w, 16)
            act.dma_start(pos[:, :, :], a["pos"].rearrange("(t p) n -> p t n", p=P)).then_inc(s_pos, 16)
            act.wait_ge(s_w, 64)
            act.activation(W[0][:, :, :, :], wst, ACT.Copy).then_inc(s_wh, 1)
            for tt in range(TT):
                act.wait_ge(s_npm, 1)
                act.activation(pos[:, tt, :], pos[:, tt, :], ACT.Exp, bias=npm[:, tt:tt + 1]).then_inc(s_ew, 1)
            for jc in range(TT):
                act.wait_ge(s_ewt, jc + 1)
                act.activation(ewT[0][:, jc, :], KB[jc % 2][:, :], ACT.Copy).then_inc(s_ewh, 1)
            with act.Fori(0, B) as i:
                turn_act(act, tn, 2 * i, lambda c: embT[0][:, c, :])
                for c in range(C):
                    act.wait_ge(s["nb"], i + 1)
                    act.activation(ek[:, c, :], KB[c][:, :], ACT.Exp, bias=km[:, 2, c:c + 1]).then_inc(s["ek"], 1)
                for c in range(C):
                    act.wait_ge(s["q"], 2 * i + c + 1)
                    act.activation(sg[:, c, :], QB[c][:, :], ACT.Exp, bias=nbq[:, c:c + 1], scale=-1.0)\
                       .then_inc(s["e"], 1)
                for src, dst, inn, done in ((KB, ekT, s["ekT"], s["ekTh"]), (VB, ekvT, s["ekvT"], s["ekvTh"])):
                    for j in range(2):
                        act.wait_ge(inn, 2 * i + j + 1)
                        act.activation(dst[0][:, 2 * j:2 * j + 2, :], src[j][:, :].rearrange("p (t d) -> p t d", d=D),
                                       ACT.Copy).then_inc(done, 1)
                for c in range(C):
                    act.wait_ge(s["y"], 2 * i + c + 1)
                    act.activation(yT[0][:, c, :], y[:, c, :], ACT.Copy).then_inc(s["yh"], 1)
                turn_act(act, tn, 2 * i + 1, lambda c: g.xT_of(i)(0, c))

        @block.gpsimd
        def _(pool):
            pool.memset(g.power[:, :], -0.5).then_inc(s_pool, 1)
            pool.wait_ge(s_pos, 16)
            pool.affine_select(out=pos[:, :, :], in_=pos[:, :, :], compare_op=ALU.is_ge, fill=0.0, base=BAND - 1,
                               pattern=[[-P, TT], [1, T]], channel_multiplier=-1).then_inc(s_band, 1)
            pool.wait_ge(s_band, 1)
            pool.affine_select(out=pos[:, :, :], in_=pos[:, :, :], compare_op=ALU.is_ge, fill=0.0, base=BAND - 1,
                               pattern=[[P, TT], [-1, T]], channel_multiplier=1).then_inc(s_band, 1)
            pool.wait_ge(s_pool, 1)
            with pool.Fori(0, B) as i:
                norm_pool(pool, nm, 2 * i, g.power)
                norm_pool(pool, nm, 2 * i + 1, g.power)
            group_split(pool, g, 0)

        @block.vector
        def _(dve):
            dve.sem_inc(tn.lo, C)
            dve.wait_ge(s_wh, 1)
            dve.tensor_tensor(W[1][:, :, :, :], wst, f(W[0][:, :, :, :]), ALU.subtract).then_inc(s_wl, 1)
            dve.wait_ge(g.consts, 48)
            dve.wait_ge(s_x, 16)
            dve.wait_ge(s_ctx, 16)
            dve.tensor_scalar(nbq[:, :], g.cols[:, col_at("bq0"):col_at("bq0") + C], -1.0, None, ALU.mult)\
               .then_inc(s_c, 1)
            dve.wait_ge(s_band, 2)
            dve.tensor_reduce(npm[:, :], pos[:, :, :], AX.X, ALU.max, negate=True).then_inc(s_npm, 1)
            for jc in range(TT):
                dve.wait_ge(s_ewh, jc + 1)
                dve.tensor_tensor(ewT[1][:, jc, :], KB[jc % 2][:, :], f(ewT[0][:, jc, :]), ALU.subtract)\
                   .then_inc(s_ewl, 1)
            with dve.Fori(0, B) as i:
                ch = Chain(dve, s_c, i * PER + PRE, PER, s_pass)
                norm_dve(dve, nm, 2 * i, ch, tile_of(g.x_res, i), own(emb))
                ch.wait()
                dve.tensor_tensor(emb[:, :, :], emb[:, :, :], g.attn[:, ds(i * TT, TT), :], ALU.add)\
                   .then_inc(tn.ready, 1)
                turn_dve(dve, tn, 2 * i, lambda c: embT[0][:, c, :], lambda c: embT[1][:, c, :])
                for c in range(C):
                    dve.wait_ge(s["k"], 2 * i + c + 1)
                    ch.inc(dve.tensor_reduce(km[:, 0, c:c + 1], KB[c][:, :], AX.X, ALU.max))
                ch.wait()
                bk = g.cols[:, col_at("bk0"):col_at("bk0") + C]
                ch.link(dve.tensor_tensor(km[:, 1, :], km[:, 0, :], bk, ALU.add))
                dve.tensor_tensor(km[:, 2, :], bk, km[:, 1, :], ALU.subtract).then_inc(s["nb"], 1)
                for c in range(C):
                    dve.wait_ge(s["v"], 2 * i + c + 1)
                    dve.wait_ge(s["ek"], 2 * i + c + 1)
                    dve.scalar_tensor_tensor(out=ekv[:, c, :], in0=VB[c][:, :], scalar=g.col("bv0", c),
                                             in1=ek[:, c, :], op0=ALU.add, op1=ALU.mult).then_inc(s["ekv"], 1)
                for tt in range(TT):
                    ch.inc(dve.tensor_tensor(emb[:, tt, :], emb[:, tt, :], g.row("bo0"), ALU.add))
                for src, dst, hi, lo in ((KB, ekT, s["ekTh"], s["ekTl"]), (VB, ekvT, s["ekvTh"], s["ekvTl"])):
                    for j in range(2):
                        dve.wait_ge(hi, 2 * i + j + 1)
                        dve.tensor_tensor(dst[1][:, 2 * j:2 * j + 2, :], src[j][:, :].rearrange("p (t d) -> p t d", d=D),
                                          f(dst[0][:, 2 * j:2 * j + 2, :]), ALU.subtract).then_inc(lo, 1)
                dve.wait_ge(s["e"], 2 * i + 2)
                for c in range(C):
                    dve.wait_ge(s["den"], 2 * i + c + 1)
                    ch.inc(dve.scalar_tensor_tensor(out=sg[:, c, :], in0=sg[:, c, :], scalar=1.0, in1=TP[c][:, :],
                                                    op0=ALU.add, op1=ALU.mult))
                ch.wait()
                ch.link(dve.reciprocal(sg[:, :, :], sg[:, :, :]))
                for c in range(C):
                    dve.wait_ge(s["num"], 2 * i + c + 1)
                    dve.tensor_tensor(y[:, c, :], KB[c][:, :], sg[:, c, :], ALU.mult).then_inc(s["y"], 1)
                for c in range(C):
                    dve.wait_ge(s["yh"], 2 * i + c + 1)
                    dve.tensor_tensor(yT[1][:, c, :], y[:, c, :], f(yT[0][:, c, :]), ALU.subtract).then_inc(s["yl"], 1)
                dve.wait_ge(s["attn"], i + 1)
                for j in range(2):
                    ch.inc(dve.tensor_tensor(emb[:, 2 * j:2 * j + 2, :], QB[j][:, :].rearrange("p (t d) -> p t d", d=D),
                                             emb[:, 2 * j:2 * j + 2, :], ALU.add))
                ch.hold()
                norm_dve(dve, nm, 2 * i + 1, ch, own(emb), own(emb), (g.row("gamma"), g.row("beta")))
                ch.hold()
                ch.inc(dve.tensor_copy(g.attn[:, ds(i * TT, TT), :], emb[:, :, :]))
                ch.wait()
                dve.sem_inc(tn.ready, 1)
                turn_dve(dve, tn, 2 * i + 1, lambda c: g.xT_of(i)(0, c), lambda c: g.xT_of(i)(1, c))
                ch.end()

        @block.tensor
        def _(pe):
            pe.wait_ge(g.consts, 48)
            pe.wait_ge(s_ew, TT)
            for jc in range(TT):
                if jc >= 2:
                    pe.wait_ge(s_ewl, jc - 1)
                for tt in range(TT):
                    last = pe.transpose(KB[jc % 2][:, tt * P:(tt + 1) * P], pos[:, tt, jc * P:(jc + 1) * P],
                                        g.ident[:, :])
                last.then_inc(s_ewt, 1)
            pe.wait_ge(s_wl, 1)
            pe.wait_ge(s_ewl, TT)
            with pe.Fori(0, B) as i:
                turn_pe(pe, tn, 2 * i, own(emb), g.ident[:, :])
                pe.wait_ge(tn.lo, 2 * i * C + 2 * C)
                for w, banks, done in ((1, KB, s["k"]), (0, QB, s["q"]), (2, VB, s["v"])):
                    for m in range(C):
                        products(pe, banks[m][:, :], lambda q, c: W[q][:, w, c, m * P:(m + 1) * P],
                                 lambda q, c: embT[q][:, c, :]).then_inc(done, 1)
                for src, banks, inn, done in ((ek, KB, s["ek"], s["ekT"]), (ekv, VB, s["ekv"], s["ekvT"])):
                    pe.wait_ge(inn, 2 * i + 2)
                    for jc in range(TT):
                        for c in range(C):
                            at = (jc % 2) * D + c * P
                            last = pe.transpose(banks[jc // 2][:, at:at + P], src[:, c, jc * P:(jc + 1) * P],
                                                g.ident[:, :])
                        if jc % 2:
                            last.then_inc(done, 1)
                for src, banks, inn, done in ((ekT, TP, s["ekTl"], s["den"]), (ekvT, KB, s["ekvTl"], s["num"])):
                    pe.wait_ge(inn, 2 * i + 2)
                    for c in range(C):
                        products(pe, banks[c][:, :], lambda q, jc: src[q][:, jc, c * P:(c + 1) * P],
                                 lambda q, jc: ewT[q][:, jc, :], chunks=TT).then_inc(done, 1)
                pe.wait_ge(s["yl"], 2 * i + 2)
                for tt in range(TT):
                    last = products(pe, QB[tt // 2][:, (tt % 2) * D:(tt % 2 + 1) * D],
                                    lambda q, c: yT[q][:, c, tt * P:(tt + 1) * P], lambda q, c: W[q][:, 3, c, :],
                                    start=tt % 2 == 0, skip=True)
                last.then_inc(s["attn"], 1)
                turn_pe(pe, tn, 2 * i + 1, own(emb), g.ident[:, :])


def two(row):
    return row.unsqueeze(1).to_broadcast([P, 2, D])


def ffn0_phase(nc, g, sb, ps):
    m = Mlp(sb, ps, g.sem, "ffn0", 1)
    with nc.Block() as block:
        @block.sync
        def _(sp):
            group_dma(sp, g, 2)

        @block.gpsimd
        def _(pool):
            group_split(pool, g, 1)

        @block.tensor
        def _(pe):
            pe.wait_ge(g.w_split, 4)
            mlp_pe(pe, m, lambda q: group_weights(g, 0), g.xT_of)

        @block.scalar
        def _(act):
            mlp_act(act, m, ACT.Relu, lambda tile: g.col("b1_0", tile.t))

        @block.vector
        def _(dve):
            def add_y(q, i, j, y):
                dst = g.attn[:, ds(i * TT + 2 * j, 2), :]
                return dve.tensor_tensor(dst, y, dst, ALU.add)
            mlp_dve(dve, m, add_y)


def router_phase(nc, g, sb, ps):
    a, sem = g.a, g.sem
    r = sb("rt_r", [P, TT, D], F32)
    xn = sb("rt_xn", [P, TT, D], F32)
    rws = sb("rt_rws", [P, C, P], F32)
    RW = [sb(f"rt_rw{p}", [P, C, P], FR) for p in "hl"]
    b2s = sb("rt_b2s", [P, D], F32)
    B2 = [sb(f"rt_b2{p}", [P, D], FR) for p in "hl"]
    lgT = sb("rt_lgT", [P, T], F32)
    lg = sb("rt_lg", [P, TT, E], F32)
    left = sb("rt_left", [P, TT, E], F32)
    top = sb("rt_top", [P, TT, K_TOP], F32)
    ntop = sb("rt_ntop", [P, TT], F32)
    ex = sb("rt_ex", [P, TT, E], F32)
    tot = sb("rt_tot", [P, TT], F32)
    cwx = sb("rt_cwx", [P, TT, GR, 2, EG], FR)
    cwTs = sb("rt_cwTs", [P, T], FR)
    TP = [ps(f"rt_tp{i}", [P, T], F32) for i in range(2)]
    LG, LT, CT = (ps("rt_" + n, [P, T], F32) for n in ("lgp", "ltp", "ctp"))
    YB = [ps(f"rt_yb{i}", [P, 2 * D], F32) for i in range(2)]
    nm, tn = Norm(sb, sem, "rt"), Turn(sem, "rt", TP)
    s_w, s_wh, s_wl, s_c, s_pass = (sem("rt_" + n) for n in ("w_loaded", "w_hi", "w_lo", "dve_chain", "dve_passed"))
    s = {n: sem("rt_s_" + n) for n in ("lg", "lgT", "lt", "ntop", "ex", "cwx", "ct", "cwTs", "yb")}
    PER = 54

    with nc.Block() as block:
        @block.sync
        def _(sp):
            sp.dma_start(rws[:, :, :], a["rw"].rearrange("(c p) n -> p c n", p=P)).then_inc(s_w, 16)
            sp.dma_start(b2s[:, :], a["eb2"]).then_inc(s_w, 16)

        @block.gpsimd
        def _(pool):
            with pool.Fori(0, B) as i:
                norm_pool(pool, nm, 2 * i, g.power)
                norm_pool(pool, nm, 2 * i + 1, g.power)

        @block.scalar
        def _(act):
            act.wait_ge(s_w, 32)
            act.activation(RW[0][:, :, :], rws[:, :, :], ACT.Copy).then_inc(s_wh, 1)
            act.activation(B2[0][:, :], b2s[:, :], ACT.Copy).then_inc(s_wh, 1)
            with act.Fori(0, B) as i:
                turn_act(act, tn, i, lambda c: g.xT_of(i)(0, c))
                act.wait_ge(s["lg"], i + 1)
                act.activation(lgT[:, :], LG[:, :], ACT.Identity, bias=g.col("rb")).then_inc(s["lgT"], 1)
                act.wait_ge(s["ntop"], i + 1)
                for tt in range(TT):
                    act.activation(ex[:, tt, :], lg[:, tt, :], ACT.Exp, bias=ntop[:, tt:tt + 1]).then_inc(s["ex"], 1)
                act.wait_ge(s["ct"], i + 1)
                act.activation(cwTs[:, :], CT[:, :], ACT.Copy).then_inc(s["cwTs"], 1)

        @block.vector
        def _(dve):
            dve.sem_inc(tn.lo, C)
            dve.wait_ge(s_wh, 2)
            dve.tensor_tensor(RW[1][:, :, :], rws[:, :, :], f(RW[0][:, :, :]), ALU.subtract).then_inc(s_wl, 1)
            dve.tensor_tensor(B2[1][:, :], b2s[:, :], f(B2[0][:, :]), ALU.subtract).then_inc(s_wl, 1)
            with dve.Fori(0, B) as i:
                ch = Chain(dve, s_c, i * PER, PER, s_pass)
                x_b = g.x_res[:, ds(i * TT, TT), :]
                at = tile_of(g.attn, i)
                for tt in range(TT):
                    ch.inc(dve.tensor_tensor(r[:, tt, :], at(tt), g.row("b2_0"), ALU.add))
                ch.hold()
                norm_dve(dve, nm, 2 * i, ch, own(r), own(r), (g.row("gamma"), g.row("beta")))
                ch.wait()
                ch.inc(dve.tensor_tensor(x_b, x_b, r[:, :, :], ALU.add))
                ch.hold()
                norm_dve(dve, nm, 2 * i + 1, ch, tile_of(g.x_res, i), own(xn))
                ch.wait()
                dve.sem_inc(tn.ready, 1)
                turn_dve(dve, tn, i, lambda c: g.xT_of(i)(0, c), lambda c: g.xT_of(i)(1, c))
                dve.wait_ge(s["lt"], i + 1)
                ch.inc(dve.tensor_copy(lg[:, :, :], LT[:, :].rearrange("p (t e) -> p t e", t=TT)[:, :, 0:E]))
                ch.hold()
                for tt in range(TT):
                    ch.inc(dve.max(top[:, tt, :], lg[:, tt, :]))
                ch.wait()
                dve.tensor_scalar(ntop[:, :], top[:, :, 0], -1.0, None, ALU.mult).then_inc(s["ntop"], 1)
                for tt in range(TT):
                    ch.inc(dve.match_replace(left[:, tt, :], top[:, tt, :], lg[:, tt, :], -3e38))
                ch.wait()
                ch.link(dve.tensor_tensor(left[:, :, :], lg[:, :, :], left[:, :, :], ALU.not_equal))
                dve.wait_ge(s["ex"], TT * i + TT)
                ch.link(dve.tensor_tensor(ex[:, :, :], ex[:, :, :], left[:, :, :], ALU.mult))
                ch.link(dve.tensor_reduce(tot[:, :], ex[:, :, :], AX.X, ALU.add))
                ch.link(dve.reciprocal(tot[:, :], tot[:, :]))
                for tt in range(TT):
                    ch.inc(dve.tensor_scalar(ex[:, tt, :], ex[:, tt, :], tot[:, tt:tt + 1], None, ALU.mult))
                ch.wait()
                cw = ex[:, :, :].rearrange("p t (g e) -> p t g e", g=GR)
                ch.link(dve.tensor_copy(cwx[:, :, :, 0, :], cw))
                dve.tensor_tensor(cwx[:, :, :, 1, :], cw, f(cwx[:, :, :, 0, :]), ALU.subtract).then_inc(s["cwx"], 1)
                dve.wait_ge(s["cwTs"], i + 1)
                dve.sem_inc(s_pass, 1)
                ch.link(dve.tensor_copy(g.cwT[:, ds(i * T, T)], CT[:, :]))
                dve.wait_ge(s["yb"], i + 1)
                for j in range(2):
                    dst = g.x_res[:, ds(i * TT + 2 * j, 2), :]
                    ch.inc(dve.tensor_tensor(dst, YB[j][:, :].rearrange("p (t d) -> p t d", d=D), dst, ALU.add))
                ch.wait()
                for n in ("sb2a", "sb2b"):
                    for j in range(2):
                        dst = g.x_res[:, ds(i * TT + 2 * j, 2), :]
                        ch.inc(dve.tensor_tensor(dst, dst, two(g.row(n)), ALU.add))
                    ch.wait()
                ch.end()

        @block.tensor
        def _(pe):
            pe.wait_ge(s_wl, 2)
            with pe.Fori(0, B) as i:
                turn_pe(pe, tn, i, own(xn), g.ident[:, :])
                pe.wait_ge(tn.lo, C * i + 2 * C)
                products(pe, LG[:, :], lambda q, c: RW[q][:, c, :], g.xT_of(i)).then_inc(s["lg"], 1)
                pe.wait_ge(s["lgT"], i + 1)
                for tt in range(TT):
                    last = pe.transpose(LT[:, tt * P:(tt + 1) * P], lgT[:, tt * P:(tt + 1) * P], g.ident[:, :])
                last.then_inc(s["lt"], 1)
                pe.wait_ge(s["cwx"], i + 1)
                for tt in range(TT):
                    last = pe.transpose(CT[:, tt * P:(tt + 1) * P],
                                        f(cwx[:, tt, :, :, :].rearrange("p g q e -> p (g q e)")), g.ident[:, :])
                last.then_inc(s["ct"], 1)
                pe.wait_ge(s["cwTs"], i + 1)
                for tt in range(TT):
                    for q in range(2):
                        last = pe.matmul(YB[tt // 2][:, (tt % 2) * D:(tt % 2 + 1) * D], cwTs[:, tt * P:(tt + 1) * P],
                                         B2[q][:, :], start=tt % 2 == 0 and q == 0, stop=q == 1, skip_group_check=True)
                last.then_inc(s["yb"], 1)


def moe_phase(nc, g, sb, ps):
    a, sem = g.a, g.sem
    m = Mlp(sb, ps, sem, "moe", GR + 1, gated=GR)
    SEL = sb("moe_sel", [P, GR * HT, P], FR)
    s_sel, s_selr = sem("moe_sel_loaded"), sem("moe_sel_ready")
    stage = g.attn[:, :, :].rearrange("p t d -> p (t d)")

    with nc.Block() as block:
        @block.sync
        def _(sp):
            sp.dma_start(stage, a["sel_gate"]).then_inc(s_sel, 16)
            for k in range(3, GR + 2):
                group_dma(sp, g, k)

        @block.gpsimd
        def _(pool):
            for k in range(2, GR + 2):
                if k > 2:
                    pool.wait_ge(m.h_used, RING + (k - 2) * B * HT)
                group_split(pool, g, k)

        @block.tensor
        def _(pe):
            pe.wait_ge(s_selr, 1)
            mlp_pe(pe, m, lambda q: group_weights(g, q + 1), g.xT_of,
                   gate=lambda tile: (SEL[:, tile.q * HT + tile.t, :], g.cwT[:, ds(tile.i * T, T)]),
                   new_group=lambda q: pe.wait_ge(g.w_split, 4 * (q + 2)))

        @block.scalar
        def _(act):
            mlp_act(act, m, ACT.Silu,
                    lambda tile: g.col("eb1", tile.q * HT + tile.t) if tile.q < GR else g.col("sb1", tile.t))

        @block.vector
        def _(dve):
            dve.wait_ge(s_sel, 16)
            dve.tensor_copy(SEL[:, :, :].rearrange("p t m -> p (t m)"), stage).then_inc(s_selr, 1)

            def add_y(q, i, j, y):
                dst = g.x_res[:, ds(i * TT + 2 * j, 2), :]
                return dve.tensor_tensor(dst, y, dst, ALU.add)
            mlp_dve(dve, m, add_y)


def norm_loops(block, g, nm, tn, xn, s_c, s_pass, before=None):
    before = before or {}

    def pre(name, eng):
        if name in before:
            before[name](eng)

    @block.gpsimd
    def _(pool):
        with pool.Fori(0, B) as i:
            norm_pool(pool, nm, i, g.power)

    @block.scalar
    def _(act):
        pre("act", act)
        with act.Fori(0, B) as i:
            turn_act(act, tn, i, lambda c: g.xT_of(i)(0, c))

    @block.vector
    def _(dve):
        dve.sem_inc(tn.lo, C)
        pre("dve", dve)
        with dve.Fori(0, B) as i:
            ch = Chain(dve, s_c, i * 2 * TT, 2 * TT, s_pass)
            norm_dve(dve, nm, i, ch, tile_of(g.x_res, i), own(xn))
            ch.wait()
            dve.sem_inc(tn.ready, 1)
            turn_dve(dve, tn, i, lambda c: g.xT_of(i)(0, c), lambda c: g.xT_of(i)(1, c))
            ch.end()

    @block.tensor
    def _(pe):
        pre("pe", pe)
        with pe.Fori(0, B) as i:
            turn_pe(pe, tn, i, own(xn), g.ident[:, :])


def norm_phase(nc, g, sb, ps, name):
    xn = sb(name + "_xn", [P, TT, D], F32)
    TP = [ps(f"{name}_tp{i}", [P, T], F32) for i in range(2)]
    nm, tn, s_c = Norm(sb, g.sem, name), Turn(g.sem, name, TP), g.sem(name + "_dve_chain")
    s_pass = g.sem(name + "_dve_passed")
    with nc.Block() as block:
        norm_loops(block, g, nm, tn, xn, s_c, s_pass)


def attention_phase(nc, g, sb, ps):
    a, sem = g.a, g.sem
    WP = [sb(f"at_w{p}", [P, 3, C, D], FR) for p in "hl"]
    WO = [sb(f"at_wo{p}", [P, HPB, D], FR) for p in "hl"]
    SELK = sb("at_selk", [P, HPB, 2, P], FR)
    SELQ = sb("at_selq", [P, 2 * HPB, 2, P], FR)
    cT = [sb(f"at_cT{p}", [P, C, T], FR) for p in "hl"]
    kT = [sb(f"at_kT{p}", [P, C, T], FR) for p in "hl"]
    qT = cT
    KST = sb("at_kst", [P, HEADS // 2, T], FR)
    QST = sb("at_qst", [P, 2, T], FR)
    VAUG = sb("at_vaug", [P, TT, HEADS, P], FR)
    PTS = [sb(f"at_pt{p}", [P, 2, T], FR) for p in "hl"]
    PR = sb("at_p", [P, 2, TT, T], F32)
    mst = sb("at_mst", [P, 2, T], I32)
    mk = sb("at_mk", [P, TT, T], BF16)
    nid = sb("at_nid", [P, P], BF16)
    nmx = sb("at_nmx", [P, 2, TT], F32)
    den = sb("at_den", [P, TT, HEADS], F32)
    stage = g.w_stage[:, :, :].rearrange("p a n -> p (a n)")
    cst = stage[:, 0:C * T].rearrange("p (c t) -> p c t", c=C)
    OS = stage[:, 1024:3072].rearrange("p (g t) -> p g t", g=HPB)
    vS = stage[:, 3072:4096].rearrange("p (t d) -> p t d", t=TT)
    wst = stage[:, 0:3 * C * D].rearrange("p (w c n) -> p w c n", w=3, c=C)
    wost = stage[:, 1536:2560].rearrange("p (g n) -> p g n", g=HPB)
    selst = PR[:, 0:2, :, :].rearrange("p a b t -> p (a b t)")[:, 0:24 * P]
    NK = 2 * HPB * P
    RDR = PR[:, 0, :, :]
    ON = (KST[:, 0:HPB, :], KST[:, HPB:2 * HPB, :])
    SB = [ps(f"at_s{i}", [P, T], F32) for i in range(2)]
    PT = [ps(f"at_tp{i}", [P, T], F32) for i in range(2)]
    OB = ps("at_o", [P, T], F32)
    QB = ps("at_qb", [P, T], F32)
    MB = [ps(f"at_m{i}", [P, T], F32) for i in range(2)]
    s_w, s_ws, s_wh, s_wl = (sem("at_" + n) for n in ("w_loaded", "sel_split", "w_hi", "w_lo"))
    s_pass = sem("at_dve_passed")
    s_c, s_z, s_nid = sem("at_dve_chain"), sem("at_zeroed"), sem("at_nid_ready")
    names = ("ctx", "cTh", "cTl", "mld", "mk", "mb", "mbf", "kqh", "kql", "v", "kst", "qs", "qst", "s", "nmx", "p",
             "pt", "pth", "ptl", "pv", "os", "rdr", "on", "onh", "onl")
    s = {n: sem("at_s_" + n) for n in names}
    SLOTS = 20
    NP = HEADS * TT
    PER = 19

    with nc.Block() as block:
        @block.sync
        def _(sp):
            for j, n in enumerate(("wq1", "wk1", "wv1")):
                sp.dma_start(wst[:, j], a[n].rearrange("(c p) n -> p c n", p=P)).then_inc(s_w, 16)
            sp.dma_start(wost, a["wo1"].rearrange("(g p) n -> p g n", p=P)).then_inc(s_w, 16)
            sp.dma_start(selst, a["sel_qk"]).then_inc(s_w, 16)
            sp.wait_ge(s_wl, 2)
            with sp.Fori(0, B) as i:
                sp.wait_ge(s["cTl"], i + 1)
                sp.dma_start(cst, a["ctxT"][:, ds(i * T, T)].rearrange("(c p) t -> p c t", p=P)).then_inc(s["ctx"], 16)
                for j in range(2):
                    sp.wait_ge(s["mk"], 2 * i + j + 1)
                    sp.dma_start(mst[:, :, :], a["mask"][ds(i * T + j * 2 * P, 2 * P), :]
                                 .rearrange("(t p) k -> p t k", p=P)).then_inc(s["mld"], 16)

        @block.gpsimd
        def _(pool):
            pool.memset(f(VAUG[:, :, :, :]), 0.0).then_inc(s_z, 1)
            pool.wait_ge(g.consts, 48)
            pool.tensor_scalar(nid[:, :], g.ident[:, :], NEG, 1.0, ALU.mult, ALU.mult).then_inc(s_nid, 1)


        @block.scalar
        def _(act):
            act.wait_ge(s_w, 80)
            act.activation(WP[0][:, :, :, :], wst, ACT.Copy).then_inc(s_wh, 1)
            act.activation(WO[0][:, :, :], wost, ACT.Copy).then_inc(s_wh, 1)
            act.activation(SELK[:, :, :, :].rearrange("p a b m -> p (a b m)"), selst[:, 0:NK], ACT.Copy).then_inc(s_ws, 1)
            act.activation(SELQ[:, :, :, :].rearrange("p a b m -> p (a b m)"), selst[:, NK:], ACT.Copy).then_inc(s_ws, 1)
            act.sem_inc(s["p"], 2)
            act.sem_inc(s["qst"], 2)
            act.wait_ge(s_ws, 2)
            with act.Fori(0, B) as i:
                act.wait_ge(s["ctx"], 16 * i + 16)
                act.activation(cT[0][:, :, :], cst, ACT.Copy).then_inc(s["cTh"], 1)
                for n, (dst, b) in enumerate(((kT, "bk1"), (qT, "bq1"))):
                    for c in range(C):
                        act.wait_ge(s["mb"], SLOTS * i + 4 * n + c + 1)
                        act.activation(dst[0][:, c, :], MB[c][:, :], ACT.Identity, bias=g.col(b, c)).then_inc(s["kqh"], 1)

                def stack(h):
                    act.wait_ge(s["qs"], HEADS * i + h + 1)
                    act.activation(QST[:, h % 2, :], QB[:, :], ACT.Copy).then_inc(s["qst"], 1)

                stack(0)
                for m in range(NP + TT):
                    h, j = divmod(m, TT)
                    if m < NP:
                        if j == 0:
                            act.wait_ge(s["pt"], NP * i + m + 1)
                        act.wait_ge(s["nmx"], NP * i + m + 1)
                        act.activation(PR[:, h % 2, j, :], SB[j % 2][:, :], ACT.Exp, bias=nmx[:, h % 2, j:j + 1],
                                       accum_out=den[:, j, h:h + 1]).then_inc(s["p"], 1)
                    if m >= TT:
                        n = NP * i + m - TT
                        act.wait_ge(s["pt"], n + 6)
                        act.wait_ge(s["pv"], n + 1)
                        act.activation(PTS[0][:, j % 2, :], PT[j % 2][:, :], ACT.Copy).then_inc(s["pth"], 1)
                    if j == 1 and h + 1 < HEADS:
                        stack(h + 1)
                for q in range(HPB):
                    act.wait_ge(s["on"], HPB * i + q + 1)
                    act.activation(ON[0][:, q, :], OS[:, q, :], ACT.Copy).then_inc(s["onh"], 1)

        @block.vector
        def _(dve):
            dve.wait_ge(s_wh, 2)
            dve.tensor_tensor(WP[1][:, :, :, :], wst, f(WP[0][:, :, :, :]), ALU.subtract).then_inc(s_wl, 1)
            dve.tensor_tensor(WO[1][:, :, :], wost, f(WO[0][:, :, :]), ALU.subtract).then_inc(s_wl, 1)
            dve.sem_inc(s["cTl"], 1)
            dve.sem_inc(s["mk"], 1)
            dve.sem_inc(s["mbf"], 2)
            dve.sem_inc(s["ptl"], 2)
            dve.sem_inc(s["os"], 1)
            dve.wait_ge(s_z, 1)
            with dve.Fori(0, B) as i:
                ch = Chain(dve, s_c, i * PER, PER, s_pass)

                def mask(j):
                    dve.wait_ge(s["mld"], 32 * i + 16 * j + 16)
                    dve.tensor_scalar(mk[:, 2 * j:2 * j + 2, :], mst[:, :, :], 1.0, None, ALU.is_equal).then_inc(s["mk"], 1)

                dve.wait_ge(s["cTh"], i + 1)
                dve.tensor_tensor(cT[1][:, :, :], cst, f(cT[0][:, :, :]), ALU.subtract).then_inc(s["cTl"], 1)
                mask(0)
                def low(n, dst, b):
                    for c in range(C):
                        dve.wait_ge(s["kqh"], 2 * C * i + 2 * n + c + 1)
                        dve.scalar_tensor_tensor(out=dst[1][:, c, :], in0=MB[c][:, :], scalar=g.col(b, c),
                                                 in1=f(dst[0][:, c, :]), op0=ALU.add, op1=ALU.subtract)\
                           .then_inc(s["mbf"], 1)

                low(0, kT, "bk1")
                for j in range(2):
                    dve.wait_ge(s["mb"], SLOTS * i + 2 + j + 1)
                    dve.tensor_tensor(vS[:, 2 * j:2 * j + 2, :], MB[j][:, :].rearrange("p (t d) -> p t d", d=D),
                                      two(g.row("bv1")), ALU.add).then_inc(s["mbf"], 1)
                mask(1)
                low(1, qT, "bq1")
                dve.wait_ge(s["mbf"], SLOTS * i + 4 + 2)
                vh = vS.rearrange("p t (h d) -> p t h d", d=HD)
                for j in range(HPB):
                    ch.inc(dve.tensor_copy(VAUG[:, :, j::HPB, 2 * HD * j:2 * HD * j + HD], vh[:, :, j::HPB, :]))
                ch.wait()
                for j in range(HPB):
                    ch.inc(dve.tensor_tensor(VAUG[:, :, j::HPB, 2 * HD * j + HD:2 * HD * (j + 1)], vh[:, :, j::HPB, :],
                                             f(VAUG[:, :, j::HPB, 2 * HD * j:2 * HD * j + HD]), ALU.subtract))
                ch.wait()
                dve.sem_inc(s["v"], 1)
                for p in range(HEADS // 2):
                    dve.wait_ge(s["mb"], SLOTS * i + 6 + p + 1)
                    dve.tensor_copy(KST[:, p, :], MB[p % 2][:, :]).then_inc(s["mbf"], 1)

                def take(q):
                    dve.wait_ge(s["pv"], NP * i + TT * HPB * (q + 1) + 2)
                    dve.tensor_copy(OS[:, q, :], OB[:, :]).then_inc(s["os"], 1)

                for m in range(NP + TT + 1):
                    h, j = divmod(m, TT)
                    if m < NP:
                        dve.wait_ge(s["s"], NP * i + m + 1)
                        dve.tensor_reduce(nmx[:, h % 2, j:j + 1], SB[j % 2][:, :], AX.X, ALU.max, negate=True)\
                           .then_inc(s["nmx"], 1)
                    k = m - TT - 1
                    if k > 0 and k % (TT * HPB) == 0:
                        take(k // (TT * HPB) - 1)
                    if k >= 0:
                        dve.wait_ge(s["pth"], NP * i + k + 1)
                        dve.tensor_tensor(PTS[1][:, k % 2, :], PT[k % 2][:, :], f(PTS[0][:, k % 2, :]), ALU.subtract)\
                           .then_inc(s["ptl"], 1)
                take(HPB - 1)
                dve.wait_ge(s["p"], NP * i + NP + 2)
                ch.link(dve.reciprocal(den[:, :, :], den[:, :, :]))
                dve.tensor_copy(RDR.rearrange("p t (h r) -> p (t h) r", r=2 * HD),
                                den[:, :, :].rearrange("p t h -> p (t h)").unsqueeze(2).to_broadcast(
                                    [P, TT * HEADS, 2 * HD])).then_inc(s["rdr"], 1)
                for q in range(HPB):
                    dve.wait_ge(s["mb"], SLOTS * i + 14 + q + 1)
                    dve.wait_ge(s["os"], HPB * i + q + 2)
                    ch.link(dve.tensor_tensor(OS[:, q, :], OS[:, q, :], MB[q % 2][:, :], ALU.mult))
                    dve.sem_inc(s["mbf"], 1)
                    dve.sem_inc(s["on"], 1)
                for q in range(HPB):
                    dve.wait_ge(s["onh"], HPB * i + q + 1)
                    dve.tensor_tensor(ON[1][:, q, :], OS[:, q, :], f(ON[0][:, q, :]), ALU.subtract).then_inc(s["onl"], 1)
                for tt in range(TT):
                    dst = tile_of(g.x_res, i)(tt)
                    ch.inc(dve.tensor_tensor(dst, dst, g.row("bo1"), ALU.add))
                ch.wait()
                for j in range(2):
                    dve.wait_ge(s["mb"], SLOTS * i + 18 + j + 1)
                    dst = g.x_res[:, ds(i * TT + 2 * j, 2), :]
                    ch.link(dve.tensor_tensor(dst, MB[j][:, :].rearrange("p (t d) -> p t d", d=D), dst, ALU.add))
                    dve.sem_inc(s["mbf"], 1)
                ch.end()

        @block.tensor
        def _(pe):
            pe.wait_ge(s_wl, 2)
            pe.wait_ge(s_ws, 2)
            pe.wait_ge(s_nid, 1)
            pe.sem_inc(s["pv"], 2)
            pe.sem_inc(s["pt"], 5)
            with pe.Fori(0, B) as i:
                slot = [0]

                def bank():
                    n = slot[0]
                    slot[0] += 1
                    pe.wait_ge(s["mbf"], SLOTS * i + n + 1)
                    return MB[n % 2]

                pe.wait_ge(s["cTl"], i + 2)
                def project(w, src):
                    for m in range(C):
                        products(pe, bank()[:, :], lambda q, c: WP[q][:, w, c, m * P:(m + 1) * P], src)\
                            .then_inc(s["mb"], 1)

                project(1, lambda q, c: cT[q][:, c, :])
                for j in range(2):
                    bk = bank()
                    for kc in (2 * j, 2 * j + 1):
                        last = products(pe, bk[:, (kc % 2) * D:(kc % 2 + 1) * D],
                                        lambda q, c: cT[q][:, c, kc * P:(kc + 1) * P], lambda q, c: WP[q][:, 2, c, :],
                                        start=kc % 2 == 0, skip=True)
                    last.then_inc(s["mb"], 1)
                project(0, g.xT_of(i))
                for p in range(HEADS // 2):
                    bk = bank()
                    for q in range(2):
                        last = pe.matmul(bk[:, :], SELK[:, p % HPB, q, :], kT[q][:, p // HPB, :], start=q == 0, stop=q == 1)
                    last.then_inc(s["mb"], 1)

                def stack(h):
                    pe.wait_ge(s["qst"], HEADS * i + h + 2)
                    for q in range(2):
                        last = pe.matmul(QB[:, :], SELQ[:, h % (2 * HPB), q, :], qT[q][:, h // (2 * HPB), :],
                                         start=q == 0, stop=q == 1)
                    last.then_inc(s["qs"], 1)

                def weigh(h, kc):
                    n = NP * i + TT * h + kc
                    pe.wait_ge(s["ptl"], n + 3)
                    if h % HPB == 0 and kc == 0:
                        pe.wait_ge(s["os"], HPB * i + h // HPB + 1)
                    for q in range(2):
                        last = pe.matmul(OB[:, :], VAUG[:, kc, h, :], PTS[q][:, kc % 2, :],
                                         start=h % HPB == 0 and kc == 0 and q == 0,
                                         stop=h % HPB == HPB - 1 and kc == TT - 1 and q == 1)
                    last.then_inc(s["pv"], 1)

                stack(0)
                pe.wait_ge(s["mbf"], SLOTS * i + 16)
                pe.wait_ge(s["v"], i + 1)

                def score(m):
                    h, j = divmod(m, TT)
                    if j == 0:
                        pe.wait_ge(s["qst"], HEADS * i + h + 3)
                    pe.wait_ge(s["p"], NP * i + m + 1)
                    pe.matmul(SB[j % 2][:, :], nid[:, :], mk[:, j, :], start=True, stop=False)
                    pe.matmul(SB[j % 2][:, :], QST[:, h % 2, j * P:(j + 1) * P], KST[:, h // 2, :],
                              start=False, stop=True).then_inc(s["s"], 1)

                score(0)
                for m in range(NP + TT + 1):
                    h, j = divmod(m, TT)
                    if m + 1 < NP:
                        score(m + 1)
                    if TT <= m < NP + TT:
                        if j == 0:
                            pe.wait_ge(s["p"], NP * i + m + 2)
                        pe.wait_ge(s["ptl"], NP * i + m - TT + 1)
                        for t in range(TT):
                            last = pe.transpose(PT[j % 2][:, t * P:(t + 1) * P],
                                                PR[:, (h - 1) % 2, t, j * P:(j + 1) * P], g.ident[:, :])
                        last.then_inc(s["pt"], 1)
                    if m > TT:
                        weigh(*divmod(m - TT - 1, TT))
                    if j == 0 and h + 1 < HEADS:
                        stack(h + 1)
                pe.wait_ge(s["rdr"], i + 1)
                for q in range(HPB):
                    bk = bank()
                    for t in range(TT):
                        last = pe.transpose(bk[:, t * P:(t + 1) * P], RDR[:, t, q * P:(q + 1) * P], g.ident[:, :])
                    last.then_inc(s["mb"], 1)
                pe.wait_ge(s["onl"], HPB * i + HPB)
                for j in range(2):
                    bk = bank()
                    for tt in (2 * j, 2 * j + 1):
                        last = products(pe, bk[:, (tt % 2) * D:(tt % 2 + 1) * D],
                                        lambda q, c: ON[q][:, c, tt * P:(tt + 1) * P], lambda q, c: WO[q][:, c, :],
                                        chunks=HPB, start=tt % 2 == 0, skip=True)
                    last.then_inc(s["mb"], 1)
                assert slot[0] == SLOTS


def binary_phase(nc, g, sb, ps):
    a, sem = g.a, g.sem
    xn = sb("bi_xn", [P, TT, D], F32)
    mag = sb("bi_mag", [P, 2, 2 * H], F32)
    low = sb("bi_low", [P, 2, 2 * H], F32)
    ones = sb("bi_ones", [P, P], F32)
    TP = [ps(f"bi_tp{i}", [P, T], F32) for i in range(2)]
    A1, A2 = ps("bi_a1", [P, HT, 2], F32), ps("bi_a2", [P, D], F32)
    nm, tn, s_c = Norm(sb, sem, "bi"), Turn(sem, "bi", TP), sem("bi_dve_chain")
    s_pass = sem("bi_dve_passed")
    s_l, s_m, s_o, s_low, s_a, s_al = (sem("bi_" + n) for n in ("loaded", "mag", "ones", "low", "sums", "alphas"))
    S = (g.S1[:, :, :].rearrange("p c n -> p (c n)"), g.S2[:, :, :].rearrange("p c n -> p (c n)"))

    def act_part(act):
        act.wait_ge(s_l, 32)
        for j in range(2):
            act.activation(mag[:, j, :], g.w_stage[:, j, :], ACT.Abs).then_inc(s_m, 1)

    def dve_part(dve):
        dve.memset(ones[:, :], 1.0).then_inc(s_o, 1)
        dve.wait_ge(s_l, 32)
        for j in range(2):
            dve.tensor_scalar(low[:, j, :], g.w_stage[:, j, :], 0.0, None, ALU.is_lt).then_inc(s_low, 1)
            dve.wait_ge(s_low, 2 * j + 1)
            dve.scalar_tensor_tensor(out=S[j], in0=g.w_stage[:, j, :], scalar=0.0, in1=low[:, j, :], op0=ALU.is_gt,
                                     op1=ALU.subtract).then_inc(s_low, 1)
        dve.wait_ge(s_a, 2)
        dve.tensor_scalar(g.alpha1[:, :], A1[:, :, 0], 1.0 / D, None, ALU.mult).then_inc(s_al, 1)
        dve.tensor_scalar(g.alpha2[:, :], A2[:, :], 1.0 / H, None, ALU.mult).then_inc(s_al, 1)

    def pe_part(pe):
        pe.wait_ge(s_m, 2)
        pe.wait_ge(s_o, 1)
        for t in range(HT):
            for c in range(C):
                at = c * H + t * P
                last = pe.matmul(A1[:, t, :], mag[:, 0, at:at + P], ones[:, 0:2], start=t == 0 and c == 0, stop=c == C - 1,
                                 skip_group_check=True)
        last.then_inc(s_a, 1)
        for t in range(HT):
            last = pe.matmul(A2[:, :], ones[:, :], mag[:, 1, t * D:(t + 1) * D], start=t == 0, stop=t == HT - 1)
        last.then_inc(s_a, 1)

    with nc.Block() as block:
        @block.sync
        def _(sp):
            sp.dma_start(g.w_stage[:, 0, :].rearrange("p (c n) -> p c n", c=C),
                         a["w1_1"].rearrange("(c p) n -> p c n", p=P)).then_inc(s_l, 16)
            sp.dma_start(g.w_stage[:, 1, :].rearrange("p (t n) -> p t n", t=HT),
                         a["w2_1"].rearrange("(t p) n -> p t n", p=P)).then_inc(s_l, 16)

        norm_loops(block, g, nm, tn, xn, s_c, s_pass, {"act": act_part, "dve": dve_part, "pe": pe_part})


def ffn1_phase(nc, g, sb, ps):
    m = Mlp(sb, ps, g.sem, "ffn1", 1)
    fin = sb("f1_fin", [P, 2, 2, D], F32)
    s_c, s_out = g.sem("f1_dve_chain"), g.sem("out_stored")
    o = g.out.rearrange("(t p) d -> p t d", p=P)
    PER = 5
    with nc.Block() as block:
        @block.sync
        def _(sp):
            with sp.Fori(0, B) as i:
                sp.wait_ge(m.y_used, i + 2)
                sp.dma_start(o[:, ds(i * TT, TT), :], g.x_res[:, ds(i * TT, TT), :]).then_inc(s_out, 16)
            sp.wait_ge(s_out, 16 * B)

        @block.tensor
        def _(pe):
            weights = (lambda q, c, t: g.S1[:, c, t * P:(t + 1) * P]), (lambda q, t: g.S2[:, t, :])
            mlp_pe(pe, m, lambda q: weights, g.xT_of, p1=((0, 0), (0, 1)), p2=((0, 0), (1, 0)))

        @block.scalar
        def _(act):
            mlp_act(act, m, ACT.Gelu, lambda tile: g.col("b1_1", tile.t),
                    scale=lambda tile: g.alpha1[:, tile.t:tile.t + 1])

        @block.vector
        def _(dve):
            chains = {}

            def add_y(q, i, j, y):
                if j == 0:
                    chains["batch"] = Chain(dve, s_c, i * PER, PER)
                ch = chains["batch"]
                dst = g.x_res[:, ds(i * TT + 2 * j, 2), :]
                ch.link(dve.tensor_tensor(fin[:, j], y, two(g.alpha2[:, :]), ALU.mult))
                ch.link(dve.tensor_tensor(fin[:, j], fin[:, j], two(g.row("b2_1")), ALU.add))
                ins = dve.tensor_tensor(dst, dst, fin[:, j], ALU.add)
                if j == 0:
                    ch.inc(ins)
                else:
                    ch.end()
                return ins
            mlp_dve(dve, m, add_y)


def gate_selector():
    import numpy as np
    row = np.arange(P)
    expert = (row // (2 * EG)) * EG + row % EG
    return (expert[:, None] == np.arange(E * HE)[None, :] // HE).astype(np.float32)


def stack_selectors():
    import numpy as np
    feat, m = np.arange(P)[:, None], np.arange(P)[None, :]
    out = []
    for p in range(HPB):
        for q in range(2):
            out.append((feat == 2 * HD * p + m % (2 * HD)) & (m // (2 * HD) % 2 == q))
    for h in range(2 * HPB):
        for q in range(2):
            out.append(((feat == 2 * HD * (h // 2) + m % (2 * HD)) & (m % (2 * HD) // HD == h % 2)
                        & (m // (2 * HD) // 2 == q)) * np.float32(HD ** -0.5))
    return np.concatenate([x.astype(np.float32) for x in out], axis=1)


def kernel(**inputs):
    import numpy as np
    import concourse.bacc as bacc
    from concourse.bass_utils import run_bass_kernel_spmd as run

    v = {k: np.asarray(x) for k, x in inputs.items()}
    cc = np.ascontiguousarray

    def cols(x):
        return cc(x.reshape(-1, P).T)

    rb, eb2 = v["L0_ffn_router_b"], v["L0_ffn_b2"]
    col = {"bq0": v["L0_xattn_bq"], "bk0": v["L0_xattn_bk"], "bv0": v["L0_xattn_bv"], "b1_0": v["L0_xattn_b1"],
           "rb": np.concatenate([rb, rb]), "eb1": v["L0_ffn_b1"], "sb1": v["L0_ffn_sb1"], "bq1": v["L1_xattn_bq"],
           "bk1": v["L1_xattn_bk"], "b1_1": v["L1_ffn_b1"]}
    row = {"bo0": v["L0_xattn_bo"], "gamma": v["L0_xattn_gamma"], "beta": v["L0_xattn_beta"], "b2_0": v["L0_xattn_b2"],
           "sb2a": v["L0_ffn_sb2"][0], "sb2b": v["L0_ffn_sb2"][1], "bv1": v["L1_xattn_bv"], "bo1": v["L1_xattn_bo"],
           "b2_1": v["L1_ffn_b2"]}
    rw = v["L0_ffn_router_w"]
    wo1 = v["L1_xattn_Wo"].T.reshape(HEADS, 1, HD, D)
    arrays = {
        "x": v["x"].reshape(B * T, D), "ctx": v["ctx_1024"].reshape(B * T, D),
        "ctxT": cc(v["ctx_1024"].reshape(B * T, D).T), "mask": v["mask_Bx1xSxS2_ik1"].reshape(B * T, T),
        "cols": cc(np.concatenate([cols(col[n]) for n in COLS], axis=1)),
        "rows": cc(np.stack([row[n] for n in ROWS])), "ident": np.eye(P, dtype=np.float32),
        "pos": v["L0_xattn_pos_bias"],
        "wq0": v["L0_xattn_wq"], "wk0": v["L0_xattn_wk"], "wv0": v["L0_xattn_wv"], "wo0": v["L0_xattn_wo"],
        "w1_0": v["L0_xattn_w1"], "w2_0": v["L0_xattn_w2"],
        "rw": cc(np.concatenate([rw, rw], axis=1)),
        "eb2": cc(np.broadcast_to(eb2.reshape(GR, 1, EG, D), (GR, 2, EG, D)).reshape(P, D)),
        "ew1": cc(v["L0_ffn_w1"].transpose(1, 0, 2).reshape(D, E * HE)), "ew2": v["L0_ffn_w2"].reshape(E * HE, D),
        "sw1": cc(v["L0_ffn_sw1"].transpose(1, 0, 2).reshape(D, H)), "sw2": v["L0_ffn_sw2"].reshape(H, D),
        "sel_gate": gate_selector(), "sel_qk": stack_selectors(),
        "wq1": cc(v["L1_xattn_Wq"].T), "wk1": cc(v["L1_xattn_Wk"].T), "wv1": cc(v["L1_xattn_Wv"].T),
        "wo1": cc(np.broadcast_to(wo1, (HEADS, 2, HD, D)).reshape(HEADS * 2 * HD, D)),
        "w1_1": cc(v["L1_ffn_w1"].T), "w2_1": cc(v["L1_ffn_w2"].T),
    }
    nc = bacc.Bacc("TRN2", target_bir_lowering=False, num_devices=1)
    aps, ins = {}, {}
    for n, x in arrays.items():
        ins["in_" + n] = cc(x)
        aps[n] = nc.dram_tensor("in_" + n, x.shape, mybir.dt.from_np(x.dtype), kind="ExternalInput").ap()
    out = nc.dram_tensor("out", (B * T, D), F32, kind="ExternalOutput").ap()
    build(nc, aps, out)
    r = run(nc, [ins], core_ids=[0])
    return r.results[0]["out"].reshape(B, T, D)
```

```python
from contextlib import ExitStack

import concourse.bass as bass
from concourse import mybir

F32 = mybir.dt.float32
FR = mybir.dt.float32r
BF16 = mybir.dt.bfloat16
I32 = mybir.dt.int32
ALU = mybir.AluOpType
ACT = mybir.ActivationFunctionType
AX = mybir.AxisListType
ds = bass.ds

P = 128
B, T, D, H = 4, 512, 256, 1024
C = D // P
NT = B * T // P
TT = T // P
HT = H // P
E, K_TOP, HE = 64, 8, 64
GR = E * HE // H
EG = E // GR
HEADS, HD = 16, 16
HPB = 4
BAND = 64
EPS = 1e-5
NEG = -(2.0 ** 100)
PASSES = ((0, 0), (1, 0), (0, 1))


class Shared:
    pass


class Chain:

    def __init__(self, eng, sem, start, per, passed=None):
        self.eng, self.sem, self.start, self.per, self.passed, self.k = eng, sem, start, per, passed, 0

    def inc(self, ins):
        self.k += 1
        ins.then_inc(self.sem, 1)

    def wait(self):
        self.eng.wait_ge(self.sem, self.start + self.k)

    def hold(self):
        self.wait()
        self.eng.sem_inc(self.passed, 1)

    def link(self, ins):
        self.inc(ins)
        self.wait()

    def end(self):
        assert self.k == self.per, (self.k, self.per)


def f(ap):
    return ap.bitcast(F32)


class Norm:

    def __init__(self, sb, sem, name):
        self.st6 = sb(name + "_st6", [P, TT, 6], F32)
        self.mv = sb(name + "_mv", [P, TT, 2], F32)
        self.var = sb(name + "_var", [P, TT], F32)
        self.rstd = sb(name + "_rstd", [P, TT], F32)
        self.stats = sem(name + "_stats")
        self.var_eps = sem(name + "_var_eps")
        self.root = sem(name + "_root")
        self.passed = sem("pool_passed")


def norm_stats(dve, nm, chain, src):
    for tt in range(TT):
        chain.inc(dve.bn_stats(nm.st6[:, tt, :], src(tt)))
    chain.hold()
    for tt in range(TT):
        dve.bn_aggr(nm.mv[:, tt, :], nm.st6[:, tt, :]).then_inc(nm.stats, 1)


def norm_apply(dve, nm, n, chain, src, dst):
    dve.wait_ge(nm.root, n + 1)
    for tt in range(TT):
        chain.inc(dve.tensor_scalar(dst(tt), src(tt), nm.mv[:, tt, 0:1], nm.rstd[:, tt:tt + 1],
                                    ALU.subtract, ALU.mult))


def norm_scaled(dve, nm, n, chain, src, mid, gamma, shift, dst):
    dve.wait_ge(nm.root, n + 1)
    for tt in range(TT):
        chain.inc(dve.scalar_tensor_tensor(out=mid(tt), in0=src(tt), scalar=nm.mv[:, tt, 0:1], in1=gamma,
                                           op0=ALU.subtract, op1=ALU.mult))
    chain.wait()
    for tt in range(TT):
        chain.inc(dve.scalar_tensor_tensor(out=dst(tt), in0=mid(tt), scalar=nm.rstd[:, tt:tt + 1], in1=shift(tt),
                                           op0=ALU.mult, op1=ALU.add))


def norm_pool(pool, nm, n, power):
    pool.wait_ge(nm.stats, n * TT + TT)
    pool.sem_inc(nm.passed, 1)
    pool.tensor_scalar(nm.var[:, :], nm.mv[:, :, 1], EPS, 0.0, ALU.add, ALU.add).then_inc(nm.var_eps, 1)
    pool.wait_ge(nm.var_eps, n + 1)
    pool.tensor_tensor(nm.rstd[:, :], nm.var[:, :], power[:, 0:TT], ALU.pow).then_inc(nm.root, 1)


class Turn:

    def __init__(self, sem, name, banks):
        self.banks = banks
        self.ready = sem(name + "_turn_in")
        self.turned = sem(name + "_turned")
        self.hi = sem(name + "_turn_hi")
        self.lo = sem(name + "_turn_lo")


def turn_pe(pe, tn, n, src, ident):
    pe.wait_ge(tn.ready, n + 1)
    for c in range(C):
        pe.wait_ge(tn.lo, n * C + c + 1)
        for tt in range(TT):
            last = pe.transpose(tn.banks[c][:, tt * P:(tt + 1) * P], src(tt)[:, c * P:(c + 1) * P], ident)
        last.then_inc(tn.turned, 1)


def turn_act(act, tn, n, hi):
    for c in range(C):
        act.wait_ge(tn.turned, n * C + c + 1)
        act.activation(hi(c), tn.banks[c][:, :], ACT.Copy).then_inc(tn.hi, 1)


def turn_dve(dve, tn, n, hi, lo):
    for c in range(C):
        dve.wait_ge(tn.hi, n * C + c + 1)
        dve.tensor_tensor(lo(c), tn.banks[c][:, :], f(hi(c)), ALU.subtract).then_inc(tn.lo, 1)


def products(pe, out, lhs, rhs, chunks=C, passes=PASSES, start=True, stop=True, skip=False):
    n, m = 0, chunks * len(passes)
    for c in range(chunks):
        for a, b in passes:
            last = pe.matmul(out, lhs(a, c), rhs(b, c), start=start and n == 0, stop=stop and n == m - 1,
                             skip_group_check=skip)
            n += 1
    return last


RING = 4
LAG = 2


class Mlp:

    def __init__(self, sb, ps, sem, name, groups, gated=0):
        self.groups, self.gated = groups, gated
        self.hid = [ps(f"{name}_hid{i}", [P, T], F32) for i in range(2)]
        self.y = [ps(f"{name}_y{i}", [P, 2 * D], F32) for i in range(2)]
        self.hs = sb(name + "_hs", [P, 2, T], F32)
        self.h = [sb(f"{name}_h{'hl'[i]}", [P, RING, T], FR) for i in range(2)]
        if gated:
            self.gate = [ps(f"{name}_gate{i}", [P, T], F32) for i in range(2)]
            self.ms = sb(name + "_ms", [P, RING, T], F32)
            self.gate_ready = sem(name + "_gate_ready")
            self.gate_used = sem(name + "_gated")
        self.hid_ready = sem(name + "_hid_ready")
        self.activated = sem(name + "_activated")
        self.hi_gated = sem(name + "_hi_gated")
        self.hi_plain = sem(name + "_hi_plain")
        self.split = sem(name + "_split")
        self.h_used = sem(name + "_h_used")
        self.y_used = sem(name + "_y_used")


class Tile:

    def __init__(self, q, i, s, first=False):
        self.first = first
        self.q, self.i, self.t, self.n = q, i, s, q * B * HT + i * HT + s
        if s >= HT:
            self.i, self.t = i + 1, s - HT


def mlp_stream(eng, m, step, batch_end=None):
    for s in range(LAG):
        step(Tile(0, 0, s, s == 0), Tile(0, 0, s - 1) if s else None, None)

    def batch(q, i, peeled):
        def at(s):
            if not peeled or s < HT:
                return Tile(q, i, s)
            return Tile(q + 1, 0, s - HT, s == HT) if q + 1 < m.groups else None
        for s in range(LAG, HT + LAG):
            step(at(s), at(s - 1), at(s - LAG))
        if batch_end is not None:
            batch_end(q, i)

    for q in range(m.groups):
        with eng.Fori(0, B - 1) as i:
            batch(q, i, False)
        batch(q, B - 1, True)


def mlp_pe(pe, m, weights, xt, gate=None, new_group=None, p1=PASSES, p2=PASSES):
    pe.sem_inc(m.h_used, RING)

    def step(cur, _, back):
        if cur is not None:
            if new_group is not None and cur.first:
                new_group(cur.q)
            pe.wait_ge(m.activated, cur.n + 1)
            x = xt(cur.i)
            w1 = weights(cur.q)[0]
            products(pe, m.hid[cur.t % 2][:, :], lambda a, c: w1(a, c, cur.t), x, passes=p1).then_inc(m.hid_ready, 1)
            if cur.q < m.gated:
                pe.wait_ge(m.gate_used, cur.n + 1)
                pe.matmul(m.gate[cur.t % 2][:, :], *gate(cur), start=True, stop=True).then_inc(m.gate_ready, 1)
        if back is not None:
            t, w2 = back.t, weights(back.q)[1]
            pe.wait_ge(m.split, back.n + 1 + RING)
            if t == 0:
                pe.wait_ge(m.y_used, back.q * B + back.i + 1)
            for tt in range(TT):
                last = products(pe, m.y[tt // 2][:, (tt % 2) * D:(tt % 2 + 1) * D],
                                lambda a, c: m.h[a][:, t % RING, tt * P:(tt + 1) * P], lambda b, c: w2(b, t), chunks=1,
                                passes=p2, start=t == 0 and tt % 2 == 0, stop=t == HT - 1, skip=True)
            last.then_inc(m.h_used, 1)

    mlp_stream(pe, m, step)


def mlp_act(act, m, func, bias, scale=None):
    act.sem_inc(m.activated, 2)

    def step(cur, prev, _):
        if cur is not None:
            act.wait_ge(m.hid_ready, cur.n + 1)
            if cur.q < m.gated:
                act.wait_ge(m.gate_used, cur.n + 1)
            else:
                act.wait_ge(m.split, cur.n + RING - 1)
            act.activation(m.hs[:, cur.t % 2, :], m.hid[cur.t % 2][:, :], func, bias=bias(cur),
                           scale=1.0 if scale is None else scale(cur)).then_inc(m.activated, 1)
        if prev is not None and prev.q < m.gated:
            act.wait_ge(m.gate_used, prev.n + 3)
            act.wait_ge(m.h_used, prev.n + 1)
            act.activation(m.h[0][:, prev.t % RING, :], m.ms[:, prev.t % RING, :], ACT.Copy).then_inc(m.hi_gated, 1)

    mlp_stream(act, m, step)


def mlp_dve(dve, m, add_y):
    dve.sem_inc(m.split, RING)
    dve.sem_inc(m.y_used, 1)
    if m.gated:
        dve.sem_inc(m.gate_used, 2)

    def step(cur, prev, _):
        if cur is not None:
            r = cur.t % RING
            dve.wait_ge(m.activated, cur.n + 3)
            if cur.q < m.gated:
                dve.wait_ge(m.gate_ready, cur.n + 1)
                dve.wait_ge(m.split, cur.n + 1)
                dve.tensor_tensor(m.ms[:, r, :], m.hs[:, cur.t % 2, :], m.gate[cur.t % 2][:, :], ALU.mult)\
                   .then_inc(m.gate_used, 1)
            else:
                dve.wait_ge(m.h_used, cur.n + 1)
                dve.tensor_copy(m.h[0][:, r, :], m.hs[:, cur.t % 2, :]).then_inc(m.hi_plain, 1)
        if prev is not None:
            r = prev.t % RING
            src = m.ms[:, r, :] if prev.q < m.gated else m.hs[:, prev.t % 2, :]
            if prev.q < m.gated:
                dve.wait_ge(m.hi_gated, prev.n + 1)
            else:
                dve.wait_ge(m.hi_plain, prev.n + 1 - m.gated * B * HT)
            dve.tensor_tensor(m.h[1][:, r, :], src, f(m.h[0][:, r, :]), ALU.subtract).then_inc(m.split, 1)

    def batch_end(q, i):
        dve.wait_ge(m.h_used, Tile(q, i, HT).n + RING)
        for j in range(2):
            last = add_y(q, i, j, m.y[j][:, :].rearrange("p (t d) -> p t d", d=D))
        last.then_inc(m.y_used, 1)

    mlp_stream(dve, m, step, batch_end)


COLS = {"bq0": C, "bk0": C, "bv0": C, "b1_0": HT, "rb": 1, "eb1": GR * HT, "sb1": HT, "bq1": C, "bk1": C,
        "b1_1": HT}
ROWS = ("bo0", "gamma", "beta", "b2_0", "sb2a", "sb2b", "bv1", "bo1", "b2_1")


def col_at(name, j=0):
    names = list(COLS)
    return sum(COLS[n] for n in names[:names.index(name)]) + j


def tile_of(buf, i):
    return lambda tt: buf[:, ds(i * TT + tt, 1), :].rearrange("p a d -> p (a d)")


def own(buf):
    return lambda tt: buf[:, tt, :]


def split_dma(sp, s, dst, srcs):
    for j, src in enumerate(srcs):
        sp.dma_start(dst[:, j], src.rearrange("(c p) n -> p c n", p=P)).then_inc(s, 16)


def build(nc, a, out):
    with ExitStack() as whole:
        def maker(stack):
            def sb(name, shape, dt):
                return stack.enter_context(nc.sbuf_tensor(name, shape, dt))

            def ps(name, shape, dt):
                return stack.enter_context(nc.psum_tensor(name, shape, dt))
            return sb, ps

        sems = {}

        def sem(name):
            if name not in sems:
                sems[name] = whole.enter_context(nc.semaphore(name))
            return sems[name]

        g = Shared()
        g.a, g.out, g.sem = a, out, sem
        sb, _ = maker(whole)
        g.x_res = sb("x_res", [P, NT, D], F32)
        g.xT = [sb(f"xT_{p}", [P, C, B * T], FR) for p in "hl"]
        g.ident = sb("ident", [P, P], F32)
        g.power = sb("power", [P, TT], F32)
        g.cols = sb("cols", [P, sum(COLS.values())], F32)
        g.rows = sb("rows", [P, len(ROWS), D], F32)
        g.w_stage = sb("w_stage", [P, 2, 2 * H], F32)
        g.consts = sem("constants_loaded")
        g.w_staged = sem("w_stage_loaded")
        g.w_split = sem("w_split")
        g.col = lambda name, j=0: g.cols[:, col_at(name, j):col_at(name, j) + 1]
        g.row = lambda name: g.rows[:, ROWS.index(name), :]
        g.xT_of = lambda i: (lambda q, c: g.xT[q][:, c, ds(i * T, T)])

        g.W1, g.W2 = [], []

        def group_buffers(stack, k):
            gsb, _ = maker(stack)
            g.W1.append([gsb(f"W1_{k}{p}", [P, C, H], FR) for p in "hl"])
            g.W2.append([gsb(f"W2_{k}{p}", [P, HT, D], FR) for p in "hl"])

        with ExitStack() as st:
            group_buffers(st, 0)
            g.attn = maker(st)[0]("attn", [P, NT, D], F32)
            with ExitStack() as st1:
                aft_phase(nc, g, *maker(st1))
            with ExitStack() as st1:
                group_buffers(st1, 1)
                g.cwT = maker(st1)[0]("cwT", [P, B * T], FR)
                with ExitStack() as st2:
                    ffn0_phase(nc, g, *maker(st2))
                with ExitStack() as st2:
                    router_phase(nc, g, *maker(st2))
                with ExitStack() as st2:
                    moe_phase(nc, g, *maker(st2))
        with ExitStack() as st1:
            norm_phase(nc, g, *maker(st1), "n1")
        with ExitStack() as st1:
            attention_phase(nc, g, *maker(st1))
        with ExitStack() as st1:
            sb1, ps1 = maker(st1)
            g.S1 = sb1("S1", [P, C, H], FR)
            g.S2 = sb1("S2", [P, HT, D], FR)
            g.alpha1 = sb1("alpha1", [P, HT], F32)
            g.alpha2 = sb1("alpha2", [P, D], F32)
            with ExitStack() as st2:
                binary_phase(nc, g, *maker(st2))
            ffn1_phase(nc, g, sb1, ps1)


def group_dma(sp, g, k):
    if k:
        sp.wait_ge(g.w_split, 4 * k)
    name1, name2, at = (("w1_0", "w2_0", 0) if k == 0 else ("ew1", "ew2", (k - 1) * H) if k <= GR
                        else ("sw1", "sw2", 0) if k == GR + 1 else ("w1_1", "w2_1", 0))
    sp.dma_start(g.w_stage[:, 0, :].rearrange("p (c n) -> p c n", c=C),
                 g.a[name1][:, at:at + H].rearrange("(c p) n -> p c n", p=P)).then_inc(g.w_staged, 16)
    sp.dma_start(g.w_stage[:, 1, :].rearrange("p (t n) -> p t n", t=HT),
                 g.a[name2][at:at + H, :].rearrange("(t p) n -> p t n", p=P)).then_inc(g.w_staged, 16)


def group_split(pool, g, k):
    pool.wait_ge(g.w_staged, 32 * (k + 1))
    for j, w in enumerate((g.W1, g.W2)):
        hi, lo = (w[k % 2][q][:, :, :].rearrange("p a b -> p (a b)") for q in range(2))
        pool.tensor_copy(hi, g.w_stage[:, j, :]).then_inc(g.w_split, 1)
        pool.wait_ge(g.w_split, 4 * k + 2 * j + 1)
        pool.tensor_tensor(lo, g.w_stage[:, j, :], f(hi), ALU.subtract).then_inc(g.w_split, 1)


def group_weights(g, k):
    return (lambda q, c, t: g.W1[k % 2][q][:, c, t * P:(t + 1) * P]), (lambda q, t: g.W2[k % 2][q][:, t, :])


def aft_phase(nc, g, sb, ps):
    a, sem = g.a, g.sem
    pair = sb("aft_pair", [P, 2, C, T], F32)
    wst = pair[:, :, :, :].rearrange("p a c t -> p (a c t)").rearrange("p (w c n) -> p w c n", w=4, c=C)
    ek, ekv = pair[:, 0], pair[:, 1]
    W = [sb(f"aft_w{p}", [P, 4, C, D], FR) for p in "hl"]
    pos = sb("aft_pos", [P, TT, T], F32)
    npm = sb("aft_npm", [P, TT], F32)
    ewT = [sb(f"aft_ewT{p}", [P, TT, T], FR) for p in "hl"]
    emb = sb("aft_emb", [P, TT, D], F32)
    embT = [sb(f"aft_embT{p}", [P, C, T], FR) for p in "hl"]
    km = sb("aft_km", [P, 3, C], F32)
    nbq = sb("aft_nbq", [P, C], F32)
    sg = sb("aft_sg", [P, C, T], F32)
    ekT = [sb(f"aft_ekT{p}", [P, TT, D], FR) for p in "hl"]
    ekvT = [sb(f"aft_ekvT{p}", [P, TT, D], FR) for p in "hl"]
    y, yT = ekv, embT
    TP = [ps(f"aft_tp{i}", [P, T], F32) for i in range(2)]
    KB = [ps(f"aft_k{i}", [P, T], F32) for i in range(2)]
    VB = [ps(f"aft_v{i}", [P, T], F32) for i in range(2)]
    QB = [ps(f"aft_q{i}", [P, T], F32) for i in range(2)]
    nm, tn = Norm(sb, sem, "aft"), Turn(sem, "aft", TP)
    s_x, s_w, s_pos, s_ctx = (sem("aft_" + n) for n in ("x_loaded", "w_loaded", "pos_loaded", "ctx_loaded"))
    s_wh, s_wl = sem("aft_w_hi"), sem("aft_w_lo")
    s_band, s_npm, s_ew = sem("aft_band"), sem("aft_npm_done"), sem("aft_ew_done")
    s_ewt, s_ewh, s_ewl = sem("aft_ew_turned"), sem("aft_ew_hi"), sem("aft_ew_lo")
    s_c, s_pass = sem("aft_dve_chain"), sem("dve_passed")
    s_pool = sem("aft_pool")
    names = ("k", "q", "v", "nb", "ek", "e", "ekv", "ekT", "ekTh", "ekTl", "ekvT", "ekvTh", "ekvTl", "den",
             "num", "y", "yh", "yl", "attn")
    s = {n: sem("aft_s_" + n) for n in names}
    PRE, PER = 1, 33

    with nc.Block() as block:
        @block.sync
        def _(sp):
            sp.dma_start(g.x_res[:, :, :], a["x"].rearrange("(t p) d -> p t d", p=P)).then_inc(s_x, 16)
            sp.dma_start(g.attn[:, :, :], a["ctx"].rearrange("(t p) d -> p t d", p=P)).then_inc(s_ctx, 16)
            sp.dma_start(g.cols[:, :], a["cols"]).then_inc(g.consts, 16)
            sp.dma_start(g.ident[:, :], a["ident"]).then_inc(g.consts, 16)
            sp.dma_start(g.rows[:, :, :].rearrange("p r d -> p (r d)"),
                         a["rows"].rearrange("r d -> (r d)").partition_broadcast(P)).then_inc(g.consts, 16)
            group_dma(sp, g, 0)
            group_dma(sp, g, 1)

        @block.scalar
        def _(act):
            for j, n in enumerate(("wq0", "wk0", "wv0", "wo0")):
                act.dma_start(wst[:, j], a[n].rearrange("(c p) n -> p c n", p=P)).then_inc(s_w, 16)
            act.dma_start(pos[:, :, :], a["pos"].rearrange("(t p) n -> p t n", p=P)).then_inc(s_pos, 16)
            act.wait_ge(s_w, 64)
            act.activation(W[0][:, :, :, :], wst, ACT.Copy).then_inc(s_wh, 1)
            for tt in range(TT):
                act.wait_ge(s_npm, 1)
                act.activation(pos[:, tt, :], pos[:, tt, :], ACT.Exp, bias=npm[:, tt:tt + 1]).then_inc(s_ew, 1)
            for jc in range(TT):
                act.wait_ge(s_ewt, jc + 1)
                act.activation(ewT[0][:, jc, :], KB[jc % 2][:, :], ACT.Copy).then_inc(s_ewh, 1)
            with act.Fori(0, B) as i:
                turn_act(act, tn, 2 * i, lambda c: embT[0][:, c, :])
                for c in range(C):
                    act.wait_ge(s["nb"], i + 1)
                    act.activation(ek[:, c, :], KB[c][:, :], ACT.Exp, bias=km[:, 2, c:c + 1]).then_inc(s["ek"], 1)
                for c in range(C):
                    act.wait_ge(s["q"], 2 * i + c + 1)
                    act.activation(sg[:, c, :], QB[c][:, :], ACT.Exp, bias=nbq[:, c:c + 1], scale=-1.0)\
                       .then_inc(s["e"], 1)
                for src, dst, inn, done in ((KB, ekT, s["ekT"], s["ekTh"]), (VB, ekvT, s["ekvT"], s["ekvTh"])):
                    for j in range(2):
                        act.wait_ge(inn, 2 * i + j + 1)
                        act.activation(dst[0][:, 2 * j:2 * j + 2, :], src[j][:, :].rearrange("p (t d) -> p t d", d=D),
                                       ACT.Copy).then_inc(done, 1)
                for c in range(C):
                    act.wait_ge(s["y"], 2 * i + c + 1)
                    act.activation(yT[0][:, c, :], y[:, c, :], ACT.Copy).then_inc(s["yh"], 1)
                turn_act(act, tn, 2 * i + 1, lambda c: g.xT_of(i)(0, c))

        @block.gpsimd
        def _(pool):
            pool.memset(g.power[:, :], -0.5).then_inc(s_pool, 1)
            pool.wait_ge(s_pos, 16)
            pool.affine_select(out=pos[:, :, :], in_=pos[:, :, :], compare_op=ALU.is_ge, fill=0.0, base=BAND - 1,
                               pattern=[[-P, TT], [1, T]], channel_multiplier=-1).then_inc(s_band, 1)
            pool.wait_ge(s_band, 1)
            pool.affine_select(out=pos[:, :, :], in_=pos[:, :, :], compare_op=ALU.is_ge, fill=0.0, base=BAND - 1,
                               pattern=[[P, TT], [-1, T]], channel_multiplier=1).then_inc(s_band, 1)
            pool.wait_ge(s_pool, 1)
            with pool.Fori(0, B) as i:
                norm_pool(pool, nm, 2 * i, g.power)
                norm_pool(pool, nm, 2 * i + 1, g.power)
            group_split(pool, g, 0)

        @block.vector
        def _(dve):
            dve.sem_inc(tn.lo, C)
            dve.wait_ge(s_wh, 1)
            dve.tensor_tensor(W[1][:, :, :, :], wst, f(W[0][:, :, :, :]), ALU.subtract).then_inc(s_wl, 1)
            dve.wait_ge(g.consts, 48)
            dve.wait_ge(s_x, 16)
            dve.wait_ge(s_ctx, 16)
            dve.tensor_scalar(nbq[:, :], g.cols[:, col_at("bq0"):col_at("bq0") + C], -1.0, None, ALU.mult)\
               .then_inc(s_c, 1)
            dve.wait_ge(s_band, 2)
            dve.tensor_reduce(npm[:, :], pos[:, :, :], AX.X, ALU.max, negate=True).then_inc(s_npm, 1)
            for jc in range(TT):
                dve.wait_ge(s_ewh, jc + 1)
                dve.tensor_tensor(ewT[1][:, jc, :], KB[jc % 2][:, :], f(ewT[0][:, jc, :]), ALU.subtract)\
                   .then_inc(s_ewl, 1)
            with dve.Fori(0, B) as i:
                ch = Chain(dve, s_c, i * PER + PRE, PER, s_pass)
                norm_stats(dve, nm, ch, tile_of(g.x_res, i))
                norm_apply(dve, nm, 2 * i, ch, tile_of(g.x_res, i), own(emb))
                ch.wait()
                dve.tensor_tensor(emb[:, :, :], emb[:, :, :], g.attn[:, ds(i * TT, TT), :], ALU.add)\
                   .then_inc(tn.ready, 1)
                turn_dve(dve, tn, 2 * i, lambda c: embT[0][:, c, :], lambda c: embT[1][:, c, :])
                for c in range(C):
                    dve.wait_ge(s["k"], 2 * i + c + 1)
                    ch.inc(dve.tensor_reduce(km[:, 0, c:c + 1], KB[c][:, :], AX.X, ALU.max))
                ch.wait()
                bk = g.cols[:, col_at("bk0"):col_at("bk0") + C]
                ch.link(dve.tensor_tensor(km[:, 1, :], km[:, 0, :], bk, ALU.add))
                dve.tensor_tensor(km[:, 2, :], bk, km[:, 1, :], ALU.subtract).then_inc(s["nb"], 1)
                for c in range(C):
                    dve.wait_ge(s["v"], 2 * i + c + 1)
                    dve.wait_ge(s["ek"], 2 * i + c + 1)
                    dve.scalar_tensor_tensor(out=ekv[:, c, :], in0=VB[c][:, :], scalar=g.col("bv0", c),
                                             in1=ek[:, c, :], op0=ALU.add, op1=ALU.mult).then_inc(s["ekv"], 1)
                for tt in range(TT):
                    ch.inc(dve.tensor_tensor(emb[:, tt, :], emb[:, tt, :], g.row("bo0"), ALU.add))
                for src, dst, hi, lo in ((KB, ekT, s["ekTh"], s["ekTl"]), (VB, ekvT, s["ekvTh"], s["ekvTl"])):
                    for j in range(2):
                        dve.wait_ge(hi, 2 * i + j + 1)
                        dve.tensor_tensor(dst[1][:, 2 * j:2 * j + 2, :], src[j][:, :].rearrange("p (t d) -> p t d", d=D),
                                          f(dst[0][:, 2 * j:2 * j + 2, :]), ALU.subtract).then_inc(lo, 1)
                dve.wait_ge(s["e"], 2 * i + 2)
                for c in range(C):
                    dve.wait_ge(s["den"], 2 * i + c + 1)
                    ch.inc(dve.scalar_tensor_tensor(out=sg[:, c, :], in0=sg[:, c, :], scalar=1.0, in1=TP[c][:, :],
                                                    op0=ALU.add, op1=ALU.mult))
                ch.wait()
                ch.link(dve.reciprocal(sg[:, :, :], sg[:, :, :]))
                for c in range(C):
                    dve.wait_ge(s["num"], 2 * i + c + 1)
                    dve.tensor_tensor(y[:, c, :], KB[c][:, :], sg[:, c, :], ALU.mult).then_inc(s["y"], 1)
                for c in range(C):
                    dve.wait_ge(s["yh"], 2 * i + c + 1)
                    dve.tensor_tensor(yT[1][:, c, :], y[:, c, :], f(yT[0][:, c, :]), ALU.subtract).then_inc(s["yl"], 1)
                dve.wait_ge(s["attn"], i + 1)
                for j in range(2):
                    ch.inc(dve.tensor_tensor(emb[:, 2 * j:2 * j + 2, :], QB[j][:, :].rearrange("p (t d) -> p t d", d=D),
                                             emb[:, 2 * j:2 * j + 2, :], ALU.add))
                ch.hold()
                norm_stats(dve, nm, ch, own(emb))
                norm_scaled(dve, nm, 2 * i + 1, ch, own(emb), own(emb), g.row("gamma"), lambda tt: g.row("beta"), own(emb))
                ch.hold()
                ch.inc(dve.tensor_copy(g.attn[:, ds(i * TT, TT), :], emb[:, :, :]))
                ch.wait()
                dve.sem_inc(tn.ready, 1)
                turn_dve(dve, tn, 2 * i + 1, lambda c: g.xT_of(i)(0, c), lambda c: g.xT_of(i)(1, c))
                ch.end()

        @block.tensor
        def _(pe):
            pe.wait_ge(g.consts, 48)
            pe.wait_ge(s_ew, TT)
            for jc in range(TT):
                if jc >= 2:
                    pe.wait_ge(s_ewl, jc - 1)
                for tt in range(TT):
                    last = pe.transpose(KB[jc % 2][:, tt * P:(tt + 1) * P], pos[:, tt, jc * P:(jc + 1) * P],
                                        g.ident[:, :])
                last.then_inc(s_ewt, 1)
            pe.wait_ge(s_wl, 1)
            pe.wait_ge(s_ewl, TT)
            with pe.Fori(0, B) as i:
                turn_pe(pe, tn, 2 * i, own(emb), g.ident[:, :])
                pe.wait_ge(tn.lo, 2 * i * C + 2 * C)
                for w, banks, done in ((1, KB, s["k"]), (0, QB, s["q"]), (2, VB, s["v"])):
                    for m in range(C):
                        products(pe, banks[m][:, :], lambda q, c: W[q][:, w, c, m * P:(m + 1) * P],
                                 lambda q, c: embT[q][:, c, :]).then_inc(done, 1)
                for src, banks, inn, done in ((ek, KB, s["ek"], s["ekT"]), (ekv, VB, s["ekv"], s["ekvT"])):
                    pe.wait_ge(inn, 2 * i + 2)
                    for jc in range(TT):
                        for c in range(C):
                            at = (jc % 2) * D + c * P
                            last = pe.transpose(banks[jc // 2][:, at:at + P], src[:, c, jc * P:(jc + 1) * P],
                                                g.ident[:, :])
                        if jc % 2:
                            last.then_inc(done, 1)
                for src, banks, inn, done in ((ekT, TP, s["ekTl"], s["den"]), (ekvT, KB, s["ekvTl"], s["num"])):
                    pe.wait_ge(inn, 2 * i + 2)
                    for c in range(C):
                        products(pe, banks[c][:, :], lambda q, jc: src[q][:, jc, c * P:(c + 1) * P],
                                 lambda q, jc: ewT[q][:, jc, :], chunks=TT).then_inc(done, 1)
                pe.wait_ge(s["yl"], 2 * i + 2)
                for tt in range(TT):
                    last = products(pe, QB[tt // 2][:, (tt % 2) * D:(tt % 2 + 1) * D],
                                    lambda q, c: yT[q][:, c, tt * P:(tt + 1) * P], lambda q, c: W[q][:, 3, c, :],
                                    start=tt % 2 == 0, skip=True)
                last.then_inc(s["attn"], 1)
                turn_pe(pe, tn, 2 * i + 1, own(emb), g.ident[:, :])


def tiles(row, n=2):
    return row.unsqueeze(1).to_broadcast([P, n, D])


def ffn0_phase(nc, g, sb, ps):
    m = Mlp(sb, ps, g.sem, "ffn0", 1)
    s_b2, s_beta = g.sem("ffn0_b2_added"), g.sem("ffn0_beta_added")
    with nc.Block() as block:
        @block.sync
        def _(sp):
            group_dma(sp, g, 2)

        @block.gpsimd
        def _(pool):
            pool.tensor_tensor(g.attn[:, :, :], g.attn[:, :, :], tiles(g.row("b2_0"), NT), ALU.add).then_inc(s_b2, 1)
            pool.tensor_tensor(g.x_res[:, :, :], g.x_res[:, :, :], tiles(g.row("beta"), NT), ALU.add).then_inc(s_beta, 1)
            group_split(pool, g, 1)
            pool.wait_ge(s_beta, 1)

        @block.tensor
        def _(pe):
            pe.wait_ge(g.w_split, 4)
            mlp_pe(pe, m, lambda q: group_weights(g, 0), g.xT_of)

        @block.scalar
        def _(act):
            mlp_act(act, m, ACT.Relu, lambda tile: g.col("b1_0", tile.t))

        @block.vector
        def _(dve):
            def add_y(q, i, j, y):
                dst = g.attn[:, ds(i * TT + 2 * j, 2), :]
                return dve.tensor_tensor(dst, y, dst, ALU.add)
            dve.wait_ge(s_b2, 1)
            mlp_dve(dve, m, add_y)


def router_phase(nc, g, sb, ps):
    a, sem = g.a, g.sem
    xn = sb("rt_xn", [P, TT, D], F32)
    rws = sb("rt_rws", [P, C, P], F32)
    RW = [sb(f"rt_rw{p}", [P, C, P], FR) for p in "hl"]
    b2s = sb("rt_b2s", [P, D], F32)
    B2 = [sb(f"rt_b2{p}", [P, D], FR) for p in "hl"]
    lgT = sb("rt_lgT", [P, T], F32)
    lg = sb("rt_lg", [P, TT, E], F32)
    left = sb("rt_left", [P, TT, E], F32)
    top = sb("rt_top", [P, TT, K_TOP], F32)
    ntop = sb("rt_ntop", [P, TT], F32)
    ex = sb("rt_ex", [P, TT, E], F32)
    tot = sb("rt_tot", [P, TT], F32)
    cwx = sb("rt_cwx", [P, TT, GR, 2, EG], FR)
    cwTs = sb("rt_cwTs", [P, T], FR)
    TP = [ps(f"rt_tp{i}", [P, T], F32) for i in range(2)]
    LG, LT, CT = (ps("rt_" + n, [P, T], F32) for n in ("lgp", "ltp", "ctp"))
    YB = [ps(f"rt_yb{i}", [P, 2 * D], F32) for i in range(2)]
    nm, tn = Norm(sb, sem, "rt"), Turn(sem, "rt", TP)
    s_w, s_wh, s_wl, s_c = (sem("rt_" + n) for n in ("w_loaded", "w_hi", "w_lo", "dve_chain"))
    s_pass = sem("dve_passed")
    s = {n: sem("rt_s_" + n) for n in ("lg", "lgT", "lt", "ntop", "ex", "cwx", "ct", "cwTs", "yb")}
    sb2 = sb("rt_sb2", [P, D], F32)
    s_sum, s_sb2 = sem("rt_sb2_summed"), sem("rt_sb2_added")
    PRE, PER, LAST = 20, 40, 20

    with nc.Block() as block:
        @block.sync
        def _(sp):
            sp.dma_start(rws[:, :, :], a["rw"].rearrange("(c p) n -> p c n", p=P)).then_inc(s_w, 16)
            sp.dma_start(b2s[:, :], a["eb2"]).then_inc(s_w, 16)

        @block.gpsimd
        def _(pool):
            pool.tensor_tensor(sb2[:, :], g.row("sb2a"), g.row("sb2b"), ALU.add).then_inc(s_sum, 1)

            def roots(i):
                norm_pool(pool, nm, 2 * i, g.power)
                norm_pool(pool, nm, 2 * i + 1, g.power)

            def add_sb2(i):
                pool.wait_ge(tn.ready, i + 1)
                pool.sem_inc(nm.passed, 1)
                x_b = g.x_res[:, ds(i * TT, TT), :]
                pool.tensor_tensor(x_b, x_b, tiles(sb2[:, :], TT), ALU.add).then_inc(s_sb2, 1)

            roots(0)
            pool.wait_ge(s_sum, 1)
            with pool.Fori(0, B - 1) as i:
                add_sb2(i)
                roots(i + 1)
            add_sb2(B - 1)

        @block.scalar
        def _(act):
            act.sem_inc(s["cwTs"], 1)
            act.wait_ge(s_w, 32)
            act.activation(RW[0][:, :, :], rws[:, :, :], ACT.Copy).then_inc(s_wh, 1)
            act.activation(B2[0][:, :], b2s[:, :], ACT.Copy).then_inc(s_wh, 1)
            with act.Fori(0, B) as i:
                turn_act(act, tn, i, lambda c: g.xT_of(i)(0, c))
                act.wait_ge(s["lg"], i + 1)
                act.activation(lgT[:, :], LG[:, :], ACT.Identity, bias=g.col("rb")).then_inc(s["lgT"], 1)
                act.wait_ge(s["ntop"], i + 1)
                for tt in range(TT):
                    act.activation(ex[:, tt, :], lg[:, tt, :], ACT.Exp, bias=ntop[:, tt:tt + 1]).then_inc(s["ex"], 1)
                act.wait_ge(s["ct"], i + 1)
                act.activation(cwTs[:, :], CT[:, :], ACT.Copy).then_inc(s["cwTs"], 1)
                act.activation(g.cwT[:, ds(i * T, T)], CT[:, :], ACT.Copy).then_inc(s["cwTs"], 1)

        @block.vector
        def _(dve):
            dve.sem_inc(tn.lo, C)
            dve.wait_ge(s_wh, 2)
            dve.tensor_tensor(RW[1][:, :, :], rws[:, :, :], f(RW[0][:, :, :]), ALU.subtract).then_inc(s_wl, 1)
            dve.tensor_tensor(B2[1][:, :], b2s[:, :], f(B2[0][:, :]), ALU.subtract).then_inc(s_wl, 1)

            def x_new(i, ch):
                norm_scaled(dve, nm, 2 * i, ch, tile_of(g.attn, i), own(xn), g.row("gamma"), tile_of(g.x_res, i),
                            tile_of(g.x_res, i))

            def x_stats(i, ch):
                ch.hold()
                norm_stats(dve, nm, ch, tile_of(g.x_res, i))

            def x_norm(i, ch):
                norm_apply(dve, nm, 2 * i + 1, ch, tile_of(g.x_res, i), own(xn))
                ch.wait()
                dve.sem_inc(tn.ready, 1)

            ch = Chain(dve, s_c, 0, PRE, s_pass)
            norm_stats(dve, nm, ch, tile_of(g.attn, 0))
            x_new(0, ch)
            x_stats(0, ch)
            x_norm(0, ch)
            ch.end()

            def batch(i, ch, following):
                turn_dve(dve, tn, i, lambda c: g.xT_of(i)(0, c), lambda c: g.xT_of(i)(1, c))
                if following:
                    norm_stats(dve, nm, ch, tile_of(g.attn, i + 1))
                    x_new(i + 1, ch)
                dve.wait_ge(s["lt"], i + 1)
                ch.inc(dve.tensor_copy(lg[:, :, :], LT[:, :].rearrange("p (t e) -> p t e", t=TT)[:, :, 0:E]))
                ch.hold()
                for tt in range(TT):
                    ch.inc(dve.max(top[:, tt, :], lg[:, tt, :]))
                ch.wait()
                dve.tensor_scalar(ntop[:, :], top[:, :, 0], -1.0, None, ALU.mult).then_inc(s["ntop"], 1)
                for tt in range(TT):
                    ch.inc(dve.match_replace(left[:, tt, :], top[:, tt, :], lg[:, tt, :], -3e38))
                ch.wait()
                ch.link(dve.tensor_tensor(left[:, :, :], lg[:, :, :], left[:, :, :], ALU.not_equal))
                dve.wait_ge(s["ex"], TT * i + TT)
                ch.link(dve.tensor_tensor(ex[:, :, :], ex[:, :, :], left[:, :, :], ALU.mult))
                ch.link(dve.tensor_reduce(tot[:, :], ex[:, :, :], AX.X, ALU.add))
                ch.link(dve.reciprocal(tot[:, :], tot[:, :]))
                for tt in range(TT):
                    ch.inc(dve.tensor_scalar(ex[:, tt, :], ex[:, tt, :], tot[:, tt:tt + 1], None, ALU.mult))
                ch.wait()
                cw = ex[:, :, :].rearrange("p t (g e) -> p t g e", g=GR)
                ch.link(dve.tensor_copy(cwx[:, :, :, 0, :], cw))
                dve.tensor_tensor(cwx[:, :, :, 1, :], cw, f(cwx[:, :, :, 0, :]), ALU.subtract).then_inc(s["cwx"], 1)
                if following:
                    x_stats(i + 1, ch)
                    x_norm(i + 1, ch)
                dve.wait_ge(s_sb2, i + 1)
                dve.wait_ge(s["yb"], i + 1)
                for j in range(2):
                    dst = g.x_res[:, ds(i * TT + 2 * j, 2), :]
                    ch.inc(dve.tensor_tensor(dst, YB[j][:, :].rearrange("p (t d) -> p t d", d=D), dst, ALU.add))
                ch.wait()
                ch.end()

            with dve.Fori(0, B - 1) as i:
                batch(i, Chain(dve, s_c, PRE + i * PER, PER, s_pass), True)
            batch(B - 1, Chain(dve, s_c, PRE + (B - 1) * PER, LAST, s_pass), False)

        @block.tensor
        def _(pe):
            pe.wait_ge(s_wl, 2)
            with pe.Fori(0, B) as i:
                turn_pe(pe, tn, i, own(xn), g.ident[:, :])
                pe.wait_ge(tn.lo, C * i + 2 * C)
                products(pe, LG[:, :], lambda q, c: RW[q][:, c, :], g.xT_of(i)).then_inc(s["lg"], 1)
                pe.wait_ge(s["lgT"], i + 1)
                for tt in range(TT):
                    last = pe.transpose(LT[:, tt * P:(tt + 1) * P], lgT[:, tt * P:(tt + 1) * P], g.ident[:, :])
                last.then_inc(s["lt"], 1)
                pe.wait_ge(s["cwx"], i + 1)
                pe.wait_ge(s["cwTs"], 2 * i + 1)
                for tt in range(TT):
                    last = pe.transpose(CT[:, tt * P:(tt + 1) * P],
                                        f(cwx[:, tt, :, :, :].rearrange("p g q e -> p (g q e)")), g.ident[:, :])
                last.then_inc(s["ct"], 1)
                pe.wait_ge(s["cwTs"], 2 * i + 2)
                for tt in range(TT):
                    for q in range(2):
                        last = pe.matmul(YB[tt // 2][:, (tt % 2) * D:(tt % 2 + 1) * D], cwTs[:, tt * P:(tt + 1) * P],
                                         B2[q][:, :], start=tt % 2 == 0 and q == 0, stop=q == 1, skip_group_check=True)
                last.then_inc(s["yb"], 1)


def moe_phase(nc, g, sb, ps):
    a, sem = g.a, g.sem
    m = Mlp(sb, ps, sem, "moe", GR + 1, gated=GR)
    SEL = sb("moe_sel", [P, GR * HT, P], FR)
    s_sel, s_selr = sem("moe_sel_loaded"), sem("moe_sel_ready")
    stage = g.attn[:, :, :].rearrange("p t d -> p (t d)")

    with nc.Block() as block:
        @block.sync
        def _(sp):
            sp.dma_start(stage, a["sel_gate"]).then_inc(s_sel, 16)
            for k in range(3, GR + 2):
                group_dma(sp, g, k)

        @block.gpsimd
        def _(pool):
            for k in range(2, GR + 2):
                if k > 2:
                    pool.wait_ge(m.h_used, RING + (k - 2) * B * HT)
                group_split(pool, g, k)

        @block.tensor
        def _(pe):
            pe.wait_ge(s_selr, 1)
            mlp_pe(pe, m, lambda q: group_weights(g, q + 1), g.xT_of,
                   gate=lambda tile: (SEL[:, tile.q * HT + tile.t, :], g.cwT[:, ds(tile.i * T, T)]),
                   new_group=lambda q: pe.wait_ge(g.w_split, 4 * (q + 2)))

        @block.scalar
        def _(act):
            mlp_act(act, m, ACT.Silu,
                    lambda tile: g.col("eb1", tile.q * HT + tile.t) if tile.q < GR else g.col("sb1", tile.t))

        @block.vector
        def _(dve):
            dve.wait_ge(s_sel, 16)
            dve.tensor_copy(SEL[:, :, :].rearrange("p t m -> p (t m)"), stage).then_inc(s_selr, 1)

            def add_y(q, i, j, y):
                dst = g.x_res[:, ds(i * TT + 2 * j, 2), :]
                return dve.tensor_tensor(dst, y, dst, ALU.add)
            mlp_dve(dve, m, add_y)


def norm_loops(block, g, nm, tn, xn, s_c, s_pass, before=None):
    before = before or {}

    def pre(name, eng):
        if name in before:
            before[name](eng)

    @block.gpsimd
    def _(pool):
        with pool.Fori(0, B) as i:
            norm_pool(pool, nm, i, g.power)

    @block.scalar
    def _(act):
        pre("act", act)
        with act.Fori(0, B) as i:
            turn_act(act, tn, i, lambda c: g.xT_of(i)(0, c))

    @block.vector
    def _(dve):
        dve.sem_inc(tn.lo, C)
        pre("dve", dve)
        with dve.Fori(0, B) as i:
            ch = Chain(dve, s_c, i * 2 * TT, 2 * TT, s_pass)
            norm_stats(dve, nm, ch, tile_of(g.x_res, i))
            norm_apply(dve, nm, i, ch, tile_of(g.x_res, i), own(xn))
            ch.wait()
            dve.sem_inc(tn.ready, 1)
            turn_dve(dve, tn, i, lambda c: g.xT_of(i)(0, c), lambda c: g.xT_of(i)(1, c))
            ch.end()

    @block.tensor
    def _(pe):
        pre("pe", pe)
        with pe.Fori(0, B) as i:
            turn_pe(pe, tn, i, own(xn), g.ident[:, :])


def norm_phase(nc, g, sb, ps, name):
    xn = sb(name + "_xn", [P, TT, D], F32)
    TP = [ps(f"{name}_tp{i}", [P, T], F32) for i in range(2)]
    nm, tn, s_c = Norm(sb, g.sem, name), Turn(g.sem, name, TP), g.sem(name + "_dve_chain")
    s_pass = g.sem("dve_passed")
    with nc.Block() as block:
        norm_loops(block, g, nm, tn, xn, s_c, s_pass)


def attention_phase(nc, g, sb, ps):
    a, sem = g.a, g.sem
    WP = [sb(f"at_w{p}", [P, 3, C, D], FR) for p in "hl"]
    WO = [sb(f"at_wo{p}", [P, HPB, D], FR) for p in "hl"]
    SELK = sb("at_selk", [P, HPB, 2, P], FR)
    SELQ = sb("at_selq", [P, 2 * HPB, 2, P], FR)
    cT = [sb(f"at_cT{p}", [P, C, T], FR) for p in "hl"]
    kT = [sb(f"at_kT{p}", [P, C, T], FR) for p in "hl"]
    qT = kT
    KST = sb("at_kst", [P, HEADS // 2, T], FR)
    QST = sb("at_qst", [P, 2, T], FR)
    VAUG = sb("at_vaug", [P, TT, HEADS, P], FR)
    PTS = [sb(f"at_pt{p}", [P, 2, T], FR) for p in "hl"]
    PR = sb("at_p", [P, 2, TT, T], F32)
    mst = sb("at_mst", [P, 2, T], I32)
    mk = sb("at_mk", [P, TT, T], BF16)
    nid = sb("at_nid", [P, P], BF16)
    nmx = sb("at_nmx", [P, 2, TT], F32)
    den = sb("at_den", [P, TT, HEADS], F32)
    stage = g.w_stage[:, :, :].rearrange("p a n -> p (a n)")
    cst = stage[:, 0:C * T].rearrange("p (c t) -> p c t", c=C)
    OS = stage[:, 1024:3072].rearrange("p (g t) -> p g t", g=HPB)
    vS = stage[:, 3072:4096].rearrange("p (t d) -> p t d", t=TT)
    wst = stage[:, 0:3 * C * D].rearrange("p (w c n) -> p w c n", w=3, c=C)
    wost = stage[:, 1536:2560].rearrange("p (g n) -> p g n", g=HPB)
    selst = PR[:, 0:2, :, :].rearrange("p a b t -> p (a b t)")[:, 0:24 * P]
    NK = 2 * HPB * P
    RDR = PR[:, 0, :, :]
    ON = (KST[:, 0:HPB, :], KST[:, HPB:2 * HPB, :])
    PT = [ps(f"at_tp{i}", [P, T], F32) for i in range(2)]
    OB = ps("at_o", [P, T], F32)
    QB = ps("at_qb", [P, T], F32)
    SB = [ps(f"at_s{i}", [P, T], F32) for i in range(TT)]
    MB, NB = SB, len(SB)
    s_w, s_ws, s_wh, s_wl = (sem("at_" + n) for n in ("w_loaded", "sel_split", "w_hi", "w_lo"))
    s_pass = sem("dve_passed")
    s_c, s_z, s_nid = sem("at_dve_chain"), sem("at_zeroed"), sem("at_nid_ready")
    names = ("ctx", "cTh", "cTl", "mld", "mk", "mb", "mbf", "kqh", "v", "vh", "kst", "qs", "qst", "s", "nmx", "p",
             "pt", "pth", "ptl", "pv", "os", "rdr", "on", "onh", "onl")
    s = {n: sem("at_s_" + n) for n in names}
    SLOTS = 20
    NP = HEADS * TT
    PER = 11
    ACT_SLOTS = (5, 7, 9, 11)
    DS = SLOTS - len(ACT_SLOTS)

    def emptied(eng, i, n):
        if n in ACT_SLOTS:
            eng.wait_ge(s["kst"], len(ACT_SLOTS) * i + ACT_SLOTS.index(n) + 1)
        else:
            eng.wait_ge(s["mbf"], DS * i + NB + sum(k not in ACT_SLOTS for k in range(n + 1)) + min(n + 1, 0))

    with nc.Block() as block:
        @block.sync
        def _(sp):
            for j, n in enumerate(("wq1", "wk1", "wv1")):
                sp.dma_start(wst[:, j], a[n].rearrange("(c p) n -> p c n", p=P)).then_inc(s_w, 16)
            sp.dma_start(wost, a["wo1"].rearrange("(g p) n -> p g n", p=P)).then_inc(s_w, 16)
            sp.dma_start(selst, a["sel_qk"]).then_inc(s_w, 16)
            sp.wait_ge(s_wl, 2)
            with sp.Fori(0, B) as i:
                sp.wait_ge(s["cTl"], i + 1)
                sp.dma_start(cst, a["ctxT"][:, ds(i * T, T)].rearrange("(c p) t -> p c t", p=P)).then_inc(s["ctx"], 16)
                for j in range(2):
                    sp.wait_ge(s["mk"], 2 * i + j + 1)
                    sp.dma_start(mst[:, :, :], a["mask"][ds(i * T + j * 2 * P, 2 * P), :]
                                 .rearrange("(t p) k -> p t k", p=P)).then_inc(s["mld"], 16)
            sp.wait_ge(s["ctx"], 16 * B)
            sp.sem_inc(s["ctx"], 16)

        @block.gpsimd
        def _(pool):
            pool.memset(f(VAUG[:, :, :, :]), 0.0).then_inc(s_z, 1)
            pool.sem_inc(s["v"], 1)
            pool.wait_ge(g.consts, 48)
            pool.tensor_scalar(nid[:, :], g.ident[:, :], NEG, 1.0, ALU.mult, ALU.mult).then_inc(s_nid, 1)
            vh = vS.rearrange("p t (h d) -> p t h d", d=HD)
            pool.wait_ge(s_z, 1)
            with pool.Fori(0, B) as i:
                emptied(pool, i, 3)
                pool.sem_inc(sem("pool_passed"), 1)
                for j in range(HPB):
                    pool.tensor_copy(VAUG[:, :, j::HPB, 2 * HD * j:2 * HD * j + HD], vh[:, :, j::HPB, :])\
                        .then_inc(s["vh"], 1)
                pool.wait_ge(s["vh"], HPB * i + HPB)
                for j in range(HPB):
                    pool.tensor_tensor(VAUG[:, :, j::HPB, 2 * HD * j + HD:2 * HD * (j + 1)], vh[:, :, j::HPB, :],
                                       f(VAUG[:, :, j::HPB, 2 * HD * j:2 * HD * j + HD]), ALU.subtract)\
                        .then_inc(s["v"], 1)


        @block.scalar
        def _(act):
            act.wait_ge(s_w, 80)
            act.activation(WP[0][:, :, :, :], wst, ACT.Copy).then_inc(s_wh, 1)
            act.activation(WO[0][:, :, :], wost, ACT.Copy).then_inc(s_wh, 1)
            act.activation(SELK[:, :, :, :].rearrange("p a b m -> p (a b m)"), selst[:, 0:NK], ACT.Copy).then_inc(s_ws, 1)
            act.activation(SELQ[:, :, :, :].rearrange("p a b m -> p (a b m)"), selst[:, NK:], ACT.Copy).then_inc(s_ws, 1)
            act.sem_inc(s["p"], TT)
            act.sem_inc(s["qst"], 2)
            act.wait_ge(s_ws, 2)
            act.wait_ge(s["ctx"], 16)
            act.activation(cT[0][:, :, :], cst, ACT.Copy).then_inc(s["cTh"], 1)
            with act.Fori(0, B) as i:
                def project(n, dst, b, slot):
                    for c in range(C):
                        act.wait_ge(s["mb"], SLOTS * i + slot + c + 1)
                        act.activation(dst[0][:, c, :], MB[c][:, :], ACT.Identity, bias=g.col(b, c)).then_inc(s["kqh"], 1)

                project(0, kT, "bk1", 0)
                for p in range(1, HEADS // 2, 2):
                    act.wait_ge(s["mb"], SLOTS * i + 4 + p + 1)
                    act.activation(KST[:, p, :], MB[(4 + p) % NB][:, :], ACT.Copy).then_inc(s["kst"], 1)
                project(1, qT, "bq1", 12)

                def stack(h):
                    act.wait_ge(s["qs"], HEADS * i + h + 1)
                    act.activation(QST[:, h % 2, :], QB[:, :], ACT.Copy).then_inc(s["qst"], 1)

                stack(0)
                for m in range(NP + TT):
                    h, j = divmod(m, TT)
                    if m < NP:
                        if j == 0:
                            act.wait_ge(s["pt"], NP * i + m + 1)
                        act.wait_ge(s["nmx"], NP * i + m + 1)
                        act.activation(PR[:, h % 2, j, :], SB[j][:, :], ACT.Exp, bias=nmx[:, h % 2, j:j + 1],
                                       accum_out=den[:, j, h:h + 1]).then_inc(s["p"], 1)
                    if m >= TT:
                        n = NP * i + m - TT
                        act.wait_ge(s["pt"], n + 6)
                        act.wait_ge(s["pv"], n + 1)
                        act.activation(PTS[0][:, j % 2, :], PT[j % 2][:, :], ACT.Copy).then_inc(s["pth"], 1)
                    if j == 0 and h + 1 < HEADS:
                        stack(h + 1)
                    if m == NP:
                        act.wait_ge(s["ctx"], 16 * i + 32)
                        act.activation(cT[0][:, :, :], cst, ACT.Copy).then_inc(s["cTh"], 1)
                for q in range(HPB):
                    act.wait_ge(s["on"], HPB * i + q + 1)
                    act.activation(ON[0][:, q, :], OS[:, q, :], ACT.Copy).then_inc(s["onh"], 1)

        @block.vector
        def _(dve):
            dve.wait_ge(s_wh, 2)
            dve.tensor_tensor(WP[1][:, :, :, :], wst, f(WP[0][:, :, :, :]), ALU.subtract).then_inc(s_wl, 1)
            dve.tensor_tensor(WO[1][:, :, :], wost, f(WO[0][:, :, :]), ALU.subtract).then_inc(s_wl, 1)
            dve.sem_inc(s["cTl"], 1)
            dve.sem_inc(s["mk"], 1)
            dve.sem_inc(s["mbf"], NB)
            dve.sem_inc(s["ptl"], 2)
            dve.sem_inc(s["os"], 1)
            dve.wait_ge(s["cTh"], 1)
            dve.tensor_tensor(cT[1][:, :, :], cst, f(cT[0][:, :, :]), ALU.subtract).then_inc(s["cTl"], 1)
            with dve.Fori(0, B) as i:
                ch = Chain(dve, s_c, i * PER, PER, s_pass)

                def mask(j):
                    dve.wait_ge(s["mld"], 32 * i + 16 * j + 16)
                    dve.tensor_scalar(mk[:, 2 * j:2 * j + 2, :], mst[:, :, :], 1.0, None, ALU.is_equal).then_inc(s["mk"], 1)

                mask(0)

                def low(n, dst, b):
                    for c in range(C):
                        dve.wait_ge(s["kqh"], 2 * C * i + 2 * n + c + 1)
                        dve.scalar_tensor_tensor(out=dst[1][:, c, :], in0=MB[c][:, :], scalar=g.col(b, c),
                                                 in1=f(dst[0][:, c, :]), op0=ALU.add, op1=ALU.subtract)\
                           .then_inc(s["mbf"], 1)

                low(0, kT, "bk1")
                dve.wait_ge(s["v"], HPB * i + 1)
                for j in range(2):
                    dve.wait_ge(s["mb"], SLOTS * i + 2 + j + 1)
                    dve.tensor_tensor(vS[:, 2 * j:2 * j + 2, :], MB[2 + j][:, :].rearrange("p (t d) -> p t d", d=D),
                                      tiles(g.row("bv1")), ALU.add).then_inc(s["mbf"], 1)
                for p in range(0, HEADS // 2, 2):
                    dve.wait_ge(s["mb"], SLOTS * i + 4 + p + 1)
                    dve.tensor_copy(KST[:, p, :], MB[(4 + p) % NB][:, :]).then_inc(s["mbf"], 1)
                mask(1)
                low(1, qT, "bq1")

                def take(q):
                    dve.wait_ge(s["pv"], NP * i + TT * HPB * (q + 1) + 2)
                    dve.tensor_copy(OS[:, q, :], OB[:, :]).then_inc(s["os"], 1)

                def scale(q):
                    dve.wait_ge(s["mb"], SLOTS * i + 14 + q + 1)
                    dve.wait_ge(s["os"], HPB * i + q + 2)
                    ch.link(dve.tensor_tensor(OS[:, q, :], OS[:, q, :], MB[(14 + q) % NB][:, :], ALU.mult))
                    dve.sem_inc(s["mbf"], 1)
                    dve.sem_inc(s["on"], 1)

                for m in range(NP + TT + 1):
                    h, j = divmod(m, TT)
                    if m < NP:
                        dve.wait_ge(s["s"], NP * i + m + 1)
                        dve.tensor_reduce(nmx[:, h % 2, j:j + 1], SB[j][:, :], AX.X, ALU.max, negate=True)\
                           .then_inc(s["nmx"], 1)
                    k = m - TT - 1
                    if k >= 0:
                        dve.wait_ge(s["pth"], NP * i + k + 1)
                        dve.tensor_tensor(PTS[1][:, k % 2, :], PT[k % 2][:, :], f(PTS[0][:, k % 2, :]), ALU.subtract)\
                           .then_inc(s["ptl"], 1)
                    if k > 0 and k % (TT * HPB) == 0:
                        take(k // (TT * HPB) - 1)
                    if m == NP:
                        dve.wait_ge(s["p"], NP * i + NP + TT)
                        ch.link(dve.reciprocal(den[:, :, :], den[:, :, :]))
                    if m == NP + 1:
                        dve.tensor_copy(RDR.rearrange("p t (h r) -> p (t h) r", r=2 * HD),
                                        den[:, :, :].rearrange("p t h -> p (t h)").unsqueeze(2).to_broadcast(
                                            [P, TT * HEADS, 2 * HD])).then_inc(s["rdr"], 1)
                    if m > NP + 1:
                        scale(m - NP - 2)
                for q in range(HPB):
                    if q == HPB - 1:
                        take(q)
                        scale(q)
                    dve.wait_ge(s["onh"], HPB * i + q + 1)
                    dve.tensor_tensor(ON[1][:, q, :], OS[:, q, :], f(ON[0][:, q, :]), ALU.subtract).then_inc(s["onl"], 1)
                for tt in range(TT):
                    dst = tile_of(g.x_res, i)(tt)
                    ch.inc(dve.tensor_tensor(dst, dst, g.row("bo1"), ALU.add))
                ch.wait()
                dve.wait_ge(s["cTh"], i + 2)
                dve.tensor_tensor(cT[1][:, :, :], cst, f(cT[0][:, :, :]), ALU.subtract).then_inc(s["cTl"], 1)
                for j in range(2):
                    dve.wait_ge(s["mb"], SLOTS * i + 18 + j + 1)
                    dst = g.x_res[:, ds(i * TT + 2 * j, 2), :]
                    ch.link(dve.tensor_tensor(dst, MB[(18 + j) % NB][:, :].rearrange("p (t d) -> p t d", d=D), dst, ALU.add))
                    dve.sem_inc(s["mbf"], 1)
                ch.end()

        @block.tensor
        def _(pe):
            pe.wait_ge(s_wl, 2)
            pe.wait_ge(s_ws, 2)
            pe.wait_ge(s_nid, 1)
            pe.sem_inc(s["pv"], 2)
            pe.sem_inc(s["pt"], 5)
            with pe.Fori(0, B) as i:
                slot = [0]

                def bank():
                    n = slot[0]
                    slot[0] += 1
                    emptied(pe, i, n - NB)
                    return MB[n % NB]

                pe.wait_ge(s["cTl"], i + 2)

                def project(w, src):
                    for m in range(C):
                        products(pe, bank()[:, :], lambda q, c: WP[q][:, w, c, m * P:(m + 1) * P], src)\
                            .then_inc(s["mb"], 1)

                project(1, lambda q, c: cT[q][:, c, :])
                for j in range(2):
                    bk = bank()
                    for kc in (2 * j, 2 * j + 1):
                        last = products(pe, bk[:, (kc % 2) * D:(kc % 2 + 1) * D],
                                        lambda q, c: cT[q][:, c, kc * P:(kc + 1) * P], lambda q, c: WP[q][:, 2, c, :],
                                        start=kc % 2 == 0, skip=True)
                    last.then_inc(s["mb"], 1)
                for p in range(HEADS // 2):
                    bk = bank()
                    for q in range(2):
                        last = pe.matmul(bk[:, :], SELK[:, p % HPB, q, :], kT[q][:, p // HPB, :], start=q == 0, stop=q == 1)
                    last.then_inc(s["mb"], 1)
                project(0, g.xT_of(i))

                def stack(h):
                    pe.wait_ge(s["qst"], HEADS * i + h + 2)
                    for q in range(2):
                        last = pe.matmul(QB[:, :], SELQ[:, h % (2 * HPB), q, :], qT[q][:, h // (2 * HPB), :],
                                         start=q == 0, stop=q == 1)
                    last.then_inc(s["qs"], 1)

                def weigh(h, kc):
                    n = NP * i + TT * h + kc
                    pe.wait_ge(s["ptl"], n + 3)
                    if h % HPB == 0 and kc == 0:
                        pe.wait_ge(s["os"], HPB * i + h // HPB + 1)
                    for q in range(2):
                        last = pe.matmul(OB[:, :], VAUG[:, kc, h, :], PTS[q][:, kc % 2, :],
                                         start=h % HPB == 0 and kc == 0 and q == 0,
                                         stop=h % HPB == HPB - 1 and kc == TT - 1 and q == 1)
                    last.then_inc(s["pv"], 1)

                emptied(pe, i, 13)
                stack(0)
                emptied(pe, i, 11)

                def score(m):
                    h, j = divmod(m, TT)
                    if j == 0:
                        pe.wait_ge(s["qst"], HEADS * i + h + 3)
                    pe.wait_ge(s["p"], NP * i + m + 1)
                    pe.matmul(SB[j][:, :], nid[:, :], mk[:, j, :], start=True, stop=False)
                    pe.matmul(SB[j][:, :], QST[:, h % 2, j * P:(j + 1) * P], KST[:, h // 2, :],
                              start=False, stop=True).then_inc(s["s"], 1)

                def spread(q):
                    bk = bank()
                    for t in range(TT):
                        last = pe.transpose(bk[:, t * P:(t + 1) * P], RDR[:, t, q * P:(q + 1) * P], g.ident[:, :])
                    last.then_inc(s["mb"], 1)

                score(0)
                score(1)
                stack(1)
                for m in range(NP + TT + 2):
                    h, j = divmod(m, TT)
                    if m + 2 < NP:
                        score(m + 2)
                    if m == TT + 2:
                        pe.wait_ge(s["v"], HPB * i + HPB + 1)
                    if m > TT + 1:
                        weigh(*divmod(m - TT - 2, TT))
                    if TT <= m < NP + TT:
                        if j == 0:
                            pe.wait_ge(s["p"], NP * i + m + TT)
                        pe.wait_ge(s["ptl"], NP * i + m - TT + 1)
                        for t in range(TT):
                            last = pe.transpose(PT[j % 2][:, t * P:(t + 1) * P],
                                                PR[:, (h - 1) % 2, t, j * P:(j + 1) * P], g.ident[:, :])
                        last.then_inc(s["pt"], 1)
                    if j == 2 and h + 2 < HEADS:
                        stack(h + 2)
                    if m == NP + 2:
                        pe.wait_ge(s["rdr"], i + 1)
                        spread(0)
                    if NP + 2 <= m < NP + 1 + HPB:
                        spread(m - NP - 1)
                pe.wait_ge(s["onl"], HPB * i + HPB)
                for j in range(2):
                    bk = bank()
                    for tt in (2 * j, 2 * j + 1):
                        last = products(pe, bk[:, (tt % 2) * D:(tt % 2 + 1) * D],
                                        lambda q, c: ON[q][:, c, tt * P:(tt + 1) * P], lambda q, c: WO[q][:, c, :],
                                        chunks=HPB, start=tt % 2 == 0, skip=True)
                    last.then_inc(s["mb"], 1)
                assert slot[0] == SLOTS


def binary_phase(nc, g, sb, ps):
    a, sem = g.a, g.sem
    xn = sb("bi_xn", [P, TT, D], F32)
    mag = sb("bi_mag", [P, 2, 2 * H], F32)
    low = sb("bi_low", [P, 2, 2 * H], F32)
    ones = sb("bi_ones", [P, P], F32)
    TP = [ps(f"bi_tp{i}", [P, T], F32) for i in range(2)]
    A1, A2 = ps("bi_a1", [P, HT, 2], F32), ps("bi_a2", [P, D], F32)
    nm, tn, s_c = Norm(sb, sem, "bi"), Turn(sem, "bi", TP), sem("bi_dve_chain")
    s_pass = sem("dve_passed")
    s_l, s_m, s_o, s_low, s_a, s_al = (sem("bi_" + n) for n in ("loaded", "mag", "ones", "low", "sums", "alphas"))
    S = (g.S1[:, :, :].rearrange("p c n -> p (c n)"), g.S2[:, :, :].rearrange("p c n -> p (c n)"))

    def act_part(act):
        act.wait_ge(s_l, 32)
        for j in range(2):
            act.activation(mag[:, j, :], g.w_stage[:, j, :], ACT.Abs).then_inc(s_m, 1)

    def dve_part(dve):
        dve.memset(ones[:, :], 1.0).then_inc(s_o, 1)
        dve.wait_ge(s_l, 32)
        for j in range(2):
            dve.tensor_scalar(low[:, j, :], g.w_stage[:, j, :], 0.0, None, ALU.is_lt).then_inc(s_low, 1)
            dve.wait_ge(s_low, 2 * j + 1)
            dve.scalar_tensor_tensor(out=S[j], in0=g.w_stage[:, j, :], scalar=0.0, in1=low[:, j, :], op0=ALU.is_gt,
                                     op1=ALU.subtract).then_inc(s_low, 1)
        dve.wait_ge(s_a, 2)
        dve.tensor_scalar(g.alpha1[:, :], A1[:, :, 0], 1.0 / D, None, ALU.mult).then_inc(s_al, 1)
        dve.tensor_scalar(g.alpha2[:, :], A2[:, :], 1.0 / H, None, ALU.mult).then_inc(s_al, 1)

    def pe_part(pe):
        pe.wait_ge(s_m, 2)
        pe.wait_ge(s_o, 1)
        for t in range(HT):
            for c in range(C):
                at = c * H + t * P
                last = pe.matmul(A1[:, t, :], mag[:, 0, at:at + P], ones[:, 0:2], start=t == 0 and c == 0, stop=c == C - 1,
                                 skip_group_check=True)
        last.then_inc(s_a, 1)
        for t in range(HT):
            last = pe.matmul(A2[:, :], ones[:, :], mag[:, 1, t * D:(t + 1) * D], start=t == 0, stop=t == HT - 1)
        last.then_inc(s_a, 1)

    with nc.Block() as block:
        @block.sync
        def _(sp):
            sp.dma_start(g.w_stage[:, 0, :].rearrange("p (c n) -> p c n", c=C),
                         a["w1_1"].rearrange("(c p) n -> p c n", p=P)).then_inc(s_l, 16)
            sp.dma_start(g.w_stage[:, 1, :].rearrange("p (t n) -> p t n", t=HT),
                         a["w2_1"].rearrange("(t p) n -> p t n", p=P)).then_inc(s_l, 16)

        norm_loops(block, g, nm, tn, xn, s_c, s_pass, {"act": act_part, "dve": dve_part, "pe": pe_part})


def ffn1_phase(nc, g, sb, ps):
    m = Mlp(sb, ps, g.sem, "ffn1", 1)
    fin = sb("f1_fin", [P, 2, 2, D], F32)
    s_c, s_out = g.sem("f1_dve_chain"), g.sem("out_stored")
    o = g.out.rearrange("(t p) d -> p t d", p=P)
    PER = 5
    with nc.Block() as block:
        @block.sync
        def _(sp):
            with sp.Fori(0, B) as i:
                sp.wait_ge(m.y_used, i + 2)
                sp.dma_start(o[:, ds(i * TT, TT), :], g.x_res[:, ds(i * TT, TT), :]).then_inc(s_out, 16)
            sp.wait_ge(s_out, 16 * B)

        @block.tensor
        def _(pe):
            weights = (lambda q, c, t: g.S1[:, c, t * P:(t + 1) * P]), (lambda q, t: g.S2[:, t, :])
            mlp_pe(pe, m, lambda q: weights, g.xT_of, p1=((0, 0), (0, 1)), p2=((0, 0), (1, 0)))

        @block.scalar
        def _(act):
            mlp_act(act, m, ACT.Gelu, lambda tile: g.col("b1_1", tile.t),
                    scale=lambda tile: g.alpha1[:, tile.t:tile.t + 1])

        @block.vector
        def _(dve):
            chains = {}

            def add_y(q, i, j, y):
                if j == 0:
                    chains["batch"] = Chain(dve, s_c, i * PER, PER)
                ch = chains["batch"]
                dst = g.x_res[:, ds(i * TT + 2 * j, 2), :]
                ch.link(dve.tensor_tensor(fin[:, j], y, tiles(g.alpha2[:, :]), ALU.mult))
                ch.link(dve.tensor_tensor(fin[:, j], fin[:, j], tiles(g.row("b2_1")), ALU.add))
                ins = dve.tensor_tensor(dst, dst, fin[:, j], ALU.add)
                if j == 0:
                    ch.inc(ins)
                else:
                    ch.end()
                return ins
            mlp_dve(dve, m, add_y)


def gate_selector():
    import numpy as np
    row = np.arange(P)
    expert = (row // (2 * EG)) * EG + row % EG
    return (expert[:, None] == np.arange(E * HE)[None, :] // HE).astype(np.float32)


def stack_selectors():
    import numpy as np
    feat, m = np.arange(P)[:, None], np.arange(P)[None, :]
    out = []
    for p in range(HPB):
        for q in range(2):
            out.append((feat == 2 * HD * p + m % (2 * HD)) & (m // (2 * HD) % 2 == q))
    for h in range(2 * HPB):
        for q in range(2):
            out.append(((feat == 2 * HD * (h // 2) + m % (2 * HD)) & (m % (2 * HD) // HD == h % 2)
                        & (m // (2 * HD) // 2 == q)) * np.float32(HD ** -0.5))
    return np.concatenate([x.astype(np.float32) for x in out], axis=1)


def kernel(**inputs):
    import numpy as np
    import concourse.bacc as bacc
    from concourse.bass_utils import run_bass_kernel_spmd as run

    v = {k: np.asarray(x) for k, x in inputs.items()}
    cc = np.ascontiguousarray

    def cols(x):
        return cc(x.reshape(-1, P).T)

    rb, eb2 = v["L0_ffn_router_b"], v["L0_ffn_b2"]
    col = {"bq0": v["L0_xattn_bq"], "bk0": v["L0_xattn_bk"], "bv0": v["L0_xattn_bv"], "b1_0": v["L0_xattn_b1"],
           "rb": np.concatenate([rb, rb]), "eb1": v["L0_ffn_b1"], "sb1": v["L0_ffn_sb1"], "bq1": v["L1_xattn_bq"],
           "bk1": v["L1_xattn_bk"], "b1_1": v["L1_ffn_b1"]}
    row = {"bo0": v["L0_xattn_bo"], "gamma": v["L0_xattn_gamma"], "beta": v["L0_xattn_beta"], "b2_0": v["L0_xattn_b2"],
           "sb2a": v["L0_ffn_sb2"][0], "sb2b": v["L0_ffn_sb2"][1], "bv1": v["L1_xattn_bv"], "bo1": v["L1_xattn_bo"],
           "b2_1": v["L1_ffn_b2"]}
    rw = v["L0_ffn_router_w"]
    wo1 = v["L1_xattn_Wo"].T.reshape(HEADS, 1, HD, D)
    arrays = {
        "x": v["x"].reshape(B * T, D), "ctx": v["ctx_1024"].reshape(B * T, D),
        "ctxT": cc(v["ctx_1024"].reshape(B * T, D).T), "mask": v["mask_Bx1xSxS2_ik1"].reshape(B * T, T),
        "cols": cc(np.concatenate([cols(col[n]) for n in COLS], axis=1)),
        "rows": cc(np.stack([row[n] for n in ROWS])), "ident": np.eye(P, dtype=np.float32),
        "pos": v["L0_xattn_pos_bias"],
        "wq0": v["L0_xattn_wq"], "wk0": v["L0_xattn_wk"], "wv0": v["L0_xattn_wv"], "wo0": v["L0_xattn_wo"],
        "w1_0": v["L0_xattn_w1"], "w2_0": v["L0_xattn_w2"],
        "rw": cc(np.concatenate([rw, rw], axis=1)),
        "eb2": cc(np.broadcast_to(eb2.reshape(GR, 1, EG, D), (GR, 2, EG, D)).reshape(P, D)),
        "ew1": cc(v["L0_ffn_w1"].transpose(1, 0, 2).reshape(D, E * HE)), "ew2": v["L0_ffn_w2"].reshape(E * HE, D),
        "sw1": cc(v["L0_ffn_sw1"].transpose(1, 0, 2).reshape(D, H)), "sw2": v["L0_ffn_sw2"].reshape(H, D),
        "sel_gate": gate_selector(), "sel_qk": stack_selectors(),
        "wq1": cc(v["L1_xattn_Wq"].T), "wk1": cc(v["L1_xattn_Wk"].T), "wv1": cc(v["L1_xattn_Wv"].T),
        "wo1": cc(np.broadcast_to(wo1, (HEADS, 2, HD, D)).reshape(HEADS * 2 * HD, D)),
        "w1_1": cc(v["L1_ffn_w1"].T), "w2_1": cc(v["L1_ffn_w2"].T),
    }
    nc = bacc.Bacc("TRN2", target_bir_lowering=False, num_devices=1)
    aps, ins = {}, {}
    for n, x in arrays.items():
        ins["in_" + n] = cc(x)
        aps[n] = nc.dram_tensor("in_" + n, x.shape, mybir.dt.from_np(x.dtype), kind="ExternalInput").ap()
    out = nc.dram_tensor("out", (B * T, D), F32, kind="ExternalOutput").ap()
    build(nc, aps, out)
    r = run(nc, [ins], core_ids=[0])
    return r.results[0]["out"].reshape(B, T, D)
```

```python
from contextlib import ExitStack

import concourse.bass as bass
from concourse import mybir

F32 = mybir.dt.float32
FR = mybir.dt.float32r
BF16 = mybir.dt.bfloat16
I32 = mybir.dt.int32
ALU = mybir.AluOpType
ACT = mybir.ActivationFunctionType
AX = mybir.AxisListType
ds = bass.ds

P = 128
B, T, D, H = 4, 512, 256, 1024
C = D // P
NT = B * T // P
TT = T // P
HT = H // P
E, K_TOP, HE = 64, 8, 64
GR = E * HE // H
EG = E // GR
HEADS, HD = 16, 16
HPB = 4
BAND = 64
EPS = 1e-5
NEG = -(2.0 ** 100)
PASSES = ((0, 0), (1, 0), (0, 1))


class Shared:
    pass


class Chain:

    def __init__(self, eng, sem, start, per, passed=None):
        self.eng, self.sem, self.start, self.per, self.passed, self.k = eng, sem, start, per, passed, 0

    def inc(self, ins):
        self.k += 1
        ins.then_inc(self.sem, 1)

    def wait(self):
        self.eng.wait_ge(self.sem, self.start + self.k)

    def hold(self):
        self.wait()
        self.eng.sem_inc(self.passed, 1)

    def link(self, ins):
        self.inc(ins)
        self.wait()

    def end(self):
        assert self.k == self.per, (self.k, self.per)


def f(ap):
    return ap.bitcast(F32)


class Norm:

    def __init__(self, sb, sem, name):
        self.st6 = sb(name + "_st6", [P, TT, 6], F32)
        self.mv = sb(name + "_mv", [P, TT, 2], F32)
        self.var = sb(name + "_var", [P, TT], F32)
        self.rstd = sb(name + "_rstd", [P, TT], F32)
        self.stats = sem(name + "_stats")
        self.var_eps = sem(name + "_var_eps")
        self.root = sem(name + "_root")
        self.passed = sem("pool_passed")


def norm_stats(dve, nm, chain, src):
    for tt in range(TT):
        chain.inc(dve.bn_stats(nm.st6[:, tt, :], src(tt)))
    chain.hold()
    for tt in range(TT):
        dve.bn_aggr(nm.mv[:, tt, :], nm.st6[:, tt, :]).then_inc(nm.stats, 1)


def norm_apply(dve, nm, n, chain, src, dst):
    dve.wait_ge(nm.root, n + 1)
    for tt in range(TT):
        chain.inc(dve.tensor_scalar(dst(tt), src(tt), nm.mv[:, tt, 0:1], nm.rstd[:, tt:tt + 1],
                                    ALU.subtract, ALU.mult))


def norm_scaled(dve, nm, n, chain, src, mid, gamma, shift, dst):
    dve.wait_ge(nm.root, n + 1)
    for tt in range(TT):
        chain.inc(dve.scalar_tensor_tensor(out=mid(tt), in0=src(tt), scalar=nm.mv[:, tt, 0:1], in1=gamma,
                                           op0=ALU.subtract, op1=ALU.mult))
    chain.wait()
    for tt in range(TT):
        chain.inc(dve.scalar_tensor_tensor(out=dst(tt), in0=mid(tt), scalar=nm.rstd[:, tt:tt + 1], in1=shift(tt),
                                           op0=ALU.mult, op1=ALU.add))


def norm_pool(pool, nm, n, power):
    pool.wait_ge(nm.stats, n * TT + TT)
    pool.sem_inc(nm.passed, 1)
    pool.tensor_scalar(nm.var[:, :], nm.mv[:, :, 1], EPS, 0.0, ALU.add, ALU.add).then_inc(nm.var_eps, 1)
    pool.wait_ge(nm.var_eps, n + 1)
    pool.tensor_tensor(nm.rstd[:, :], nm.var[:, :], power[:, 0:TT], ALU.pow).then_inc(nm.root, 1)


class Turn:

    def __init__(self, sem, name, banks):
        self.banks = banks
        self.ready = sem(name + "_turn_in")
        self.turned = sem(name + "_turned")
        self.hi = sem(name + "_turn_hi")
        self.lo = sem(name + "_turn_lo")


def turn_pe(pe, tn, n, src, ident):
    pe.wait_ge(tn.ready, n + 1)
    for c in range(C):
        pe.wait_ge(tn.lo, n * C + c + 1)
        for tt in range(TT):
            last = pe.transpose(tn.banks[c][:, tt * P:(tt + 1) * P], src(tt)[:, c * P:(c + 1) * P], ident)
        last.then_inc(tn.turned, 1)


def turn_act(act, tn, n, hi):
    for c in range(C):
        act.wait_ge(tn.turned, n * C + c + 1)
        act.activation(hi(c), tn.banks[c][:, :], ACT.Copy).then_inc(tn.hi, 1)


def turn_dve(dve, tn, n, hi, lo):
    for c in range(C):
        dve.wait_ge(tn.hi, n * C + c + 1)
        dve.tensor_tensor(lo(c), tn.banks[c][:, :], f(hi(c)), ALU.subtract).then_inc(tn.lo, 1)


def products(pe, out, lhs, rhs, chunks=C, passes=PASSES, start=True, stop=True, skip=False):
    n, m = 0, chunks * len(passes)
    for c in range(chunks):
        for a, b in passes:
            last = pe.matmul(out, lhs(a, c), rhs(b, c), start=start and n == 0, stop=stop and n == m - 1,
                             skip_group_check=skip)
            n += 1
    return last


RING = 4
LAG = 2


class Mlp:

    def __init__(self, sb, ps, sem, name, groups, gated=0):
        self.groups, self.gated = groups, gated
        self.hid = [ps(f"{name}_hid{i}", [P, T], F32) for i in range(2)]
        self.y = [ps(f"{name}_y{i}", [P, 2 * D], F32) for i in range(2)]
        self.hs = sb(name + "_hs", [P, 2, T], F32)
        self.h = [sb(f"{name}_h{'hl'[i]}", [P, RING, T], FR) for i in range(2)]
        if gated:
            self.gate = [ps(f"{name}_gate{i}", [P, T], F32) for i in range(2)]
            self.ms = sb(name + "_ms", [P, RING, T], F32)
            self.gate_ready = sem(name + "_gate_ready")
            self.gate_used = sem(name + "_gated")
        self.hid_ready = sem(name + "_hid_ready")
        self.activated = sem(name + "_activated")
        self.hi_gated = sem(name + "_hi_gated")
        self.hi_plain = sem(name + "_hi_plain")
        self.split = sem(name + "_split")
        self.h_used = sem(name + "_h_used")
        self.y_used = sem(name + "_y_used")


class Tile:

    def __init__(self, q, i, s, first=False):
        self.first = first
        self.q, self.i, self.t, self.n = q, i, s, q * B * HT + i * HT + s
        if s >= HT:
            self.i, self.t = i + 1, s - HT


def mlp_stream(eng, m, step, batch_end=None):
    for s in range(LAG):
        step(Tile(0, 0, s, s == 0), Tile(0, 0, s - 1) if s else None, None)

    def batch(q, i, peeled):
        def at(s):
            if not peeled or s < HT:
                return Tile(q, i, s)
            return Tile(q + 1, 0, s - HT, s == HT) if q + 1 < m.groups else None
        for s in range(LAG, HT + LAG):
            step(at(s), at(s - 1), at(s - LAG))
        if batch_end is not None:
            batch_end(q, i)

    for q in range(m.groups):
        with eng.Fori(0, B - 1) as i:
            batch(q, i, False)
        batch(q, B - 1, True)


def mlp_pe(pe, m, weights, xt, gate=None, new_group=None, p1=PASSES, p2=PASSES):
    pe.sem_inc(m.h_used, RING)

    def step(cur, _, back):
        if cur is not None:
            if new_group is not None and cur.first:
                new_group(cur.q)
            pe.wait_ge(m.activated, cur.n + 1)
            x = xt(cur.i)
            w1 = weights(cur.q)[0]
            products(pe, m.hid[cur.t % 2][:, :], lambda a, c: w1(a, c, cur.t), x, passes=p1).then_inc(m.hid_ready, 1)
            if cur.q < m.gated:
                pe.wait_ge(m.gate_used, cur.n + 1)
                pe.matmul(m.gate[cur.t % 2][:, :], *gate(cur), start=True, stop=True).then_inc(m.gate_ready, 1)
        if back is not None:
            t, w2 = back.t, weights(back.q)[1]
            pe.wait_ge(m.split, back.n + 1 + RING)
            if t == 0:
                pe.wait_ge(m.y_used, back.q * B + back.i + 1)
            for tt in range(TT):
                last = products(pe, m.y[tt // 2][:, (tt % 2) * D:(tt % 2 + 1) * D],
                                lambda a, c: m.h[a][:, t % RING, tt * P:(tt + 1) * P], lambda b, c: w2(b, t), chunks=1,
                                passes=p2, start=t == 0 and tt % 2 == 0, stop=t == HT - 1, skip=True)
            last.then_inc(m.h_used, 1)

    mlp_stream(pe, m, step)


def mlp_act(act, m, func, bias, scale=None):
    act.sem_inc(m.activated, 2)

    def step(cur, prev, _):
        if cur is not None:
            act.wait_ge(m.hid_ready, cur.n + 1)
            if cur.q < m.gated:
                act.wait_ge(m.gate_used, cur.n + 1)
            else:
                act.wait_ge(m.split, cur.n + RING - 1)
            act.activation(m.hs[:, cur.t % 2, :], m.hid[cur.t % 2][:, :], func, bias=bias(cur),
                           scale=1.0 if scale is None else scale(cur)).then_inc(m.activated, 1)
        if prev is not None and prev.q < m.gated:
            act.wait_ge(m.gate_used, prev.n + 3)
            act.wait_ge(m.h_used, prev.n + 1)
            act.activation(m.h[0][:, prev.t % RING, :], m.ms[:, prev.t % RING, :], ACT.Copy).then_inc(m.hi_gated, 1)

    mlp_stream(act, m, step)


def mlp_dve(dve, m, add_y):
    dve.sem_inc(m.split, RING)
    dve.sem_inc(m.y_used, 1)
    if m.gated:
        dve.sem_inc(m.gate_used, 2)

    def low(prev):
        r = prev.t % RING
        src = m.ms[:, r, :] if prev.q < m.gated else m.hs[:, prev.t % 2, :]
        if prev.q < m.gated:
            dve.wait_ge(m.hi_gated, prev.n + 1)
        else:
            dve.wait_ge(m.hi_plain, prev.n + 1 - m.gated * B * HT)
        dve.tensor_tensor(m.h[1][:, r, :], src, f(m.h[0][:, r, :]), ALU.subtract).then_inc(m.split, 1)

    def step(cur, prev, _):
        if prev is not None and prev.q >= m.gated:
            low(prev)
        if cur is not None:
            r = cur.t % RING
            dve.wait_ge(m.activated, cur.n + 3)
            if cur.q < m.gated:
                dve.wait_ge(m.gate_ready, cur.n + 1)
                dve.wait_ge(m.split, cur.n + 1)
                dve.tensor_tensor(m.ms[:, r, :], m.hs[:, cur.t % 2, :], m.gate[cur.t % 2][:, :], ALU.mult)\
                   .then_inc(m.gate_used, 1)
            else:
                dve.wait_ge(m.h_used, cur.n + 1)
                dve.tensor_copy(m.h[0][:, r, :], m.hs[:, cur.t % 2, :]).then_inc(m.hi_plain, 1)
        if prev is not None and prev.q < m.gated:
            low(prev)

    def batch_end(q, i):
        dve.wait_ge(m.h_used, Tile(q, i, HT).n + RING)
        for j in range(2):
            last = add_y(q, i, j, m.y[j][:, :].rearrange("p (t d) -> p t d", d=D))
        last.then_inc(m.y_used, 1)

    mlp_stream(dve, m, step, batch_end)


COLS = {"bq0": C, "bk0": C, "bv0": C, "b1_0": HT, "rb": 1, "eb1": GR * HT, "sb1": HT, "bq1": C, "bk1": C,
        "b1_1": HT}
ROWS = ("bo0", "gamma", "beta", "b2_0", "sb2a", "sb2b", "bv1", "bo1", "b2_1")


def col_at(name, j=0):
    names = list(COLS)
    return sum(COLS[n] for n in names[:names.index(name)]) + j


def tile_of(buf, i):
    return lambda tt: buf[:, ds(i * TT + tt, 1), :].rearrange("p a d -> p (a d)")


def own(buf):
    return lambda tt: buf[:, tt, :]


def split_dma(sp, s, dst, srcs):
    for j, src in enumerate(srcs):
        sp.dma_start(dst[:, j], src.rearrange("(c p) n -> p c n", p=P)).then_inc(s, 16)


def build(nc, a, out):
    with ExitStack() as whole:
        def maker(stack):
            def sb(name, shape, dt):
                return stack.enter_context(nc.sbuf_tensor(name, shape, dt))

            def ps(name, shape, dt):
                return stack.enter_context(nc.psum_tensor(name, shape, dt))
            return sb, ps

        sems = {}

        def sem(name):
            if name not in sems:
                sems[name] = whole.enter_context(nc.semaphore(name))
            return sems[name]

        g = Shared()
        g.a, g.out, g.sem = a, out, sem
        sb, _ = maker(whole)
        g.x_res = sb("x_res", [P, NT, D], F32)
        g.xT = [sb(f"xT_{p}", [P, C, B * T], FR) for p in "hl"]
        g.ident = sb("ident", [P, P], F32)
        g.power = sb("power", [P, TT], F32)
        g.cols = sb("cols", [P, sum(COLS.values())], F32)
        g.rows = sb("rows", [P, len(ROWS), D], F32)
        g.w_stage = sb("w_stage", [P, 2, 2 * H], F32)
        g.consts = sem("constants_loaded")
        g.w_staged = sem("w_stage_loaded")
        g.w_split = sem("w_split")
        g.col = lambda name, j=0: g.cols[:, col_at(name, j):col_at(name, j) + 1]
        g.row = lambda name: g.rows[:, ROWS.index(name), :]
        g.xT_of = lambda i: (lambda q, c: g.xT[q][:, c, ds(i * T, T)])

        g.W1, g.W2 = [], []

        def group_buffers(stack, k):
            gsb, _ = maker(stack)
            g.W1.append([gsb(f"W1_{k}{p}", [P, C, H], FR) for p in "hl"])
            g.W2.append([gsb(f"W2_{k}{p}", [P, HT, D], FR) for p in "hl"])

        with ExitStack() as st:
            group_buffers(st, 0)
            g.attn = maker(st)[0]("attn", [P, NT, D], F32)
            with ExitStack() as st1:
                aft_phase(nc, g, *maker(st1))
            with ExitStack() as st1:
                group_buffers(st1, 1)
                g.cwT = maker(st1)[0]("cwT", [P, B * T], FR)
                g.gate_sel = maker(st1)[0]("gate_sel", [P, E], F32)
                with ExitStack() as st2:
                    ffn0_phase(nc, g, *maker(st2))
                with ExitStack() as st2:
                    router_phase(nc, g, *maker(st2))
                with ExitStack() as st2:
                    moe_phase(nc, g, *maker(st2))
        with ExitStack() as st1:
            attention_phase(nc, g, *maker(st1))
        with ExitStack() as st1:
            sb1, ps1 = maker(st1)
            g.S1 = sb1("S1", [P, C, H], FR)
            g.S2 = sb1("S2", [P, HT, D], FR)
            g.alpha1 = sb1("alpha1", [P, HT], F32)
            g.alpha2 = sb1("alpha2", [P, D], F32)
            with ExitStack() as st2:
                binary_phase(nc, g, *maker(st2))
            ffn1_phase(nc, g, sb1, ps1)


def group_dma(sp, g, k):
    if k:
        sp.wait_ge(g.w_split, 4 * k)
    name1, name2, at = (("w1_0", "w2_0", 0) if k == 0 else ("ew1", "ew2", (k - 1) * H) if k <= GR
                        else ("sw1", "sw2", 0) if k == GR + 1 else ("w1_1", "w2_1", 0))
    sp.dma_start(g.w_stage[:, 0, :].rearrange("p (c n) -> p c n", c=C),
                 g.a[name1][:, at:at + H].rearrange("(c p) n -> p c n", p=P)).then_inc(g.w_staged, 16)
    sp.dma_start(g.w_stage[:, 1, :].rearrange("p (t n) -> p t n", t=HT),
                 g.a[name2][at:at + H, :].rearrange("(t p) n -> p t n", p=P)).then_inc(g.w_staged, 16)


def group_split(pool, g, k):
    pool.wait_ge(g.w_staged, 32 * (k + 1))
    for j, w in enumerate((g.W1, g.W2)):
        hi, lo = (w[k % 2][q][:, :, :].rearrange("p a b -> p (a b)") for q in range(2))
        pool.tensor_copy(hi, g.w_stage[:, j, :]).then_inc(g.w_split, 1)
        pool.wait_ge(g.w_split, 4 * k + 2 * j + 1)
        pool.tensor_tensor(lo, g.w_stage[:, j, :], f(hi), ALU.subtract).then_inc(g.w_split, 1)


def group_weights(g, k):
    return (lambda q, c, t: g.W1[k % 2][q][:, c, t * P:(t + 1) * P]), (lambda q, t: g.W2[k % 2][q][:, t, :])


def aft_phase(nc, g, sb, ps):
    a, sem = g.a, g.sem
    pair = sb("aft_pair", [P, 2, C, T], F32)
    wst = pair[:, :, :, :].rearrange("p a c t -> p (a c t)").rearrange("p (w c n) -> p w c n", w=4, c=C)
    ek, ekv = pair[:, 0], pair[:, 1]
    W = [sb(f"aft_w{p}", [P, 4, C, D], FR) for p in "hl"]
    pos = sb("aft_pos", [P, TT, T], F32)
    npm = sb("aft_npm", [P, TT], F32)
    ewT = [sb(f"aft_ewT{p}", [P, TT, T], FR) for p in "hl"]
    emb = sb("aft_emb", [P, TT, D], F32)
    embT = [sb(f"aft_embT{p}", [P, C, T], FR) for p in "hl"]
    km = sb("aft_km", [P, 3, C], F32)
    nbq = sb("aft_nbq", [P, C], F32)
    sg = sb("aft_sg", [P, C, T], F32)
    ekT = [sb(f"aft_ekT{p}", [P, TT, D], FR) for p in "hl"]
    ekvT = [sb(f"aft_ekvT{p}", [P, TT, D], FR) for p in "hl"]
    y, yT = ekv, embT
    z = pos[:, :, :].rearrange("p a b -> p (a b)")[:, 0:TT * D].rearrange("p (t d) -> p t d", d=D)
    TP = [ps(f"aft_tp{i}", [P, T], F32) for i in range(2)]
    KB = [ps(f"aft_k{i}", [P, T], F32) for i in range(2)]
    VB = [ps(f"aft_v{i}", [P, T], F32) for i in range(2)]
    QB = [ps(f"aft_q{i}", [P, T], F32) for i in range(2)]
    nm, tn = Norm(sb, sem, "aft"), Turn(sem, "aft", TP)
    s_x, s_w, s_pos, s_ctx = (sem("aft_" + n) for n in ("x_loaded", "w_loaded", "pos_loaded", "ctx_loaded"))
    s_wh, s_wl, s_rest = sem("aft_w_hi"), sem("aft_w_lo"), sem("aft_other_batches_loaded")
    s_band, s_npm, s_ew = sem("aft_band"), sem("aft_npm_done"), sem("aft_ew_done")
    s_ewt, s_ewh, s_ewl = sem("aft_ew_turned"), sem("aft_ew_hi"), sem("aft_ew_lo")
    s_c, s_pass = sem("aft_dve_chain"), sem("dve_passed")
    s_pool = sem("aft_pool")
    names = ("k", "q", "v", "nb", "ek", "e", "ekv", "ekT", "ekTh", "ekTl", "ekvT", "ekvTh", "ekvTl", "den",
             "num", "y", "yh", "yl", "attn", "z")
    s = {n: sem("aft_s_" + n) for n in names}
    PRE, PER, LAST = 16, 32, 17

    def n_emb(i):
        return 2 * i - 1

    def n_attn(i, last=False):
        return 2 * i + (1 if last else 2)

    with nc.Block() as block:
        @block.sync
        def _(sp):
            x, ctx = (a[n].rearrange("(t p) d -> p t d", p=P) for n in ("x", "ctx"))
            sp.dma_start(g.x_res[:, 0:TT, :], x[:, 0:TT]).then_inc(s_x, 16)
            sp.dma_start(g.attn[:, 0:TT, :], ctx[:, 0:TT]).then_inc(s_ctx, 16)
            sp.dma_start(g.cols[:, :], a["cols"]).then_inc(g.consts, 16)
            sp.dma_start(g.ident[:, :], a["ident"]).then_inc(g.consts, 16)
            sp.dma_start(g.rows[:, :, :].rearrange("p r d -> p (r d)"),
                         a["rows"].rearrange("r d -> (r d)").partition_broadcast(P)).then_inc(g.consts, 16)
            sp.dma_start(g.x_res[:, TT:, :], x[:, TT:]).then_inc(s_rest, 16)
            sp.dma_start(g.attn[:, TT:, :], ctx[:, TT:]).then_inc(s_rest, 16)
            group_dma(sp, g, 0)
            group_dma(sp, g, 1)

        @block.scalar
        def _(act):
            act.dma_start(pos[:, :, :], a["pos"].rearrange("(t p) n -> p t n", p=P)).then_inc(s_pos, 16)
            for j, n in enumerate(("wq0", "wk0", "wv0", "wo0")):
                act.dma_start(wst[:, j], a[n].rearrange("(c p) n -> p c n", p=P)).then_inc(s_w, 16)
            act.wait_ge(s_w, 64)
            act.activation(W[0][:, :, :, :], wst, ACT.Copy).then_inc(s_wh, 1)
            for tt in range(TT):
                act.wait_ge(s_npm, 1)
                act.activation(pos[:, tt, :], pos[:, tt, :], ACT.Exp, bias=npm[:, tt:tt + 1]).then_inc(s_ew, 1)
            turn_act(act, tn, 0, lambda c: embT[0][:, c, :])
            for jc in range(TT):
                act.wait_ge(s_ewt, jc + 1)
                act.activation(ewT[0][:, jc, :], QB[jc % 2][:, :], ACT.Copy).then_inc(s_ewh, 1)

            def exponentials(i):
                for c in range(C):
                    act.wait_ge(s["nb"], i + 1)
                    act.activation(ek[:, c, :], KB[c][:, :], ACT.Exp, bias=km[:, 2, c:c + 1]).then_inc(s["ek"], 1)
                for c in range(C):
                    act.wait_ge(s["q"], 2 * i + c + 1)
                    act.activation(sg[:, c, :], QB[c][:, :], ACT.Exp, bias=nbq[:, c:c + 1], scale=-1.0)\
                       .then_inc(s["e"], 1)

            def main(i):
                for src, dst, inn, done in ((KB, ekT, s["ekT"], s["ekTh"]), (VB, ekvT, s["ekvT"], s["ekvTh"])):
                    for j in range(2):
                        act.wait_ge(inn, 2 * i + j + 1)
                        act.activation(dst[0][:, 2 * j:2 * j + 2, :], src[j][:, :].rearrange("p (t d) -> p t d", d=D),
                                       ACT.Copy).then_inc(done, 1)
                for c in range(C):
                    act.wait_ge(s["y"], 2 * i + c + 1)
                    act.activation(yT[0][:, c, :], y[:, c, :], ACT.Copy).then_inc(s["yh"], 1)

            exponentials(0)
            with act.Fori(0, B - 1) as i:
                main(i)
                turn_act(act, tn, n_emb(i + 1), lambda c: embT[0][:, c, :])
                exponentials(i + 1)
                turn_act(act, tn, n_attn(i), lambda c: g.xT_of(i)(0, c))
            main(B - 1)
            turn_act(act, tn, n_attn(B - 1, True), lambda c: g.xT_of(B - 1)(0, c))

        @block.gpsimd
        def _(pool):
            pool.memset(g.power[:, :], -0.5).then_inc(s_pool, 1)
            pool.wait_ge(s_pool, 1)
            norm_pool(pool, nm, 0, g.power)
            pool.wait_ge(s_pos, 16)
            pool.affine_select(out=pos[:, :, :], in_=pos[:, :, :], compare_op=ALU.is_ge, fill=0.0, base=BAND - 1,
                               pattern=[[-P, TT], [1, T]], channel_multiplier=-1).then_inc(s_band, 1)
            pool.wait_ge(s_band, 1)
            pool.affine_select(out=pos[:, :, :], in_=pos[:, :, :], compare_op=ALU.is_ge, fill=0.0, base=BAND - 1,
                               pattern=[[P, TT], [-1, T]], channel_multiplier=1).then_inc(s_band, 1)
            group_split(pool, g, 0)
            with pool.Fori(0, B - 1) as i:
                norm_pool(pool, nm, n_emb(i + 1), g.power)
                norm_pool(pool, nm, n_attn(i), g.power)
            norm_pool(pool, nm, n_attn(B - 1, True), g.power)

        @block.vector
        def _(dve):
            dve.sem_inc(tn.lo, C)

            def emb_stats(i, ch):
                norm_stats(dve, nm, ch, tile_of(g.x_res, i))

            def emb_norm(i, n, ch):
                norm_apply(dve, nm, n, ch, tile_of(g.x_res, i), own(emb))

            def emb_add(i, n, ch):
                ch.wait()
                dve.tensor_tensor(emb[:, :, :], emb[:, :, :], g.attn[:, ds(i * TT, TT), :], ALU.add)\
                   .then_inc(tn.ready, 1)
                dve.wait_ge(tn.ready, n + 1)
                dve.sem_inc(s_pass, 1)
                for tt in range(TT):
                    ch.inc(dve.tensor_tensor(tile_of(g.attn, i)(tt), emb[:, tt, :], g.row("bo0"), ALU.add))

            def turn_emb(n):
                turn_dve(dve, tn, n, lambda c: embT[0][:, c, :], lambda c: embT[1][:, c, :])

            def k_max(i, ch):
                for c in range(C):
                    dve.wait_ge(s["k"], 2 * i + c + 1)
                    ch.inc(dve.tensor_reduce(km[:, 0, c:c + 1], KB[c][:, :], AX.X, ALU.max))
                ch.wait()
                bk = g.cols[:, col_at("bk0"):col_at("bk0") + C]
                ch.link(dve.tensor_tensor(km[:, 1, :], km[:, 0, :], bk, ALU.add))
                dve.tensor_tensor(km[:, 2, :], bk, km[:, 1, :], ALU.subtract).then_inc(s["nb"], 1)

            def weighted(i):
                for c in range(C):
                    dve.wait_ge(s["v"], 2 * i + c + 1)
                    dve.wait_ge(s["ek"], 2 * i + c + 1)
                    dve.scalar_tensor_tensor(out=ekv[:, c, :], in0=VB[c][:, :], scalar=g.col("bv0", c),
                                             in1=ek[:, c, :], op0=ALU.add, op1=ALU.mult).then_inc(s["ekv"], 1)

            def main(i, ch, following):
                for src, dst, hi, lo in ((KB, ekT, s["ekTh"], s["ekTl"]), (VB, ekvT, s["ekvTh"], s["ekvTl"])):
                    for j in range(2):
                        dve.wait_ge(hi, 2 * i + j + 1)
                        dve.tensor_tensor(dst[1][:, 2 * j:2 * j + 2, :], src[j][:, :].rearrange("p (t d) -> p t d", d=D),
                                          f(dst[0][:, 2 * j:2 * j + 2, :]), ALU.subtract).then_inc(lo, 1)
                if following:
                    emb_stats(i + 1, ch)
                dve.wait_ge(s["e"], 2 * i + 2)
                for c in range(C):
                    dve.wait_ge(s["den"], 2 * i + c + 1)
                    ch.link(dve.scalar_tensor_tensor(out=sg[:, c, :], in0=sg[:, c, :], scalar=1.0, in1=TP[c][:, :],
                                                     op0=ALU.add, op1=ALU.mult))
                    ch.inc(dve.reciprocal(sg[:, c, :], sg[:, c, :]))
                ch.wait()
                for c in range(C):
                    dve.wait_ge(s["num"], 2 * i + c + 1)
                    dve.tensor_tensor(y[:, c, :], KB[c][:, :], sg[:, c, :], ALU.mult).then_inc(s["y"], 1)
                if following:
                    emb_norm(i + 1, n_emb(i + 1), ch)
                for c in range(C):
                    dve.wait_ge(s["yh"], 2 * i + c + 1)
                    dve.tensor_tensor(yT[1][:, c, :], y[:, c, :], f(yT[0][:, c, :]), ALU.subtract).then_inc(s["yl"], 1)

            def attention(i, ch):
                dve.wait_ge(s["attn"], i + 1)
                for j in range(2):
                    dve.tensor_tensor(z[:, 2 * j:2 * j + 2, :], QB[j][:, :].rearrange("p (t d) -> p t d", d=D),
                                      g.attn[:, ds(i * TT + 2 * j, 2), :], ALU.add).then_inc(s["z"], 1)

            def attention_norm(i, n, ch):
                dve.wait_ge(s["z"], 2 * i + 2)
                dve.sem_inc(s_pass, 1)
                norm_stats(dve, nm, ch, own(z))
                norm_scaled(dve, nm, n, ch, own(z), own(z), g.row("gamma"), lambda tt: g.row("beta"), own(z))
                ch.wait()
                dve.sem_inc(tn.ready, 1)
                ch.inc(dve.tensor_copy(g.attn[:, ds(i * TT, TT), :], z))

            def turn_attention(i, n):
                turn_dve(dve, tn, n, lambda c: g.xT_of(i)(0, c), lambda c: g.xT_of(i)(1, c))

            dve.wait_ge(s_x, 16)
            ch = Chain(dve, s_c, 0, PRE, s_pass)
            emb_stats(0, ch)
            emb_norm(0, 0, ch)
            dve.wait_ge(s_ctx, 16)
            dve.wait_ge(g.consts, 48)
            emb_add(0, 0, ch)
            ch.inc(dve.tensor_scalar(nbq[:, :], g.cols[:, col_at("bq0"):col_at("bq0") + C], -1.0, None, ALU.mult))
            dve.wait_ge(s_band, 2)
            dve.tensor_reduce(npm[:, :], pos[:, :, :], AX.X, ALU.max, negate=True).then_inc(s_npm, 1)
            dve.wait_ge(s_wh, 1)
            dve.tensor_tensor(W[1][:, :, :, :], wst, f(W[0][:, :, :, :]), ALU.subtract).then_inc(s_wl, 1)
            turn_emb(0)
            for jc in range(TT):
                dve.wait_ge(s_ewh, jc + 1)
                dve.tensor_tensor(ewT[1][:, jc, :], QB[jc % 2][:, :], f(ewT[0][:, jc, :]), ALU.subtract)\
                   .then_inc(s_ewl, 1)
            k_max(0, ch)
            ch.end()
            dve.wait_ge(s_rest, 32)
            weighted(0)
            with dve.Fori(0, B - 1) as i:
                ch = Chain(dve, s_c, i * PER + PRE, PER, s_pass)
                main(i, ch, True)
                emb_add(i + 1, n_emb(i + 1), ch)
                attention(i, ch)
                turn_emb(n_emb(i + 1))
                attention_norm(i, n_attn(i), ch)
                k_max(i + 1, ch)
                weighted(i + 1)
                turn_attention(i, n_attn(i))
                ch.end()
            ch = Chain(dve, s_c, (B - 1) * PER + PRE, LAST, s_pass)
            main(B - 1, ch, False)
            attention(B - 1, ch)
            attention_norm(B - 1, n_attn(B - 1, True), ch)
            turn_attention(B - 1, n_attn(B - 1, True))
            ch.end()

        @block.tensor
        def _(pe):
            pe.wait_ge(g.consts, 48)
            turn_pe(pe, tn, 0, own(emb), g.ident[:, :])
            pe.wait_ge(s_ew, TT)
            for jc in range(TT):
                if jc >= 2:
                    pe.wait_ge(s_ewl, jc - 1)
                for tt in range(TT):
                    last = pe.transpose(QB[jc % 2][:, tt * P:(tt + 1) * P], pos[:, tt, jc * P:(jc + 1) * P],
                                        g.ident[:, :])
                last.then_inc(s_ewt, 1)
            pe.wait_ge(s_wl, 1)

            def project(i, n, before_q):
                pe.wait_ge(tn.lo, n * C + 2 * C)
                for w, banks, done in ((1, KB, s["k"]), (2, VB, s["v"]), (0, QB, s["q"])):
                    if w == 0:
                        before_q()
                    for m in range(C):
                        products(pe, banks[m][:, :], lambda q, c: W[q][:, w, c, m * P:(m + 1) * P],
                                 lambda q, c: embT[q][:, c, :]).then_inc(done, 1)

            def turn_weights(i, src, banks, inn, done):
                pe.wait_ge(inn, 2 * i + 2)
                for jc in range(TT):
                    for c in range(C):
                        at = (jc % 2) * D + c * P
                        last = pe.transpose(banks[jc // 2][:, at:at + P], src[:, c, jc * P:(jc + 1) * P], g.ident[:, :])
                    if jc % 2:
                        last.then_inc(done, 1)

            def turn_ek(i):
                turn_weights(i, ek, KB, s["ek"], s["ekT"])

            def turn_ekv(i):
                turn_weights(i, ekv, VB, s["ekv"], s["ekvT"])

            def main(i):
                for src, banks, inn, done in ((ekT, TP, s["ekTl"], s["den"]), (ekvT, KB, s["ekvTl"], s["num"])):
                    pe.wait_ge(inn, 2 * i + 2)
                    for c in range(C):
                        products(pe, banks[c][:, :], lambda q, jc: src[q][:, jc, c * P:(c + 1) * P],
                                 lambda q, jc: ewT[q][:, jc, :], chunks=TT).then_inc(done, 1)
                pe.wait_ge(s["yl"], 2 * i + 2)
                for tt in range(TT):
                    last = products(pe, QB[tt // 2][:, (tt % 2) * D:(tt % 2 + 1) * D],
                                    lambda q, c: yT[q][:, c, tt * P:(tt + 1) * P], lambda q, c: W[q][:, 3, c, :],
                                    start=tt % 2 == 0, skip=True)
                last.then_inc(s["attn"], 1)

            project(0, 0, lambda: pe.wait_ge(s_ewl, TT))
            turn_ek(0)
            turn_ekv(0)
            with pe.Fori(0, B - 1) as i:
                main(i)
                turn_pe(pe, tn, n_emb(i + 1), own(emb), g.ident[:, :])
                project(i + 1, n_emb(i + 1), lambda: pe.wait_ge(s["z"], 2 * i + 2))
                turn_ek(i + 1)
                turn_pe(pe, tn, n_attn(i), own(z), g.ident[:, :])
                turn_ekv(i + 1)
            main(B - 1)
            turn_pe(pe, tn, n_attn(B - 1, True), own(z), g.ident[:, :])


def tiles(row, n=2):
    return row.unsqueeze(1).to_broadcast([P, n, D])


def ffn0_phase(nc, g, sb, ps):
    m = Mlp(sb, ps, g.sem, "ffn0", 1)
    s_b2, s_beta = g.sem("ffn0_b2_added"), g.sem("ffn0_beta_added")
    with nc.Block() as block:
        @block.sync
        def _(sp):
            group_dma(sp, g, 2)

        @block.gpsimd
        def _(pool):
            pool.tensor_tensor(g.attn[:, :, :], g.attn[:, :, :], tiles(g.row("b2_0"), NT), ALU.add).then_inc(s_b2, 1)
            pool.tensor_tensor(g.x_res[:, :, :], g.x_res[:, :, :], tiles(g.row("beta"), NT), ALU.add).then_inc(s_beta, 1)
            group_split(pool, g, 1)
            pool.wait_ge(s_beta, 1)

        @block.tensor
        def _(pe):
            pe.wait_ge(g.w_split, 4)
            mlp_pe(pe, m, lambda q: group_weights(g, 0), g.xT_of)

        @block.scalar
        def _(act):
            mlp_act(act, m, ACT.Relu, lambda tile: g.col("b1_0", tile.t))

        @block.vector
        def _(dve):
            def add_y(q, i, j, y):
                dst = g.attn[:, ds(i * TT + 2 * j, 2), :]
                dve.wait_ge(s_b2, 1)
                return dve.tensor_tensor(dst, y, dst, ALU.add)
            mlp_dve(dve, m, add_y)


def router_phase(nc, g, sb, ps):
    a, sem = g.a, g.sem
    xn = sb("rt_xn", [P, TT, D], F32)
    rws = sb("rt_rws", [P, C, P], F32)
    RW = [sb(f"rt_rw{p}", [P, C, P], FR) for p in "hl"]
    b2s = sb("rt_b2s", [P, D], F32)
    B2 = [sb(f"rt_b2{p}", [P, D], FR) for p in "hl"]
    lgT = sb("rt_lgT", [P, T], F32)
    lg = sb("rt_lg", [P, TT, E], F32)
    left = sb("rt_left", [P, TT, E], F32)
    top = sb("rt_top", [P, TT, K_TOP], F32)
    ntop = sb("rt_ntop", [P, TT], F32)
    ex = sb("rt_ex", [P, TT, E], F32)
    tot = sb("rt_tot", [P, TT], F32)
    cwx = sb("rt_cwx", [P, TT, GR, 2, EG], FR)
    cwTs = sb("rt_cwTs", [P, T], FR)
    TP = [ps(f"rt_tp{i}", [P, T], F32) for i in range(2)]
    LG, LT, CT = (ps("rt_" + n, [P, T], F32) for n in ("lgp", "ltp", "ctp"))
    YB = [ps(f"rt_yb{i}", [P, 2 * D], F32) for i in range(2)]
    nm, tn = Norm(sb, sem, "rt"), Turn(sem, "rt", TP)
    s_w, s_wh, s_wl, s_c = (sem("rt_" + n) for n in ("w_loaded", "w_hi", "w_lo", "dve_chain"))
    s_pass = sem("dve_passed")
    s = {n: sem("rt_s_" + n) for n in ("lg", "lgT", "lt", "ntop", "ex", "cwx", "ct", "cwTs", "yb")}
    sb2 = sb("rt_sb2", [P, D], F32)
    s_sum, s_sb2 = sem("rt_sb2_summed"), sem("rt_sb2_added")
    PRE, PER, LAST = 20, 40, 20

    with nc.Block() as block:
        @block.sync
        def _(sp):
            sp.dma_start(rws[:, :, :], a["rw"].rearrange("(c p) n -> p c n", p=P)).then_inc(s_w, 16)
            sp.dma_start(b2s[:, :], a["eb2"]).then_inc(s_w, 16)
            sp.dma_start(g.gate_sel[:, :], a["sel_gate"]).then_inc(s_w, 16)

        @block.gpsimd
        def _(pool):
            pool.tensor_tensor(sb2[:, :], g.row("sb2a"), g.row("sb2b"), ALU.add).then_inc(s_sum, 1)

            def roots(i):
                norm_pool(pool, nm, 2 * i, g.power)
                norm_pool(pool, nm, 2 * i + 1, g.power)

            def add_sb2(i):
                pool.wait_ge(tn.ready, i + 1)
                pool.sem_inc(nm.passed, 1)
                x_b = g.x_res[:, ds(i * TT, TT), :]
                pool.tensor_tensor(x_b, x_b, tiles(sb2[:, :], TT), ALU.add).then_inc(s_sb2, 1)

            roots(0)
            pool.wait_ge(s_sum, 1)
            with pool.Fori(0, B - 1) as i:
                add_sb2(i)
                roots(i + 1)
            add_sb2(B - 1)

        @block.scalar
        def _(act):
            act.sem_inc(s["cwTs"], 1)
            act.wait_ge(s_w, 48)
            act.activation(RW[0][:, :, :], rws[:, :, :], ACT.Copy).then_inc(s_wh, 1)
            act.activation(B2[0][:, :], b2s[:, :], ACT.Copy).then_inc(s_wh, 1)
            with act.Fori(0, B) as i:
                turn_act(act, tn, i, lambda c: g.xT_of(i)(0, c))
                act.wait_ge(s["lg"], i + 1)
                act.activation(lgT[:, :], LG[:, :], ACT.Identity, bias=g.col("rb")).then_inc(s["lgT"], 1)
                act.wait_ge(s["ntop"], i + 1)
                for tt in range(TT):
                    act.activation(ex[:, tt, :], lg[:, tt, :], ACT.Exp, bias=ntop[:, tt:tt + 1]).then_inc(s["ex"], 1)
                act.wait_ge(s["ct"], i + 1)
                act.activation(cwTs[:, :], CT[:, :], ACT.Copy).then_inc(s["cwTs"], 1)
                act.activation(g.cwT[:, ds(i * T, T)], CT[:, :], ACT.Copy).then_inc(s["cwTs"], 1)

        @block.vector
        def _(dve):
            dve.sem_inc(tn.lo, C)

            def x_new(i, ch):
                norm_scaled(dve, nm, 2 * i, ch, tile_of(g.attn, i), own(xn), g.row("gamma"), tile_of(g.x_res, i),
                            tile_of(g.x_res, i))

            def x_stats(i, ch):
                ch.hold()
                norm_stats(dve, nm, ch, tile_of(g.x_res, i))

            def x_norm(i, ch):
                norm_apply(dve, nm, 2 * i + 1, ch, tile_of(g.x_res, i), own(xn))
                ch.wait()
                dve.sem_inc(tn.ready, 1)

            ch = Chain(dve, s_c, 0, PRE, s_pass)
            norm_stats(dve, nm, ch, tile_of(g.attn, 0))
            x_new(0, ch)
            x_stats(0, ch)
            x_norm(0, ch)
            ch.end()
            dve.wait_ge(s_wh, 2)
            dve.tensor_tensor(RW[1][:, :, :], rws[:, :, :], f(RW[0][:, :, :]), ALU.subtract).then_inc(s_wl, 1)
            dve.tensor_tensor(B2[1][:, :], b2s[:, :], f(B2[0][:, :]), ALU.subtract).then_inc(s_wl, 1)

            def batch(i, ch, following):
                turn_dve(dve, tn, i, lambda c: g.xT_of(i)(0, c), lambda c: g.xT_of(i)(1, c))
                if following:
                    norm_stats(dve, nm, ch, tile_of(g.attn, i + 1))
                    x_new(i + 1, ch)
                dve.wait_ge(s["lt"], i + 1)
                ch.inc(dve.tensor_copy(lg[:, :, :], LT[:, :].rearrange("p (t e) -> p t e", t=TT)[:, :, 0:E]))
                ch.hold()
                for tt in range(TT):
                    ch.inc(dve.max(top[:, tt, :], lg[:, tt, :]))
                ch.wait()
                dve.tensor_scalar(ntop[:, :], top[:, :, 0], -1.0, None, ALU.mult).then_inc(s["ntop"], 1)
                for tt in range(TT):
                    ch.inc(dve.match_replace(left[:, tt, :], top[:, tt, :], lg[:, tt, :], -3e38))
                ch.wait()
                ch.link(dve.tensor_tensor(left[:, :, :], lg[:, :, :], left[:, :, :], ALU.not_equal))
                dve.wait_ge(s["ex"], TT * i + TT)
                ch.link(dve.tensor_tensor(ex[:, :, :], ex[:, :, :], left[:, :, :], ALU.mult))
                ch.link(dve.tensor_reduce(tot[:, :], ex[:, :, :], AX.X, ALU.add))
                ch.link(dve.reciprocal(tot[:, :], tot[:, :]))
                for tt in range(TT):
                    ch.inc(dve.tensor_scalar(ex[:, tt, :], ex[:, tt, :], tot[:, tt:tt + 1], None, ALU.mult))
                ch.wait()
                cw = ex[:, :, :].rearrange("p t (g e) -> p t g e", g=GR)
                ch.link(dve.tensor_copy(cwx[:, :, :, 0, :], cw))
                dve.tensor_tensor(cwx[:, :, :, 1, :], cw, f(cwx[:, :, :, 0, :]), ALU.subtract).then_inc(s["cwx"], 1)
                if following:
                    x_stats(i + 1, ch)
                    x_norm(i + 1, ch)
                dve.wait_ge(s_sb2, i + 1)
                dve.wait_ge(s["yb"], i + 1)
                for j in range(2):
                    dst = g.x_res[:, ds(i * TT + 2 * j, 2), :]
                    ch.inc(dve.tensor_tensor(dst, YB[j][:, :].rearrange("p (t d) -> p t d", d=D), dst, ALU.add))
                ch.wait()
                ch.end()

            with dve.Fori(0, B - 1) as i:
                batch(i, Chain(dve, s_c, PRE + i * PER, PER, s_pass), True)
            batch(B - 1, Chain(dve, s_c, PRE + (B - 1) * PER, LAST, s_pass), False)

        @block.tensor
        def _(pe):
            pe.wait_ge(s_wl, 2)
            with pe.Fori(0, B) as i:
                turn_pe(pe, tn, i, own(xn), g.ident[:, :])
                pe.wait_ge(tn.lo, C * i + 2 * C)
                products(pe, LG[:, :], lambda q, c: RW[q][:, c, :], g.xT_of(i)).then_inc(s["lg"], 1)
                pe.wait_ge(s["lgT"], i + 1)
                for tt in range(TT):
                    last = pe.transpose(LT[:, tt * P:(tt + 1) * P], lgT[:, tt * P:(tt + 1) * P], g.ident[:, :])
                last.then_inc(s["lt"], 1)
                pe.wait_ge(s["cwx"], i + 1)
                pe.wait_ge(s["cwTs"], 2 * i + 1)
                for tt in range(TT):
                    last = pe.transpose(CT[:, tt * P:(tt + 1) * P],
                                        f(cwx[:, tt, :, :, :].rearrange("p g q e -> p (g q e)")), g.ident[:, :])
                last.then_inc(s["ct"], 1)
                pe.wait_ge(s["cwTs"], 2 * i + 2)
                for tt in range(TT):
                    for q in range(2):
                        last = pe.matmul(YB[tt // 2][:, (tt % 2) * D:(tt % 2 + 1) * D], cwTs[:, tt * P:(tt + 1) * P],
                                         B2[q][:, :], start=tt % 2 == 0 and q == 0, stop=q == 1, skip_group_check=True)
                last.then_inc(s["yb"], 1)


def moe_phase(nc, g, sb, ps):
    a, sem = g.a, g.sem
    m = Mlp(sb, ps, sem, "moe", GR + 1, gated=GR)
    SEL = sb("moe_sel", [P, GR * HT, P], FR)
    s_selr = sem("moe_sel_ready")

    with nc.Block() as block:
        @block.sync
        def _(sp):
            for k in range(3, GR + 2):
                group_dma(sp, g, k)

        @block.gpsimd
        def _(pool):
            for k in range(2, GR + 2):
                if k > 2:
                    pool.wait_ge(m.h_used, RING + (k - 2) * B * HT)
                group_split(pool, g, k)

        @block.tensor
        def _(pe):
            def new_group(q):
                pe.wait_ge(g.w_split, 4 * (q + 2))
                if q < GR:
                    pe.wait_ge(s_selr, q + 1)

            mlp_pe(pe, m, lambda q: group_weights(g, q + 1), g.xT_of,
                   gate=lambda tile: (SEL[:, tile.q * HT + tile.t, :], g.cwT[:, ds(tile.i * T, T)]),
                   new_group=new_group)

        @block.scalar
        def _(act):
            mlp_act(act, m, ACT.Silu,
                    lambda tile: g.col("eb1", tile.q * HT + tile.t) if tile.q < GR else g.col("sb1", tile.t))

        @block.vector
        def _(dve):
            for q in range(GR):
                dve.tensor_copy(SEL[:, q * HT:(q + 1) * HT, :].rearrange("p t m -> p (t m)").rearrange("p (e m) -> p e m", m=HE),
                                g.gate_sel[:, q * EG:(q + 1) * EG].unsqueeze(2).to_broadcast([P, EG, HE])).then_inc(s_selr, 1)

            def add_y(q, i, j, y):
                dst = g.x_res[:, ds(i * TT + 2 * j, 2), :]
                return dve.tensor_tensor(dst, y, dst, ALU.add)
            mlp_dve(dve, m, add_y)


class NormTurn:

    def __init__(self, g, sb, name, xn, banks):
        self.g, self.xn = g, xn
        self.nm, self.tn = Norm(sb, g.sem, name), Turn(g.sem, name, banks)
        self.s_c, self.s_pass = g.sem(name + "_norm_chain"), g.sem("dve_passed")

    def pool(self, pool):
        with pool.Fori(0, B) as i:
            norm_pool(pool, self.nm, i, self.g.power)

    def act(self, act, mid, before=B - 1):
        for first, last in ((0, before), (before, B)):
            with act.Fori(first, last) as i:
                turn_act(act, self.tn, i, lambda c: self.g.xT_of(i)(0, c))
            if last == before:
                mid()

    def dve(self, dve, mid):
        g, nm, tn = self.g, self.nm, self.tn

        def apply(i, ch):
            norm_apply(dve, nm, i, ch, tile_of(g.x_res, i), own(self.xn))
            ch.wait()
            dve.sem_inc(tn.ready, 1)

        def turn(i):
            turn_dve(dve, tn, i, lambda c: g.xT_of(i)(0, c), lambda c: g.xT_of(i)(1, c))

        dve.sem_inc(tn.lo, C)
        ch = Chain(dve, self.s_c, 0, 2 * TT, self.s_pass)
        norm_stats(dve, nm, ch, tile_of(g.x_res, 0))
        apply(0, ch)
        with dve.Fori(0, B - 1) as i:
            ch = Chain(dve, self.s_c, (i + 1) * 2 * TT, 2 * TT, self.s_pass)
            norm_stats(dve, nm, ch, tile_of(g.x_res, i + 1))
            turn(i)
            apply(i + 1, ch)
            ch.end()
        mid()
        turn(B - 1)

    def pe(self, pe, mid=lambda: None):
        with pe.Fori(0, B - 1) as i:
            turn_pe(pe, self.tn, i, own(self.xn), self.g.ident[:, :])
        mid()
        turn_pe(pe, self.tn, B - 1, own(self.xn), self.g.ident[:, :])


def attention_phase(nc, g, sb, ps):
    a, sem = g.a, g.sem
    WP = [sb(f"at_w{p}", [P, 3, C, D], FR) for p in "hl"]
    WO = [sb(f"at_wo{p}", [P, HPB, D], FR) for p in "hl"]
    SELK = sb("at_selk", [P, HPB, 2, P], FR)
    SELQ = sb("at_selq", [P, 2 * HPB, 2, P], FR)
    cT = [sb(f"at_cT{p}", [P, C, T], FR) for p in "hl"]
    kT = [sb(f"at_kT{p}", [P, C, T], FR) for p in "hl"]
    qT = kT
    KST = sb("at_kst", [P, HEADS // 2, T], FR)
    QST = sb("at_qst", [P, 2, T], FR)
    VAUG = sb("at_vaug", [P, TT, HEADS, P], FR)
    PTS = [sb(f"at_pt{p}", [P, 2, T], FR) for p in "hl"]
    PR = sb("at_p", [P, 2, TT, T], F32)
    mst = sb("at_mst", [P, 2, T], I32)
    mk = sb("at_mk", [P, TT, T], BF16)
    nid = sb("at_nid", [P, P], BF16)
    nmx = sb("at_nmx", [P, 2, TT], F32)
    den = sb("at_den", [P, TT, HEADS], F32)
    stage = g.w_stage[:, :, :].rearrange("p a n -> p (a n)")
    cst = stage[:, 0:C * T].rearrange("p (c t) -> p c t", c=C)
    OS = stage[:, 1024:3072].rearrange("p (g t) -> p g t", g=HPB)
    vS = stage[:, 3072:4096].rearrange("p (t d) -> p t d", t=TT)
    wst = stage[:, 1024:1024 + 3 * C * D].rearrange("p (w c n) -> p w c n", w=3, c=C)
    wost = PR[:, :, :, :].rearrange("p a b t -> p (a b t)")[:, 24 * P:24 * P + HPB * D].rearrange("p (g n) -> p g n", g=HPB)
    selst = PR[:, 0:2, :, :].rearrange("p a b t -> p (a b t)")[:, 0:24 * P]
    NK = 2 * HPB * P
    RDR = PR[:, 0, :, :]
    ON = (KST[:, 0:HPB, :], KST[:, HPB:2 * HPB, :])
    PT = [ps(f"at_tp{i}", [P, T], F32) for i in range(2)]
    OB = ps("at_o", [P, T], F32)
    QB = ps("at_qb", [P, T], F32)
    SB = [ps(f"at_s{i}", [P, T], F32) for i in range(TT)]
    MB, NB = SB, len(SB)
    nt = NormTurn(g, sb, "at", vS, PT)
    s_w, s_sel, s_ws, s_wh, s_wl = (sem("at_" + n) for n in ("w_loaded", "sel_loaded", "sel_split", "w_hi", "w_lo"))
    s_pass = sem("dve_passed")
    s_c, s_z, s_nid = sem("at_dve_chain"), sem("at_zeroed"), sem("at_nid_ready")
    names = ("ctx", "cTh", "cTl", "mld", "mk", "mb", "mbf", "kqh", "v", "vh", "kst", "qs", "qst", "s", "nmx", "p",
             "pt", "pth", "ptl", "pv", "os", "rdr", "on", "onh", "onl")
    s = {n: sem("at_s_" + n) for n in names}
    SLOTS = 20
    NP = HEADS * TT
    PER = 11
    ACT_SLOTS = (5, 7, 9, 11)
    DS = SLOTS - len(ACT_SLOTS)

    def emptied(eng, i, n):
        if n in ACT_SLOTS:
            eng.wait_ge(s["kst"], len(ACT_SLOTS) * i + ACT_SLOTS.index(n) + 1)
        else:
            eng.wait_ge(s["mbf"], DS * i + NB + sum(k not in ACT_SLOTS for k in range(n + 1)) + min(n + 1, 0))

    with nc.Block() as block:
        @block.sync
        def _(sp):
            def load_ctx(i):
                sp.dma_start(cst, a["ctxT"][:, ds(i * T, T)].rearrange("(c p) t -> p c t", p=P)).then_inc(s["ctx"], 16)

            load_ctx(0)
            for j, n in enumerate(("wq1", "wk1", "wv1")):
                sp.dma_start(wst[:, j], a[n].rearrange("(c p) n -> p c n", p=P)).then_inc(s_w, 16)
            sp.dma_start(wost, a["wo1"].rearrange("(g p) n -> p g n", p=P)).then_inc(s_w, 16)
            sp.dma_start(selst, a["sel_qk"]).then_inc(s_sel, 16)
            with sp.Fori(0, B) as i:
                for j in range(2):
                    sp.wait_ge(s["mk"], 2 * i + j + 1)
                    sp.dma_start(mst[:, :, :], a["mask"][ds(i * T + j * 2 * P, 2 * P), :]
                                 .rearrange("(t p) k -> p t k", p=P)).then_inc(s["mld"], 16)
                sp.wait_ge(s["cTl"], i + 2)
                load_ctx((i + 1) % B)

        @block.gpsimd
        def _(pool):
            nt.pool(pool)
            pool.memset(f(VAUG[:, :, :, :]), 0.0).then_inc(s_z, 1)
            pool.sem_inc(s["v"], 1)
            pool.wait_ge(g.consts, 48)
            pool.tensor_scalar(nid[:, :], g.ident[:, :], NEG, 1.0, ALU.mult, ALU.mult).then_inc(s_nid, 1)
            vh = vS.rearrange("p t (h d) -> p t h d", d=HD)
            pool.wait_ge(s_z, 1)
            with pool.Fori(0, B) as i:
                emptied(pool, i, 3)
                pool.sem_inc(sem("pool_passed"), 1)
                for j in range(HPB):
                    pool.tensor_copy(VAUG[:, :, j::HPB, 2 * HD * j:2 * HD * j + HD], vh[:, :, j::HPB, :])\
                        .then_inc(s["vh"], 1)
                pool.wait_ge(s["vh"], HPB * i + HPB)
                for j in range(HPB):
                    pool.tensor_tensor(VAUG[:, :, j::HPB, 2 * HD * j + HD:2 * HD * (j + 1)], vh[:, :, j::HPB, :],
                                       f(VAUG[:, :, j::HPB, 2 * HD * j:2 * HD * j + HD]), ALU.subtract)\
                        .then_inc(s["v"], 1)


        @block.scalar
        def _(act):
            def split_weights():
                act.wait_ge(s["ctx"], 16)
                act.activation(cT[0][:, :, :], cst, ACT.Copy).then_inc(s["cTh"], 1)
                act.wait_ge(s_w, 64)
                act.activation(WP[0][:, :, :, :], wst, ACT.Copy).then_inc(s_wh, 1)
                act.activation(WO[0][:, :, :], wost, ACT.Copy).then_inc(s_wh, 1)

            nt.act(act, split_weights)
            act.wait_ge(s_sel, 16)
            act.activation(SELK[:, :, :, :].rearrange("p a b m -> p (a b m)"), selst[:, 0:NK], ACT.Copy).then_inc(s_ws, 1)
            act.activation(SELQ[:, :, :, :].rearrange("p a b m -> p (a b m)"), selst[:, NK:], ACT.Copy).then_inc(s_ws, 1)
            act.sem_inc(s["p"], TT)
            act.sem_inc(s["qst"], 2)
            act.wait_ge(s_ws, 2)
            with act.Fori(0, B) as i:
                def project(n, dst, b, slot):
                    for c in range(C):
                        act.wait_ge(s["mb"], SLOTS * i + slot + c + 1)
                        act.activation(dst[0][:, c, :], MB[c][:, :], ACT.Identity, bias=g.col(b, c)).then_inc(s["kqh"], 1)

                project(0, kT, "bk1", 0)
                for p in range(1, HEADS // 2, 2):
                    act.wait_ge(s["mb"], SLOTS * i + 4 + p + 1)
                    act.activation(KST[:, p, :], MB[(4 + p) % NB][:, :], ACT.Copy).then_inc(s["kst"], 1)
                project(1, qT, "bq1", 12)

                def stack(h):
                    act.wait_ge(s["qs"], HEADS * i + h + 1)
                    act.activation(QST[:, h % 2, :], QB[:, :], ACT.Copy).then_inc(s["qst"], 1)

                stack(0)
                for m in range(NP + TT):
                    h, j = divmod(m, TT)
                    if m < NP:
                        if j == 0:
                            act.wait_ge(s["pt"], NP * i + m + 1)
                        act.wait_ge(s["nmx"], NP * i + m + 1)
                        act.activation(PR[:, h % 2, j, :], SB[j][:, :], ACT.Exp, bias=nmx[:, h % 2, j:j + 1],
                                       accum_out=den[:, j, h:h + 1]).then_inc(s["p"], 1)
                    if m >= TT:
                        n = NP * i + m - TT
                        act.wait_ge(s["pt"], n + 6)
                        act.wait_ge(s["pv"], n + 1)
                        act.activation(PTS[0][:, j % 2, :], PT[j % 2][:, :], ACT.Copy).then_inc(s["pth"], 1)
                    if j == 0 and h + 1 < HEADS:
                        stack(h + 1)
                    if m == NP:
                        act.wait_ge(s["ctx"], 16 * i + 32)
                        act.activation(cT[0][:, :, :], cst, ACT.Copy).then_inc(s["cTh"], 1)
                for q in range(HPB):
                    act.wait_ge(s["on"], HPB * i + q + 1)
                    act.activation(ON[0][:, q, :], OS[:, q, :], ACT.Copy).then_inc(s["onh"], 1)

        @block.vector
        def _(dve):
            def split_weights():
                dve.wait_ge(s["cTh"], 1)
                dve.sem_inc(s["cTl"], 1)
                dve.tensor_tensor(cT[1][:, :, :], cst, f(cT[0][:, :, :]), ALU.subtract).then_inc(s["cTl"], 1)
                dve.wait_ge(s_wh, 2)
                dve.tensor_tensor(WP[1][:, :, :, :], wst, f(WP[0][:, :, :, :]), ALU.subtract).then_inc(s_wl, 1)
                dve.tensor_tensor(WO[1][:, :, :], wost, f(WO[0][:, :, :]), ALU.subtract).then_inc(s_wl, 1)

            nt.dve(dve, split_weights)
            dve.sem_inc(s["mk"], 1)
            dve.sem_inc(s["mbf"], NB)
            dve.sem_inc(s["ptl"], 2)
            dve.sem_inc(s["os"], 1)
            with dve.Fori(0, B) as i:
                ch = Chain(dve, s_c, i * PER, PER, s_pass)

                def mask(j):
                    dve.wait_ge(s["mld"], 32 * i + 16 * j + 16)
                    dve.tensor_scalar(mk[:, 2 * j:2 * j + 2, :], mst[:, :, :], 1.0, None, ALU.is_equal).then_inc(s["mk"], 1)

                mask(0)

                def low(n, dst, b):
                    for c in range(C):
                        dve.wait_ge(s["kqh"], 2 * C * i + 2 * n + c + 1)
                        dve.scalar_tensor_tensor(out=dst[1][:, c, :], in0=MB[c][:, :], scalar=g.col(b, c),
                                                 in1=f(dst[0][:, c, :]), op0=ALU.add, op1=ALU.subtract)\
                           .then_inc(s["mbf"], 1)

                low(0, kT, "bk1")
                dve.wait_ge(s["v"], HPB * i + 1)
                for j in range(2):
                    dve.wait_ge(s["mb"], SLOTS * i + 2 + j + 1)
                    dve.tensor_tensor(vS[:, 2 * j:2 * j + 2, :], MB[2 + j][:, :].rearrange("p (t d) -> p t d", d=D),
                                      tiles(g.row("bv1")), ALU.add).then_inc(s["mbf"], 1)
                for p in range(0, HEADS // 2, 2):
                    dve.wait_ge(s["mb"], SLOTS * i + 4 + p + 1)
                    dve.tensor_copy(KST[:, p, :], MB[(4 + p) % NB][:, :]).then_inc(s["mbf"], 1)
                mask(1)
                low(1, qT, "bq1")

                def take(q):
                    dve.wait_ge(s["pv"], NP * i + TT * HPB * (q + 1) + 2)
                    dve.tensor_copy(OS[:, q, :], OB[:, :]).then_inc(s["os"], 1)

                def scale(q):
                    dve.wait_ge(s["mb"], SLOTS * i + 14 + q + 1)
                    dve.wait_ge(s["os"], HPB * i + q + 2)
                    ch.link(dve.tensor_tensor(OS[:, q, :], OS[:, q, :], MB[(14 + q) % NB][:, :], ALU.mult))
                    dve.sem_inc(s["mbf"], 1)
                    dve.sem_inc(s["on"], 1)

                for m in range(NP + TT + 1):
                    h, j = divmod(m, TT)
                    if m < NP:
                        dve.wait_ge(s["s"], NP * i + m + 1)
                        dve.tensor_reduce(nmx[:, h % 2, j:j + 1], SB[j][:, :], AX.X, ALU.max, negate=True)\
                           .then_inc(s["nmx"], 1)
                    k = m - TT - 1
                    if k >= 0:
                        dve.wait_ge(s["pth"], NP * i + k + 1)
                        dve.tensor_tensor(PTS[1][:, k % 2, :], PT[k % 2][:, :], f(PTS[0][:, k % 2, :]), ALU.subtract)\
                           .then_inc(s["ptl"], 1)
                    if k > 0 and k % (TT * HPB) == 0:
                        take(k // (TT * HPB) - 1)
                    if m == NP:
                        dve.wait_ge(s["p"], NP * i + NP + TT)
                        ch.link(dve.reciprocal(den[:, :, :], den[:, :, :]))
                    if m == NP + 1:
                        dve.tensor_copy(RDR.rearrange("p t (h r) -> p (t h) r", r=2 * HD),
                                        den[:, :, :].rearrange("p t h -> p (t h)").unsqueeze(2).to_broadcast(
                                            [P, TT * HEADS, 2 * HD])).then_inc(s["rdr"], 1)
                    if m > NP + 1:
                        scale(m - NP - 2)
                for q in range(HPB):
                    if q == HPB - 2:
                        take(HPB - 1)
                        scale(HPB - 1)
                    dve.wait_ge(s["onh"], HPB * i + q + 1)
                    dve.tensor_tensor(ON[1][:, q, :], OS[:, q, :], f(ON[0][:, q, :]), ALU.subtract).then_inc(s["onl"], 1)
                for tt in range(TT):
                    dst = tile_of(g.x_res, i)(tt)
                    ch.inc(dve.tensor_tensor(dst, dst, g.row("bo1"), ALU.add))
                ch.wait()
                dve.wait_ge(s["cTh"], i + 2)
                dve.tensor_tensor(cT[1][:, :, :], cst, f(cT[0][:, :, :]), ALU.subtract).then_inc(s["cTl"], 1)
                for j in range(2):
                    dve.wait_ge(s["mb"], SLOTS * i + 18 + j + 1)
                    dst = g.x_res[:, ds(i * TT + 2 * j, 2), :]
                    ch.link(dve.tensor_tensor(dst, MB[(18 + j) % NB][:, :].rearrange("p (t d) -> p t d", d=D), dst, ALU.add))
                    dve.sem_inc(s["mbf"], 1)
                ch.end()

        @block.tensor
        def _(pe):
            nt.pe(pe)
            pe.wait_ge(s_wl, 2)
            pe.wait_ge(s_nid, 1)
            pe.sem_inc(s["pv"], 2)
            pe.sem_inc(s["pt"], 5)
            with pe.Fori(0, B) as i:
                slot = [0]

                def bank():
                    n = slot[0]
                    slot[0] += 1
                    emptied(pe, i, n - NB)
                    return MB[n % NB]

                pe.wait_ge(s["cTl"], i + 2)

                def project(w, src):
                    for m in range(C):
                        products(pe, bank()[:, :], lambda q, c: WP[q][:, w, c, m * P:(m + 1) * P], src)\
                            .then_inc(s["mb"], 1)

                project(1, lambda q, c: cT[q][:, c, :])
                pe.wait_ge(s_ws, 2)
                pe.wait_ge(nt.tn.lo, C * B + C)
                for j in range(2):
                    bk = bank()
                    for kc in (2 * j, 2 * j + 1):
                        last = products(pe, bk[:, (kc % 2) * D:(kc % 2 + 1) * D],
                                        lambda q, c: cT[q][:, c, kc * P:(kc + 1) * P], lambda q, c: WP[q][:, 2, c, :],
                                        start=kc % 2 == 0, skip=True)
                    last.then_inc(s["mb"], 1)
                for p in range(HEADS // 2):
                    bk = bank()
                    for q in range(2):
                        last = pe.matmul(bk[:, :], SELK[:, p % HPB, q, :], kT[q][:, p // HPB, :], start=q == 0, stop=q == 1)
                    last.then_inc(s["mb"], 1)
                project(0, g.xT_of(i))

                def stack(h):
                    pe.wait_ge(s["qst"], HEADS * i + h + 2)
                    for q in range(2):
                        last = pe.matmul(QB[:, :], SELQ[:, h % (2 * HPB), q, :], qT[q][:, h // (2 * HPB), :],
                                         start=q == 0, stop=q == 1)
                    last.then_inc(s["qs"], 1)

                def weigh(h, kc):
                    n = NP * i + TT * h + kc
                    pe.wait_ge(s["ptl"], n + 3)
                    if h % HPB == 0 and kc == 0:
                        pe.wait_ge(s["os"], HPB * i + h // HPB + 1)
                    for q in range(2):
                        last = pe.matmul(OB[:, :], VAUG[:, kc, h, :], PTS[q][:, kc % 2, :],
                                         start=h % HPB == 0 and kc == 0 and q == 0,
                                         stop=h % HPB == HPB - 1 and kc == TT - 1 and q == 1)
                    last.then_inc(s["pv"], 1)

                emptied(pe, i, 13)
                stack(0)
                emptied(pe, i, 11)

                def score(m):
                    h, j = divmod(m, TT)
                    if j == 0:
                        pe.wait_ge(s["qst"], HEADS * i + h + 3)
                    pe.wait_ge(s["p"], NP * i + m + 1)
                    pe.matmul(SB[j][:, :], nid[:, :], mk[:, j, :], start=True, stop=False)
                    pe.matmul(SB[j][:, :], QST[:, h % 2, j * P:(j + 1) * P], KST[:, h // 2, :],
                              start=False, stop=True).then_inc(s["s"], 1)

                def spread(q):
                    bk = bank()
                    for t in range(TT):
                        last = pe.transpose(bk[:, t * P:(t + 1) * P], RDR[:, t, q * P:(q + 1) * P], g.ident[:, :])
                    last.then_inc(s["mb"], 1)

                score(0)
                score(1)
                stack(1)
                for m in range(NP + TT + 2):
                    h, j = divmod(m, TT)
                    if m + 2 < NP:
                        score(m + 2)
                    if m == TT + 2:
                        pe.wait_ge(s["v"], HPB * i + HPB + 1)
                    if m > TT + 1:
                        weigh(*divmod(m - TT - 2, TT))
                    if TT <= m < NP + TT:
                        if j == 0:
                            pe.wait_ge(s["p"], NP * i + m + TT)
                        pe.wait_ge(s["ptl"], NP * i + m - TT + 1)
                        for t in range(TT):
                            last = pe.transpose(PT[j % 2][:, t * P:(t + 1) * P],
                                                PR[:, (h - 1) % 2, t, j * P:(j + 1) * P], g.ident[:, :])
                        last.then_inc(s["pt"], 1)
                    if j == 2 and h + 2 < HEADS:
                        stack(h + 2)
                    if m == NP + 2:
                        pe.wait_ge(s["rdr"], i + 1)
                        spread(0)
                    if NP + 2 <= m < NP + 1 + HPB:
                        spread(m - NP - 1)
                pe.wait_ge(s["onl"], HPB * i + HPB)
                for j in range(2):
                    bk = bank()
                    for tt in (2 * j, 2 * j + 1):
                        last = products(pe, bk[:, (tt % 2) * D:(tt % 2 + 1) * D],
                                        lambda q, c: ON[q][:, c, tt * P:(tt + 1) * P], lambda q, c: WO[q][:, c, :],
                                        chunks=HPB, start=tt % 2 == 0, skip=True)
                    last.then_inc(s["mb"], 1)
                assert slot[0] == SLOTS


def binary_phase(nc, g, sb, ps):
    a, sem = g.a, g.sem
    xn = sb("bi_xn", [P, TT, D], F32)
    mag = sb("bi_mag", [P, 2, 2 * H], F32)
    low = sb("bi_low", [P, 2, 2 * H], F32)
    ones = sb("bi_ones", [P, P], F32)
    TP = [ps(f"bi_tp{i}", [P, T], F32) for i in range(2)]
    A1, A2 = ps("bi_a1", [P, HT, 2], F32), ps("bi_a2", [P, D], F32)
    nt = NormTurn(g, sb, "bi", xn, TP)
    s_l, s_m, s_o, s_low, s_sign, s_a, s_al = (sem("bi_" + n) for n in ("loaded", "mag", "ones", "low", "sign", "sums",
                                                                       "alphas"))
    S = (g.S1[:, :, :].rearrange("p c n -> p (c n)"), g.S2[:, :, :].rearrange("p c n -> p (c n)"))

    with nc.Block() as block:
        @block.sync
        def _(sp):
            sp.dma_start(g.w_stage[:, 0, :].rearrange("p (c n) -> p c n", c=C),
                         a["w1_1"].rearrange("(c p) n -> p c n", p=P)).then_inc(s_l, 16)
            sp.dma_start(g.w_stage[:, 1, :].rearrange("p (t n) -> p t n", t=HT),
                         a["w2_1"].rearrange("(t p) n -> p t n", p=P)).then_inc(s_l, 16)

        @block.gpsimd
        def _(pool):
            nt.pool(pool)

        @block.scalar
        def _(act):
            def magnitudes():
                act.wait_ge(s_l, 32)
                for j in range(2):
                    act.activation(mag[:, j, :], g.w_stage[:, j, :], ACT.Abs).then_inc(s_m, 1)

            nt.act(act, magnitudes, 2)

        @block.vector
        def _(dve):
            def signs():
                dve.wait_ge(s_l, 32)
                for j in range(2):
                    dve.tensor_scalar(low[:, j, :], g.w_stage[:, j, :], 0.0, None, ALU.is_lt).then_inc(s_low, 1)
                for j in range(2):
                    dve.wait_ge(s_low, j + 1)
                    dve.scalar_tensor_tensor(out=S[j], in0=g.w_stage[:, j, :], scalar=0.0, in1=low[:, j, :],
                                             op0=ALU.is_gt, op1=ALU.subtract).then_inc(s_sign, 1)

            dve.memset(ones[:, :], 1.0).then_inc(s_o, 1)
            nt.dve(dve, signs)
            dve.wait_ge(s_a, 2)
            dve.tensor_scalar(g.alpha1[:, :], A1[:, :, 0], 1.0 / D, None, ALU.mult).then_inc(s_al, 1)
            dve.tensor_scalar(g.alpha2[:, :], A2[:, :], 1.0 / H, None, ALU.mult).then_inc(s_al, 1)

        @block.tensor
        def _(pe):
            def sums1():
                pe.wait_ge(s_m, 2)
                pe.wait_ge(s_o, 1)
                for t in range(HT):
                    for c in range(C):
                        at = c * H + t * P
                        last = pe.matmul(A1[:, t, :], mag[:, 0, at:at + P], ones[:, 0:2], start=t == 0 and c == 0,
                                         stop=c == C - 1, skip_group_check=True)
                last.then_inc(s_a, 1)

            nt.pe(pe, sums1)
            for t in range(HT):
                last = pe.matmul(A2[:, :], ones[:, :], mag[:, 1, t * D:(t + 1) * D], start=t == 0, stop=t == HT - 1)
            last.then_inc(s_a, 1)


def ffn1_phase(nc, g, sb, ps):
    m = Mlp(sb, ps, g.sem, "ffn1", 1)
    fin = sb("f1_fin", [P, 2, 2, D], F32)
    s_c, s_out = g.sem("f1_dve_chain"), g.sem("out_stored")
    o = g.out.rearrange("(t p) d -> p t d", p=P)
    PER = 5
    with nc.Block() as block:
        @block.sync
        def _(sp):
            with sp.Fori(0, B) as i:
                sp.wait_ge(m.y_used, i + 2)
                sp.dma_start(o[:, ds(i * TT, TT), :], g.x_res[:, ds(i * TT, TT), :]).then_inc(s_out, 16)
            sp.wait_ge(s_out, 16 * B)

        @block.tensor
        def _(pe):
            weights = (lambda q, c, t: g.S1[:, c, t * P:(t + 1) * P]), (lambda q, t: g.S2[:, t, :])
            mlp_pe(pe, m, lambda q: weights, g.xT_of, p1=((0, 0), (0, 1)), p2=((0, 0), (1, 0)))

        @block.scalar
        def _(act):
            mlp_act(act, m, ACT.Gelu, lambda tile: g.col("b1_1", tile.t),
                    scale=lambda tile: g.alpha1[:, tile.t:tile.t + 1])

        @block.vector
        def _(dve):
            chains = {}

            def add_y(q, i, j, y):
                if j == 0:
                    chains["batch"] = Chain(dve, s_c, i * PER, PER)
                ch = chains["batch"]
                dst = g.x_res[:, ds(i * TT + 2 * j, 2), :]
                ch.link(dve.tensor_tensor(fin[:, j], y, tiles(g.alpha2[:, :]), ALU.mult))
                ch.link(dve.tensor_tensor(fin[:, j], fin[:, j], tiles(g.row("b2_1")), ALU.add))
                ins = dve.tensor_tensor(dst, dst, fin[:, j], ALU.add)
                if j == 0:
                    ch.inc(ins)
                else:
                    ch.end()
                return ins
            mlp_dve(dve, m, add_y)


def gate_selector():
    import numpy as np
    row = np.arange(P)
    expert = (row // (2 * EG)) * EG + row % EG
    return (expert[:, None] == np.arange(E)[None, :]).astype(np.float32)


def stack_selectors():
    import numpy as np
    feat, m = np.arange(P)[:, None], np.arange(P)[None, :]
    out = []
    for p in range(HPB):
        for q in range(2):
            out.append((feat == 2 * HD * p + m % (2 * HD)) & (m // (2 * HD) % 2 == q))
    for h in range(2 * HPB):
        for q in range(2):
            out.append(((feat == 2 * HD * (h // 2) + m % (2 * HD)) & (m % (2 * HD) // HD == h % 2)
                        & (m // (2 * HD) // 2 == q)) * np.float32(HD ** -0.5))
    return np.concatenate([x.astype(np.float32) for x in out], axis=1)


def kernel(**inputs):
    import numpy as np
    import concourse.bacc as bacc
    from concourse.bass_utils import run_bass_kernel_spmd as run

    v = {k: np.asarray(x) for k, x in inputs.items()}
    cc = np.ascontiguousarray

    def cols(x):
        return cc(x.reshape(-1, P).T)

    rb, eb2 = v["L0_ffn_router_b"], v["L0_ffn_b2"]
    col = {"bq0": v["L0_xattn_bq"], "bk0": v["L0_xattn_bk"], "bv0": v["L0_xattn_bv"], "b1_0": v["L0_xattn_b1"],
           "rb": np.concatenate([rb, rb]), "eb1": v["L0_ffn_b1"], "sb1": v["L0_ffn_sb1"], "bq1": v["L1_xattn_bq"],
           "bk1": v["L1_xattn_bk"], "b1_1": v["L1_ffn_b1"]}
    row = {"bo0": v["L0_xattn_bo"], "gamma": v["L0_xattn_gamma"], "beta": v["L0_xattn_beta"], "b2_0": v["L0_xattn_b2"],
           "sb2a": v["L0_ffn_sb2"][0], "sb2b": v["L0_ffn_sb2"][1], "bv1": v["L1_xattn_bv"], "bo1": v["L1_xattn_bo"],
           "b2_1": v["L1_ffn_b2"]}
    rw = v["L0_ffn_router_w"]
    wo1 = v["L1_xattn_Wo"].T.reshape(HEADS, 1, HD, D)
    arrays = {
        "x": v["x"].reshape(B * T, D), "ctx": v["ctx_1024"].reshape(B * T, D),
        "ctxT": cc(v["ctx_1024"].reshape(B * T, D).T), "mask": v["mask_Bx1xSxS2_ik1"].reshape(B * T, T),
        "cols": cc(np.concatenate([cols(col[n]) for n in COLS], axis=1)),
        "rows": cc(np.stack([row[n] for n in ROWS])), "ident": np.eye(P, dtype=np.float32),
        "pos": v["L0_xattn_pos_bias"],
        "wq0": v["L0_xattn_wq"], "wk0": v["L0_xattn_wk"], "wv0": v["L0_xattn_wv"], "wo0": v["L0_xattn_wo"],
        "w1_0": v["L0_xattn_w1"], "w2_0": v["L0_xattn_w2"],
        "rw": cc(np.concatenate([rw, rw], axis=1)),
        "eb2": cc(np.broadcast_to(eb2.reshape(GR, 1, EG, D), (GR, 2, EG, D)).reshape(P, D)),
        "ew1": cc(v["L0_ffn_w1"].transpose(1, 0, 2).reshape(D, E * HE)), "ew2": v["L0_ffn_w2"].reshape(E * HE, D),
        "sw1": cc(v["L0_ffn_sw1"].transpose(1, 0, 2).reshape(D, H)), "sw2": v["L0_ffn_sw2"].reshape(H, D),
        "sel_gate": gate_selector(), "sel_qk": stack_selectors(),
        "wq1": cc(v["L1_xattn_Wq"].T), "wk1": cc(v["L1_xattn_Wk"].T), "wv1": cc(v["L1_xattn_Wv"].T),
        "wo1": cc(np.broadcast_to(wo1, (HEADS, 2, HD, D)).reshape(HEADS * 2 * HD, D)),
        "w1_1": cc(v["L1_ffn_w1"].T), "w2_1": cc(v["L1_ffn_w2"].T),
    }
    nc = bacc.Bacc("TRN2", target_bir_lowering=False, num_devices=1)
    aps, ins = {}, {}
    for n, x in arrays.items():
        ins["in_" + n] = cc(x)
        aps[n] = nc.dram_tensor("in_" + n, x.shape, mybir.dt.from_np(x.dtype), kind="ExternalInput").ap()
    out = nc.dram_tensor("out", (B * T, D), F32, kind="ExternalOutput").ap()
    build(nc, aps, out)
    r = run(nc, [ins], core_ids=[0])
    return r.results[0]["out"].reshape(B, T, D)
```
